# Optimizing a Trainium2 kernel written in Bass

```python
import numpy as np
import jax
import jax.numpy as jnp

def _softmax(x, axis=-1):
    return jax.nn.softmax(x, axis=axis)

def _gelu(x):
    return jax.nn.gelu(x, approximate=True)

def _silu(x):
    return jax.nn.silu(x)

def _sigmoid(x):
    return jax.nn.sigmoid(x)

def _layernorm(x, axis=-1, eps=1e-05):
    m = jnp.mean(x, axis=axis, keepdims=True)
    v = jnp.var(x, axis=axis, keepdims=True)
    return (x - m) / jnp.sqrt(v + eps)

def _scatter_add(tgt, idx, src, axis=0):
    return tgt.at[idx].add(src)

def _segment_sum(src, seg, n):
    return jax.ops.segment_sum(src, seg, n)
kernel_name = 'mk_gnn_ffn_d1_gnn_r8_986ba8'

def setup_inputs(seed: int=0):
    np.random.seed(seed)
    _w = jnp.asarray

    def _rec_inputs():
        import jax
        import jax.numpy as jnp
        _gk = jax.random.key(seed)
        x = -0.0001126 + 1 * jax.random.normal(jax.random.fold_in(_gk, 1), (1250, 768), jnp.float32)
        src = jax.random.randint(jax.random.fold_in(_gk, 2), (40000,), 0, 1250, jnp.int32)
        dst = jax.random.randint(jax.random.fold_in(_gk, 3), (40000,), 0, 1250, jnp.int32)
        _o = jnp.argsort(dst, stable=True)
        src = src[_o]
        dst = dst[_o]
        return (x, src, dst)
    x, src, dst = _rec_inputs()

    def _L0_gnn_setup():
        import jax, jax.numpy as jnp
        import numpy as np
        N_NODES = 1250
        N_EDGES = 20000
        NEG_SLOPE = 0.2

        def _gat_layer(x, src, dst, W, a_src, a_dst, bias, concat):
            N = x.shape[0]
            H, C = a_src.shape
            h = (x @ W).reshape(N, H, C)
            al_s = jnp.einsum('nhc,hc->nh', h, a_src)
            al_d = jnp.einsum('nhc,hc->nh', h, a_dst)
            e = jax.nn.leaky_relu(al_s[src] + al_d[dst], NEG_SLOPE)
            m = jax.ops.segment_max(e, dst, num_segments=N)
            ex = jnp.exp(e - m[dst])
            denom = jax.ops.segment_sum(ex, dst, num_segments=N)
            alpha = ex / (denom[dst] + 1e-16)
            msg = h[src] * alpha[:, :, None]
            out = jax.ops.segment_sum(msg, dst, num_segments=N)
            out = out.reshape(N, H * C) if concat else out.mean(axis=1)
            return out + bias
        key = jax.random.key(seed)
        ks = jax.random.split(key, 10)
        in_dim, hid, out_dim, heads = (768, 512, 768, 4)
        x = jax.random.normal(ks[0], (N_NODES, in_dim), dtype=jnp.float32)
        edge_index = jax.random.randint(ks[1], (2, N_EDGES), 0, N_NODES, dtype=jnp.int64)
        g = lambda k, shape, fan: jax.random.normal(k, shape, jnp.float32) / np.sqrt(fan)
        return {'x': x, 'edge_index': edge_index, 'W1': g(ks[2], (in_dim, heads * hid), in_dim), 'att_src1': g(ks[3], (heads, hid), hid), 'att_dst1': g(ks[4], (heads, hid), hid), 'b1': jnp.zeros((heads * hid,), jnp.float32), 'W2': g(ks[5], (heads * hid, out_dim), heads * hid), 'att_src2': g(ks[6], (1, out_dim), out_dim), 'att_dst2': g(ks[7], (1, out_dim), out_dim), 'b2': jnp.zeros((out_dim,), jnp.float32)}
    _L0_gnn_all = _L0_gnn_setup()
    _L0_gnn_in = {k: v for k, v in _L0_gnn_all.items() if k in ('W1', 'att_src1', 'att_dst1', 'b1', 'W2', 'att_src2', 'att_dst2', 'b2')}
    del _L0_gnn_all

    def _L0_ffn_setup():
        import jax, jax.numpy as jnp
        import numpy as np
        DIM = 768
        FF = 384
        E = 8
        K = 2
        H = 12
        HD = DIM // H
        LN_EPS = 1e-05

        def _layernorm(x, g, b):
            m = jnp.mean(x, axis=-1, keepdims=True)
            v = jnp.var(x, axis=-1, keepdims=True)
            return (x - m) * jax.lax.rsqrt(v + LN_EPS) * g + b

        def _attention(x, Wqkv, Wproj):
            B, T, D = x.shape
            qkv = (x @ Wqkv).reshape(B, T, 3, H, HD)
            q, k, v = (qkv[:, :, 0], qkv[:, :, 1], qkv[:, :, 2])
            scores = jnp.einsum('bqhd,bkhd->bhqk', q, k) * jnp.float32(HD) ** (-0.5)
            attn = jax.nn.softmax(scores, axis=-1)
            out = jnp.einsum('bhqk,bkhd->bqhd', attn, v).reshape(B, T, D)
            return out @ Wproj

        def _moe(x, Wrouter, W1, W2):
            B, T, D = x.shape
            xf = x.reshape(-1, D)
            N = xf.shape[0]
            logits = xf @ Wrouter
            topk_w, topk_idx = jax.lax.top_k(logits, K)
            topk_w = jax.nn.softmax(topk_w.astype(jnp.float32), axis=-1).astype(x.dtype)
            we = jnp.zeros((N, E), x.dtype).at[jnp.arange(N)[:, None], topk_idx].add(topk_w)

            def body(acc, expert):
                W1e, W2e, we_e = expert
                h = jax.nn.gelu(xf @ W1e, approximate=False)
                return (acc + we_e[:, None] * (h @ W2e), None)
            out, _ = jax.lax.scan(body, jnp.zeros_like(xf), (W1, W2, we.T))
            return out.reshape(B, T, D)
        key = jax.random.key(seed)
        ks = jax.random.split(key, 7)
        B, T = (4, 1024)
        init = lambda k, shape, fan: jax.random.normal(k, shape, jnp.float32) * fan ** (-0.5)
        return {'x': jax.random.normal(ks[0], (B, T, DIM), jnp.float32), 'Wqkv': init(ks[1], (DIM, 3 * DIM), DIM), 'Wproj': init(ks[2], (DIM, DIM), DIM), 'Wrouter': init(ks[3], (DIM, E), DIM), 'W1': init(ks[4], (E, DIM, FF), DIM), 'W2': init(ks[5], (E, FF, DIM), FF), 'ln1_g': jnp.ones((DIM,), jnp.float32), 'ln1_b': jnp.zeros((DIM,), jnp.float32), 'ln2_g': jnp.ones((DIM,), jnp.float32), 'ln2_b': jnp.zeros((DIM,), jnp.float32)}
    _L0_ffn_all = _L0_ffn_setup()
    _L0_ffn_in = {k: v for k, v in _L0_ffn_all.items() if k in ('Wqkv', 'Wproj', 'Wrouter', 'W1', 'W2', 'ln1_g', 'ln1_b', 'ln2_g', 'ln2_b')}
    del _L0_ffn_all
    return {'x': x, 'src': src, 'dst': dst, 'L0_gnn_W1': _L0_gnn_in['W1'], 'L0_gnn_att_src1': _L0_gnn_in['att_src1'], 'L0_gnn_att_dst1': _L0_gnn_in['att_dst1'], 'L0_gnn_b1': _L0_gnn_in['b1'], 'L0_gnn_W2': _L0_gnn_in['W2'], 'L0_gnn_att_src2': _L0_gnn_in['att_src2'], 'L0_gnn_att_dst2': _L0_gnn_in['att_dst2'], 'L0_gnn_b2': _L0_gnn_in['b2'], 'L0_ffn_Wqkv': _L0_ffn_in['Wqkv'], 'L0_ffn_Wproj': _L0_ffn_in['Wproj'], 'L0_ffn_Wrouter': _L0_ffn_in['Wrouter'], 'L0_ffn_W1': _L0_ffn_in['W1'], 'L0_ffn_W2': _L0_ffn_in['W2'], 'L0_ffn_ln1_g': _L0_ffn_in['ln1_g'], 'L0_ffn_ln1_b': _L0_ffn_in['ln1_b'], 'L0_ffn_ln2_g': _L0_ffn_in['ln2_g'], 'L0_ffn_ln2_b': _L0_ffn_in['ln2_b']}

def reference(x, src, dst, L0_gnn_W1, L0_gnn_att_src1, L0_gnn_att_dst1, L0_gnn_b1, L0_gnn_W2, L0_gnn_att_src2, L0_gnn_att_dst2, L0_gnn_b2, L0_ffn_Wqkv, L0_ffn_Wproj, L0_ffn_Wrouter, L0_ffn_W1, L0_ffn_W2, L0_ffn_ln1_g, L0_ffn_ln1_b, L0_ffn_ln2_g, L0_ffn_ln2_b):
    import jax
    import jax.numpy as jnp

    def _L0_gnn_ref(x, edge_index, W1, att_src1, att_dst1, b1, W2, att_src2, att_dst2, b2):
        import jax, jax.numpy as jnp
        import numpy as np
        N_NODES = 1250
        N_EDGES = 20000
        NEG_SLOPE = 0.2

        def _gat_layer(x, src, dst, W, a_src, a_dst, bias, concat):
            N = x.shape[0]
            H, C = a_src.shape
            h = (x @ W).reshape(N, H, C)
            al_s = jnp.einsum('nhc,hc->nh', h, a_src)
            al_d = jnp.einsum('nhc,hc->nh', h, a_dst)
            e = jax.nn.leaky_relu(al_s[src] + al_d[dst], NEG_SLOPE)
            m = jax.ops.segment_max(e, dst, num_segments=N)
            ex = jnp.exp(e - m[dst])
            denom = jax.ops.segment_sum(ex, dst, num_segments=N)
            alpha = ex / (denom[dst] + 1e-16)
            msg = h[src] * alpha[:, :, None]
            out = jax.ops.segment_sum(msg, dst, num_segments=N)
            out = out.reshape(N, H * C) if concat else out.mean(axis=1)
            return out + bias
        N = x.shape[0]
        loops = jnp.arange(N, dtype=edge_index.dtype)
        src = jnp.concatenate([edge_index[0], loops])
        dst = jnp.concatenate([edge_index[1], loops])
        h = jax.nn.elu(_gat_layer(x, src, dst, W1, att_src1, att_dst1, b1, concat=True))
        out = _gat_layer(h, src, dst, W2, att_src2, att_dst2, b2, concat=False)
        return out

    def _L0_ffn_ref(x, Wqkv, Wproj, Wrouter, W1, W2, ln1_g, ln1_b, ln2_g, ln2_b):
        import jax, jax.numpy as jnp
        import numpy as np
        DIM = 768
        FF = 384
        E = 8
        K = 2
        H = 12
        HD = DIM // H
        LN_EPS = 1e-05

        def _layernorm(x, g, b):
            m = jnp.mean(x, axis=-1, keepdims=True)
            v = jnp.var(x, axis=-1, keepdims=True)
            return (x - m) * jax.lax.rsqrt(v + LN_EPS) * g + b

        def _attention(x, Wqkv, Wproj):
            B, T, D = x.shape
            qkv = (x @ Wqkv).reshape(B, T, 3, H, HD)
            q, k, v = (qkv[:, :, 0], qkv[:, :, 1], qkv[:, :, 2])
            scores = jnp.einsum('bqhd,bkhd->bhqk', q, k) * jnp.float32(HD) ** (-0.5)
            attn = jax.nn.softmax(scores, axis=-1)
            out = jnp.einsum('bhqk,bkhd->bqhd', attn, v).reshape(B, T, D)
            return out @ Wproj

        def _moe(x, Wrouter, W1, W2):
            B, T, D = x.shape
            xf = x.reshape(-1, D)
            N = xf.shape[0]
            logits = xf @ Wrouter
            topk_w, topk_idx = jax.lax.top_k(logits, K)
            topk_w = jax.nn.softmax(topk_w.astype(jnp.float32), axis=-1).astype(x.dtype)
            we = jnp.zeros((N, E), x.dtype).at[jnp.arange(N)[:, None], topk_idx].add(topk_w)

            def body(acc, expert):
                W1e, W2e, we_e = expert
                h = jax.nn.gelu(xf @ W1e, approximate=False)
                return (acc + we_e[:, None] * (h @ W2e), None)
            out, _ = jax.lax.scan(body, jnp.zeros_like(xf), (W1, W2, we.T))
            return out.reshape(B, T, D)
        x = x + _attention(_layernorm(x, ln1_g, ln1_b), Wqkv, Wproj)
        x = x + _moe(_layernorm(x, ln2_g, ln2_b), Wrouter, W1, W2)
        return x
    edge_index = jnp.stack([src, dst])
    x = x + _L0_gnn_ref(_layernorm(x, axis=-1), edge_index, L0_gnn_W1, L0_gnn_att_src1, L0_gnn_att_dst1, L0_gnn_b1, L0_gnn_W2, L0_gnn_att_src2, L0_gnn_att_dst2, L0_gnn_b2)
    x = x + _L0_ffn_ref(_layernorm(x, axis=-1)[None], L0_ffn_Wqkv, L0_ffn_Wproj, L0_ffn_Wrouter, L0_ffn_W1, L0_ffn_W2, L0_ffn_ln1_g, L0_ffn_ln1_b, L0_ffn_ln2_g, L0_ffn_ln2_b)[0]
    return x

_drawn_inputs = setup_inputs


def setup_inputs(seed=0):
    import zlib

    import numpy as np

    out = dict(_drawn_inputs(seed))
    spreads = {'L0_gnn_b1': (0.0, 0.1),
     'L0_gnn_b2': (0.0, 0.1),
     'L0_ffn_ln1_g': (1.0, 0.2),
     'L0_ffn_ln1_b': (0.0, 0.1),
     'L0_ffn_ln2_g': (1.0, 0.2),
     'L0_ffn_ln2_b': (0.0, 0.1)}
    factors = {'L0_gnn_att_dst1': 3.044, 'L0_gnn_att_src2': 2.742, 'L0_gnn_att_dst2': 7.268}
    for name, (base, spread) in spreads.items():
        noise = np.random.default_rng([zlib.crc32(name.encode()), seed]).standard_normal(out[name].shape)
        drawn = base * np.exp(spread * noise) if base else spread * noise
        out[name] = jnp.asarray(drawn.astype(out[name].dtype))
    for name, factor in factors.items():
        out[name] = (out[name] * factor).astype(out[name].dtype)
    return out
```

```python
from contextlib import ExitStack

import numpy as np
import concourse.bass as bass
from concourse import mybir

DT = mybir.dt
F32, F16, BF16, I32, U16 = DT.float32, DT.float16, DT.bfloat16, DT.int32, DT.uint16
ALU = mybir.AluOpType
ACT = mybir.ActivationFunctionType
AX = mybir.AxisListType

P = 128
N = 1250
NT = -(-N // P)
NPAD = NT * P
LAST = N - (NT - 1) * P
D = 768
DC = D // P
HID, HEADS = 512, 4
HC = HID * HEADS // P
EDGES = 40000
FF, EXPERTS = 384, 8
FC = FF // P
ATT_HEADS, HD = 12, 64
PAIRS = ATT_HEADS // 2
EPS = 1e-5
SLOPE = 0.2
WSCALE = 64.0
NO_EDGE = -1e30
BLOCKS = [(0, 512), (512, 512), (1024, N - 1024)]
DHALF = D // 2


def rows(t):
    return P if t < NT - 1 else LAST


class State:
    used = []


def sbuf(nc, scope, name, shape, dtype):
    return scope.enter_context(nc.sbuf_tensor(name, shape, dtype))


def semaphore(nc, scope, name):
    sem = scope.enter_context(nc.semaphore(name))
    State.used.append(sem)
    return sem


def pair_product(pe, out, lhs_hi, lhs_lo, rhs_hi, rhs_lo, first, last):
    pe.matmul(out, lhs_hi, rhs_hi, start=first, stop=False)
    pe.matmul(out, lhs_hi, rhs_lo, start=False, stop=False)
    return pe.matmul(out, lhs_lo, rhs_hi, start=False, stop=last)


def load_nodes(eng, tile, dram, sem):
    full = (NT - 1) * P
    eng.dma_start(tile[:, 0:NT - 1, :], dram[0:full, :].rearrange("(t p) d -> p t d", p=P)).then_inc(sem, 16)
    eng.dma_start(tile[0:LAST, NT - 1, :], dram[full:N, :]).then_inc(sem, 16)


def clear_semaphores(nc):
    with nc.Block() as block:

        @block.gpsimd
        def _(pool):
            for sem in State.used:
                pool.sem_clear(sem)
    State.used.clear()


def constants(nc, s):
    with ExitStack() as scope:
        zeroed = semaphore(nc, scope, "c_zeroed")
        ident_done = semaphore(nc, scope, "c_ident_done")
        block = scope.enter_context(nc.Block())

        @block.gpsimd
        def _(pool):
            pool.memset(s.ident[:, :], 0.0).then_inc(zeroed, 1)
            pool.wait_ge(zeroed, 1)
            pool.affine_select(out=s.ident[:, :], in_=s.ident[:, :], compare_op=ALU.not_equal, fill=1.0,
                               base=0, pattern=[[-1, P]], channel_multiplier=1).then_inc(ident_done, 1)

        @block.vector
        def _(dve):
            dve.memset(s.ones[:, :], 1.0)
            dve.memset(s.ones16[:, :], 1.0)
            dve.wait_ge(ident_done, 1)
            dve.tensor_copy(s.ident_bf[:, :], s.ident[:, :])
            dve.tensor_copy(s.sel[:, :, :], s.ident[0:8, 0:8].unsqueeze(2).to_broadcast([8, 8, P]))


def norm_transpose(nc, s, tag, x, out_norm, xt, twice=False, gain=None, bias=None, load=None,
                   keep=None):
    xt_hi, xt_lo = xt
    with ExitStack() as scope:
        sb = lambda name, shape, dtype: sbuf(nc, scope, f"{tag}_{name}", shape, dtype)
        sem = lambda name: semaphore(nc, scope, f"{tag}_{name}")
        stats = sb("stats", [P, NT, 2, 6], F32)
        moments = sb("moments", [P, NT, 2], F32)
        variance = sb("variance", [P, NT], F32)
        deviation = sb("deviation", [P, NT], F32)
        inverse = sb("inverse", [P, NT], F32)
        scratch = sb("scratch", [P, NT, D], F32) if twice else None
        affine = gain is not None
        if affine:
            gb = sb("gain_bias", [P, 2, DC], F32)
            shifted = sb("shifted", [P, 4, 512], F32)
        loaded = sem("loaded")
        kept = sem("kept")
        gb_loaded = sem("gb_loaded")
        pads_zeroed = sem("pads_zeroed")
        dve_step = sem("dve_step")
        variance_ready = sem("variance_ready")
        deviation_ready = sem("deviation_ready")
        normed = sem("normed")
        turned = sem("turned")
        shifted_ready = sem("shifted_ready")
        hi_ready = sem("hi_ready")
        lo_ready = sem("lo_ready")
        groups = [(c, g) for c in range(DC) for g in range(3)]
        width = [512, 512, NPAD - 1024]
        final = scratch if twice else out_norm
        passes = 2 if twice else 1
        block = scope.enter_context(nc.Block())

        @block.sync
        def _(sp):
            if load is not None:
                sp.wait_ge(pads_zeroed, 1)
                load_nodes(sp, x, load, loaded)
            if keep is not None:
                full = (NT - 1) * P
                sp.dma_start(keep[0:full, :].rearrange("(t p) d -> p t d", p=P), x[:, 0:NT - 1, :]).then_inc(kept, 16)
                sp.dma_start(keep[full:N, :], x[0:LAST, NT - 1, :]).then_inc(kept, 16)
                sp.wait_ge(kept, 32)
            if affine:
                with nc.allow_non_contiguous_dma(reason="one short vector per partition"):
                    sp.dma_start(gb[:, 0, :], gain.rearrange("(c p) -> p c", p=P)).then_inc(gb_loaded, 16)
                    sp.dma_start(gb[:, 1, :], bias.rearrange("(c p) -> p c", p=P)).then_inc(gb_loaded, 16)

        @block.vector
        def _(dve):
            steps = [0]

            def link(ins):
                steps[0] += 1
                ins.then_inc(dve_step, 1)
                dve.wait_ge(dve_step, steps[0])

            if load is not None:
                dve.memset(x[96:P, NT - 1, :], 0.0).then_inc(pads_zeroed, 1)
                dve.wait_ge(loaded, 32)
            for n in range(passes):
                src = x if n == 0 else out_norm
                dst = out_norm if n == 0 else scratch
                for t in range(NT):
                    for half in range(2):
                        ins = dve.bn_stats(stats[:, t, half, :], src[:, t, half * DHALF:(half + 1) * DHALF])
                link(ins)
                for t in range(NT):
                    ins = dve.bn_aggr(moments[:, t, :], stats[:, t, :, :].rearrange("p a b -> p (a b)"))
                link(ins)
                dve.tensor_scalar(variance[:, :], moments[:, :, 1], EPS, None, ALU.add).then_inc(variance_ready, 1)
                dve.wait_ge(deviation_ready, n + 1)
                link(dve.reciprocal(inverse[:, :], deviation[:, :]))
                if keep is not None and n == 0:
                    dve.wait_ge(kept, 32)
                for t in range(NT):
                    ins = dve.tensor_scalar(dst[:, t, :], src[:, t, :], moments[:, t, 0:1], inverse[:, t:t + 1],
                                            ALU.subtract, ALU.mult)
                    if n == passes - 1:
                        ins.then_inc(normed, 1)
                if n < passes - 1:
                    link(ins)
            if affine:
                dve.wait_ge(gb_loaded, 32)
            for n in range(len(groups) + 1):
                if affine and n < len(groups):
                    c, g = groups[n]
                    w = width[g]
                    dve.wait_ge(turned, n + 1)
                    dve.tensor_scalar(shifted[:, n % 4, 0:w], s.ps[n % 4][:, 0:w], gb[:, 0, c:c + 1],
                                      gb[:, 1, c:c + 1], ALU.mult, ALU.add).then_inc(shifted_ready, 1)
                m = n - 1
                if m >= 0:
                    c, g = groups[m]
                    w = width[g]
                    cols = slice(g * 512, g * 512 + w)
                    whole = shifted[:, m % 4, 0:w] if affine else s.ps[m % 4][:, 0:w]
                    dve.wait_ge(hi_ready, m + 1)
                    dve.tensor_tensor(xt_lo[:, c, cols], whole, xt_hi[:, c, cols], ALU.subtract).then_inc(lo_ready, 1)

        @block.scalar
        def _(act):
            for n in range(passes):
                act.wait_ge(variance_ready, n + 1)
                act.activation(deviation[:, :], variance[:, :], ACT.Sqrt).then_inc(deviation_ready, 1)
            for n, (c, g) in enumerate(groups):
                w = width[g]
                cols = slice(g * 512, g * 512 + w)
                if affine:
                    act.wait_ge(shifted_ready, n + 1)
                    whole = shifted[:, n % 4, 0:w]
                else:
                    act.wait_ge(turned, n + 1)
                    whole = s.ps[n % 4][:, 0:w]
                act.activation(xt_hi[:, c, cols], whole, ACT.Copy).then_inc(hi_ready, 1)

        @block.tensor
        def _(pe):
            for n, (c, g) in enumerate(groups):
                pe.wait_ge(normed, min(4 * g + 4, NT))
                if n >= 4:
                    pe.wait_ge(lo_ready, n - 3)
                for t in range(4 * g, min(4 * g + 4, NT)):
                    ins = pe.transpose(s.ps[n % 4][:, (t % 4) * P:(t % 4 + 1) * P],
                                       final[:, t, c * P:(c + 1) * P], s.ident[:, :])
                ins.then_inc(turned, 1)


TILE_E = 125
GROUP = 8
TILES_E = EDGES // TILE_E
GROUPS_E = TILES_E // GROUP
WIN = 64
KEYS = NT * WIN
CT_COLS = NPAD + WIN


def count_edges(nc, s):
    chunks = [(0, P), (P, P), (2 * P, TILES_E - 2 * P)]
    with ExitStack() as scope:
        sb = lambda name, shape, dtype: sbuf(nc, scope, f"e_{name}", shape, dtype)
        sem = lambda name: semaphore(nc, scope, f"e_{name}")
        src_i = sb("src_i", [P, 3, TILE_E], I32)
        dst_i = sb("dst_i", [P, 3, TILE_E], I32)
        part_i = sb("part_i", [P, 2, 3, TILE_E], I32)
        part_f = sb("part_f", [P, 3, 3, TILE_E], F32)
        extent = sb("extent", [P, 6], F32)
        least = sb("least", [1, 48], F32)
        greatest = sb("greatest", [1, 48], F32)
        span = sb("span", [1, 48], F32)
        window_i = sb("window_i", [1, GROUPS_E, 2], I32)
        span_i = sb("span_i", [1, 48], I32)
        base = sb("base", [P, GROUPS_E], F32)
        table = sb("table", [P, GROUPS_E, 4, GROUP], F32)
        inside = sb("inside", [P, GROUPS_E, GROUP], F32)
        mine = sb("mine", [P, 4, GROUP], F32)
        test = sb("test", [P, GROUP], F32)
        iota_i = sb("iota_i", [P, KEYS], I32)
        iota = sb("iota", [P, KEYS], F16)
        one_key = sb("one_key", [P, GROUP, KEYS], F16)
        one_src = sb("one_src", [P, GROUP, P], F16)
        loaded = sem("loaded")
        iota_ready = sem("iota_ready")
        dve_step = sem("dve_step")
        parts_ready = sem("parts_ready")
        parts_turned = sem("parts_turned")
        extent_ready = sem("extent_ready")
        extent_turned = sem("extent_turned")
        least_ready = sem("least_ready")
        base_turned = sem("base_turned")
        windows_ready = sem("windows_ready")
        group_step = sem("group_step")
        visit_step = sem("visit_step")
        onehots_ready = sem("onehots_ready")
        slots_used = sem("slots_used")
        piece_added = sem("piece_added")
        block = scope.enter_context(nc.Block())

        @block.sync
        def _(sp):
            for dst_tile, dram in ((src_i, s.src), (dst_i, s.dst)):
                sp.dma_start(dst_tile[:, 0:2, :], dram[0:2 * P * TILE_E].rearrange("(a p e) -> p a e", a=2, e=TILE_E)
                             ).then_inc(loaded, 16)
                sp.dma_start(dst_tile[0:chunks[2][1], 2, :], dram[2 * P * TILE_E:EDGES].rearrange("(p e) -> p e", e=TILE_E)
                             ).then_inc(loaded, 16)

        @block.gpsimd
        def _(pool):
            pool.iota(iota_i[:, :], pattern=[[1, KEYS]], base=0, channel_multiplier=0).then_inc(iota_ready, 1)

        @block.vector
        def _(dve):
            steps = [0]

            def link(ins):
                steps[0] += 1
                ins.then_inc(dve_step, 1)
                dve.wait_ge(dve_step, steps[0])

            dve.memset(s.CT[:, :, :], 0)
            link(dve.memset(extent[:, :], 0.0))
            dve.wait_ge(iota_ready, 1)
            dve.tensor_copy(iota[:, :], iota_i[:, :])
            dve.wait_ge(loaded, 64)
            for a, (_, k) in enumerate(chunks):
                dve.tensor_scalar(part_i[0:k, 0, a, :], src_i[0:k, a, :], 7, 6, ALU.logical_shift_right,
                                  ALU.logical_shift_left)
                dve.tensor_scalar(part_i[0:k, 1, a, :], src_i[0:k, a, :], P - 1, None, ALU.bitwise_and)
                ins = dve.tensor_copy(part_f[0:k, 2, a, :], dst_i[0:k, a, :])
            link(ins)
            for a, (_, k) in enumerate(chunks):
                dve.tensor_reduce(extent[0:k, a:a + 1], part_f[0:k, 2, a, :], AX.X, ALU.min)
                ins = dve.tensor_reduce(extent[0:k, 3 + a:4 + a], part_f[0:k, 2, a, :], AX.X, ALU.max)
            ins.then_inc(extent_ready, 1)
            for a, (_, k) in enumerate(chunks):
                ins = dve.tensor_copy(part_f[0:k, 0:2, a, :], part_i[0:k, :, a, :])
            ins.then_inc(parts_ready, 1)
            dve.wait_ge(extent_turned, 1)
            dve.tensor_reduce(least[:, :], s.ps[0][0:1, 0:384].rearrange("p (g t) -> p g t", t=GROUP), AX.X, ALU.min
                              ).then_inc(least_ready, 1)
            link(dve.tensor_reduce(greatest[:, :], s.ps[1][0:1, 0:384].rearrange("p (g t) -> p g t", t=GROUP), AX.X,
                                   ALU.max))
            link(dve.tensor_tensor(span[:, :], greatest[:, :], least[:, :], ALU.subtract))
            link(dve.tensor_copy(span_i[:, :], span[:, :]))
            link(dve.tensor_scalar(span_i[:, :], span_i[:, :], 6, None, ALU.logical_shift_right))
            dve.tensor_scalar(window_i[:, :, 1], span_i[:, 0:GROUPS_E], 1, None, ALU.add).then_inc(windows_ready, 1)
            dve.tensor_copy(window_i[:, :, 0], least[:, 0:GROUPS_E]).then_inc(windows_ready, 1)
            dve.wait_ge(base_turned, 1)
            link(dve.tensor_copy(base[:, :], s.ps[0][:, 400:400 + GROUPS_E]))
            dve.wait_ge(parts_turned, 3)
            turned = [s.ps[2 + i][0:TILE_E, 0:TILES_E].rearrange("p (g t) -> p g t", t=GROUP) for i in range(3)]
            dve.tensor_copy(table[0:TILE_E, :, 2, :], turned[0])
            dve.tensor_copy(table[0:TILE_E, :, 1, :], turned[1])
            rel = table[0:TILE_E, :, 3, :]
            key = table[0:TILE_E, :, 0, :]
            link(dve.tensor_tensor(rel, turned[2],
                                   base[0:TILE_E, :].unsqueeze(2).to_broadcast([TILE_E, GROUPS_E, GROUP]),
                                   ALU.subtract))
            link(dve.scalar_tensor_tensor(out=key, in0=table[0:TILE_E, :, 2, :], scalar=1.0, in1=rel,
                                          op0=ALU.add, op1=ALU.add))
            link(dve.scalar_tensor_tensor(out=key, in0=rel, scalar=float(WIN), in1=key, op0=ALU.is_lt, op1=ALU.mult))
            dve.tensor_scalar(key, key, 1.0, None, ALU.subtract).then_inc(visit_step, 1)
            dve.wait_ge(windows_ready, 2)
            dve.memset(test[:, 0:1], 0.0).then_inc(piece_added, 1)
            dve.memset(test[:, 1:2], 0.0).then_inc(slots_used, GROUP)
            STEPS = 7
            visit = dve.alloc_register("e_dve_visit")
            window_start = dve.alloc_register("e_window_start")
            dve.reg_mov(visit, 0)
            E_ = TILE_E
            with dve.Fori(0, GROUPS_E) as g:
                first = dve.value_load(window_i[0:1, bass.ds(g, 1), 0], min_val=0, max_val=N - 1)
                windows = dve.value_load(window_i[0:1, bass.ds(g, 1), 1], min_val=1, max_val=N // WIN + 1)
                dve.wait_ge(visit_step, dve.snap(visit) * STEPS + 1)
                dve.tensor_copy(mine[0:E_, :, :], table[0:E_, bass.ds(g, 1), :, :]
                                .rearrange("p g k t -> p (g k) t")).then_inc(group_step, 1)
                dve.reg_mov(window_start, first)
                with dve.Fori(0, windows):
                    v = dve.snap(visit)
                    dve.wait_ge(group_step, g + 1)
                    dve.wait_ge(visit_step, v * STEPS + 1)
                    for j in range(GROUP):
                        dve.wait_ge(slots_used, v * GROUP + (j + 1))
                        dve.tensor_scalar(one_key[0:E_, j, :], iota[0:E_, :], mine[0:E_, 0, j:j + 1], None, ALU.is_equal)
                        dve.tensor_scalar(one_src[0:E_, j, :], iota[0:E_, 0:P], mine[0:E_, 1, j:j + 1], None,
                                          ALU.is_equal).then_inc(onehots_ready, 1)
                    rel_m, key_m, high_m = mine[0:E_, 3, :], mine[0:E_, 0, :], mine[0:E_, 2, :]
                    dve.wait_ge(onehots_ready, (v + 1) * GROUP)
                    dve.tensor_scalar(rel_m, rel_m, float(WIN), None, ALU.subtract).then_inc(visit_step, 1)
                    dve.wait_ge(visit_step, v * STEPS + 2)
                    dve.scalar_tensor_tensor(out=key_m, in0=high_m, scalar=1.0, in1=rel_m, op0=ALU.add,
                                             op1=ALU.add).then_inc(visit_step, 1)
                    dve.wait_ge(visit_step, v * STEPS + 3)
                    dve.scalar_tensor_tensor(out=key_m, in0=rel_m, scalar=float(WIN), in1=key_m, op0=ALU.is_lt,
                                             op1=ALU.mult).then_inc(visit_step, 1)
                    dve.wait_ge(visit_step, v * STEPS + 4)
                    dve.scalar_tensor_tensor(out=key_m, in0=rel_m, scalar=0.0, in1=key_m, op0=ALU.is_ge,
                                             op1=ALU.mult).then_inc(visit_step, 1)
                    dve.wait_ge(visit_step, v * STEPS + 5)
                    dve.tensor_scalar(key_m, key_m, 1.0, None, ALU.subtract).then_inc(visit_step, 1)
                    dve.wait_ge(slots_used, v * GROUP + 2 * GROUP)
                    column = dve.snap(window_start, min_val=0, max_val=N - 1)
                    for half in range(2):
                        piece = s.CT[:, half * NT // 2:(half + 1) * NT // 2, bass.ds(column, WIN)]
                        dve.tensor_tensor(piece, piece, s.ps[6 + half][:, 0:KEYS // 2]
                                          .rearrange("p (c w) -> p c w", w=WIN), ALU.add).then_inc(visit_step, 1)
                    dve.nop().then_inc(piece_added, 1)
                    dve.reg_add(visit, visit, 1)
                    dve.reg_add(window_start, window_start, WIN)
            dve.wait_ge(visit_step, dve.snap(visit) * STEPS + 1)
            for t in range(NT):
                loop = s.CT[:, t, t * P:t * P + rows(t)]
                ins = dve.tensor_tensor(loop, loop, s.ident[:, 0:rows(t)], ALU.add)
            link(ins)

        @block.tensor
        def _(pe):
            pe.wait_ge(extent_ready, 1)
            for a in range(6):
                ins = pe.transpose(s.ps[a // 3][0:1, (a % 3) * P:(a % 3 + 1) * P], extent[:, a:a + 1], s.ident[:, :])
            ins.then_inc(extent_turned, 1)
            pe.wait_ge(least_ready, 1)
            pe.matmul(s.ps[0][:, 400:400 + GROUPS_E], s.ones[0:1, :], least[0:1, 0:GROUPS_E], start=True,
                      stop=True).then_inc(base_turned, 1)
            pe.wait_ge(parts_ready, 1)
            for i in range(3):
                for a, (at, k) in enumerate(chunks):
                    ins = pe.transpose(s.ps[2 + i][0:TILE_E, at:at + k], part_f[0:k, i, a, :], s.ident[0:k, 0:k])
                ins.then_inc(parts_turned, 1)
            pe.wait_ge(windows_ready, 2)
            visit = pe.alloc_register("e_pe_visit")
            pe.reg_mov(visit, 0)
            with pe.Fori(0, GROUPS_E) as g:
                windows = pe.value_load(window_i[0:1, bass.ds(g, 1), 1], min_val=1, max_val=N // WIN + 1)
                with pe.Fori(0, windows):
                    v = pe.snap(visit)
                    pe.wait_ge(piece_added, v + 1)
                    for j in range(GROUP):
                        pe.wait_ge(onehots_ready, v * GROUP + (j + 1))
                        for half in range(2):
                            ins = pe.matmul(s.ps[6 + half][:, 0:KEYS // 2], one_src[0:TILE_E, j, :],
                                            one_key[0:TILE_E, j, half * KEYS // 2:(half + 1) * KEYS // 2],
                                            start=(j == 0), stop=(j == GROUP - 1))
                        ins.then_inc(slots_used, 1)
                    pe.reg_add(visit, visit, 1)


def project_nodes(nc, s, tag, xt, weights, att_src, att_dst, heads, h_hi, h_lo, attention, load_xt=None):
    cols = weights.shape[1] // heads
    kc = weights.shape[0] // P
    xt_hi, xt_lo = xt
    with ExitStack() as scope:
        sb = lambda name, shape, dtype: sbuf(nc, scope, f"{tag}_{name}", shape, dtype)
        sem = lambda name: semaphore(nc, scope, f"{tag}_{name}")
        w32 = sb("w32", [P, kc, cols], F32)
        split_w = s.x1[:, :, :].rearrange("p t d -> p (t d)").bitcast(F16)[:, 0:4 * kc * cols].rearrange(
            "p (i a k n) -> p i a k n", i=2, a=2, k=kc)
        w_hi, w_lo = split_w[:, 0], split_w[:, 1]
        att = sb("att", [P, 2, 2, cols], F32)
        product = sb("product", [P, 2, cols], F32)
        w_loaded = sem("w_loaded")
        att_loaded = [sem(f"att_loaded{i}") for i in range(2)]
        w_hi_ready = sem("w_hi_ready")
        w_lo_ready = sem("w_lo_ready")
        summed = sem("summed")
        hi_ready = sem("hi_ready")
        lo_ready = sem("lo_ready")
        block = scope.enter_context(nc.Block())

        @block.sync
        def _(sp):
            for j in range(heads):
                if j >= 1:
                    sp.wait_ge(w_lo_ready, j)
                sp.dma_start(w32[:, :, :], weights[:, j * cols:(j + 1) * cols].rearrange("(k p) n -> p k n", p=P)
                             ).then_inc(w_loaded, 16)
                if j >= 2:
                    sp.wait_ge(lo_ready, NT * (j - 1))
                for i, vector in enumerate((att_src, att_dst)):
                    sp.dma_start(att[:, j % 2, i, :], vector[j:j + 1, :].to_broadcast([P, cols])
                                 ).then_inc(att_loaded[j % 2], 16)

        @block.scalar
        def _(act):
            def split(j):
                act.wait_ge(w_loaded, 16 * (j + 1))
                if j >= 2:
                    act.wait_ge(summed, NT * (j - 1))
                act.activation(w_hi[:, j % 2, :, :], w32[:, :, :], ACT.Copy, scale=WSCALE).then_inc(w_hi_ready, 1)

            split(0)
            for j in range(heads):
                if j + 1 < heads:
                    act.wait_ge(w_lo_ready, j + 1)
                    split(j + 1)
                for t in range(NT):
                    n = j * NT + t
                    act.wait_ge(summed, n + 1)
                    act.activation(h_hi[:, t, j * cols:(j + 1) * cols], s.ps[n % 4][:, 0:cols], ACT.Copy,
                                   scale=1 / WSCALE).then_inc(hi_ready, 1)

        @block.vector
        def _(dve):
            def split(j):
                dve.wait_ge(w_hi_ready, j + 1)
                dve.scalar_tensor_tensor(out=w_lo[:, j % 2, :, :], in0=w32[:, :, :], scalar=WSCALE,
                                         in1=w_hi[:, j % 2, :, :], op0=ALU.mult, op1=ALU.subtract
                                         ).then_inc(w_lo_ready, 1)

            split(0)
            for j in range(heads):
                if j + 1 < heads:
                    split(j + 1)
                dve.wait_ge(att_loaded[j % 2], 32 * (j // 2 + 1))
                for t in range(NT):
                    n = j * NT + t
                    dve.wait_ge(hi_ready, n + 1)
                    for i in range(2):
                        if n >= 1:
                            dve.wait_ge(lo_ready, n)
                        dve.tensor_tensor_reduce(out=product[:, i, :], in0=s.ps[n % 4][:, 0:cols],
                                                 in1=att[:, j % 2, i, :], scale=1 / WSCALE, scalar=0.0, op0=ALU.mult,
                                                 op1=ALU.add, accum_out=attention[:, t, i * heads + j:i * heads + j + 1])
                    dve.scalar_tensor_tensor(out=h_lo[:, t, j * cols:(j + 1) * cols], in0=s.ps[n % 4][:, 0:cols],
                                             scalar=1 / WSCALE, in1=h_hi[:, t, j * cols:(j + 1) * cols],
                                             op0=ALU.mult, op1=ALU.subtract).then_inc(lo_ready, 1)

        @block.tensor
        def _(pe):
            for j in range(heads):
                pe.wait_ge(w_lo_ready, j + 1)
                for t in range(NT):
                    n = j * NT + t
                    if n >= 4:
                        pe.wait_ge(lo_ready, n - 3)
                    for k in range(kc):
                        ins = pair_product(pe, s.ps[n % 4][:, 0:cols], xt_hi[:, k, t * P:(t + 1) * P],
                                           xt_lo[:, k, t * P:(t + 1) * P], w_hi[:, j % 2, k, :],
                                           w_lo[:, j % 2, k, :], k == 0, k == kc - 1)
                    ins.then_inc(summed, 1)


def edge_maxima(nc, s, tag, heads, attention, source02, offsets, offsets_b=None):
    with ExitStack() as scope:
        sb = lambda name, shape, dtype: sbuf(nc, scope, f"{tag}_{name}", shape, dtype)
        sem = lambda name: semaphore(nc, scope, f"{tag}_{name}")
        mask_t = sb("mask_t", [P, NT, N], BF16)
        mask = sb("mask", [P, 2, NPAD], BF16)
        att_rows = sb("att_rows", [8, NPAD], F32)
        att_b = sb("att_b", [P, heads, NPAD], F32)
        shifted = sb("shifted", [P, NPAD], F32)
        greatest = sb("greatest", [P, NT, heads], F32)
        maximum = sb("maximum", [P, NT, heads], F32)
        rest = sb("rest", [P, NT, 8], F32)
        dve_step = sem("dve_step")
        mask_ready = sem("mask_ready")
        rows_turned = sem("rows_turned")
        rows_ready = sem("rows_ready")
        spread = sem("spread")
        spread_copied = sem("spread_copied")
        mask_turned = sem("mask_turned")
        mask_copied = sem("mask_copied")
        tile_done = sem("tile_done")
        rest_ready = sem("rest_ready")
        rest_turned = sem("rest_turned")
        rest_copied = sem("rest_copied")
        offsets_ready = sem("offsets_ready")
        offsets_spread = sem("offsets_spread")
        width = [512, 512, NPAD - 1024]
        spreads = [(j, g) for j in range(heads) for g in range(3)]
        block = scope.enter_context(nc.Block())

        @block.vector
        def _(dve):
            steps = [0]

            def link(ins):
                steps[0] += 1
                ins.then_inc(dve_step, 1)
                dve.wait_ge(dve_step, steps[0])

            dve.tensor_scalar(mask_t[:, :, :], s.CT[:, :, 0:N], 0.0, NO_EDGE, ALU.is_equal, ALU.mult
                              ).then_inc(mask_ready, 1)
            dve.memset(greatest[:, :, :], 0.0)
            dve.memset(rest[:, :, :], 0.0)
            link(dve.tensor_scalar(source02[:, :, 0:heads], attention[:, :, 0:heads], SLOPE, None, ALU.mult))
            dve.wait_ge(spread_copied, len(spreads))
            for t in range(NT):
                dve.wait_ge(mask_copied, t + 1)
                for j in range(heads):
                    r = rows(t)
                    ins = dve.tensor_tensor_reduce(out=shifted[0:r, :], in0=mask[0:r, t % 2, :], in1=att_b[0:r, j, :],
                                                   scale=1.0, scalar=NO_EDGE * 2, op0=ALU.add, op1=ALU.max,
                                                   accum_out=greatest[0:r, t, j:j + 1])
                    link(ins)
                dve.nop().then_inc(tile_done, 1)
            dest = attention[:, :, heads:2 * heads]
            link(dve.tensor_tensor(maximum[:, :, :], greatest[:, :, :], dest, ALU.add))
            link(dve.scalar_tensor_tensor(out=maximum[:, :, :], in0=maximum[:, :, :], scalar=SLOPE,
                                          in1=maximum[:, :, :], op0=ALU.mult, op1=ALU.max))
            pairs = rest[:, :, :].rearrange("p t (j i) -> p t j i", i=2)
            dve.tensor_tensor(pairs[:, :, 0:heads, 0], dest, maximum[:, :, :], ALU.subtract)
            dve.scalar_tensor_tensor(out=pairs[:, :, 0:heads, 1], in0=dest, scalar=SLOPE, in1=maximum[:, :, :],
                                     op0=ALU.mult, op1=ALU.subtract).then_inc(rest_ready, 1)

        @block.tensor
        def _(pe):
            k = 2 * heads
            for t in range(NT):
                ins = pe.transpose(s.ps[t // 4][0:k, (t % 4) * P:(t % 4 + 1) * P], attention[:, t, 0:k], s.ident[:, :])
            ins.then_inc(rows_turned, 1)
            pe.wait_ge(rows_ready, 1)
            for n, (j, g) in enumerate(spreads):
                if n >= 2:
                    pe.wait_ge(spread_copied, n - 1)
                pe.matmul(s.ps[3 + n % 2][:, 0:width[g]], s.sel[0:k, j, :], att_rows[0:k, g * 512:g * 512 + width[g]],
                          start=True, stop=True).then_inc(spread, 1)
            pe.wait_ge(mask_ready, 1)
            for t in range(NT):
                if t >= 1:
                    if t >= 2:
                        pe.wait_ge(mask_copied, t - 1)
                lead, tail = mask_banks(s, t)
                for c in range(NT):
                    out = lead[0:rows(t), c * P:(c + 1) * P] if c < 8 else tail[0:rows(t), (c - 8) * P:(c - 7) * P]
                    ins = pe.transpose(out, mask_t[:, c, t * P:t * P + rows(t)], s.ident_bf[:, :])
                ins.then_inc(mask_turned, 1)
            pe.wait_ge(rest_ready, 1)
            for t in range(NT):
                ins = pe.transpose(s.ps[1 + t // 4][0:8, (t % 4) * P:(t % 4 + 1) * P], rest[:, t, :], s.ident[:, :])
            ins.then_inc(rest_turned, 1)
            if offsets_b is not None:
                pe.wait_ge(offsets_ready, 1)
                for i in range(2):
                    for g in range(3):
                        ins = pe.matmul(s.ps[[0, 1, 2, 5, 6, 7][3 * i + g]][:, 0:width[g]], s.sel[:, i, :],
                                        offsets[:, g * 512:g * 512 + width[g]], start=True, stop=True)
                ins.then_inc(offsets_spread, 1)

        @block.scalar
        def _(act):
            k = 2 * heads
            act.wait_ge(rows_turned, 1)
            for g in range(3):
                ins = act.activation(att_rows[0:k, g * 512:g * 512 + width[g]], s.ps[g][0:k, 0:width[g]], ACT.Copy)
            ins.then_inc(rows_ready, 1)
            for n, (j, g) in enumerate(spreads):
                act.wait_ge(spread, n + 1)
                act.activation(att_b[:, j, g * 512:g * 512 + width[g]], s.ps[3 + n % 2][:, 0:width[g]], ACT.Copy
                               ).then_inc(spread_copied, 1)
            for t in range(NT):
                act.wait_ge(mask_turned, t + 1)
                if t >= 2:
                    act.wait_ge(tile_done, t - 1)
                lead, tail = mask_banks(s, t)
                r = rows(t)
                act.activation(mask[0:r, t % 2, 0:1024], lead[0:r, :], ACT.Copy)
                act.activation(mask[0:r, t % 2, 1024:NPAD], tail[0:r, 0:NPAD - 1024], ACT.Copy).then_inc(mask_copied, 1)
            act.wait_ge(rest_turned, 1)
            for g in range(3):
                ins = act.activation(offsets[:, g * 512:g * 512 + width[g]], s.ps[1 + g][0:8, 0:width[g]], ACT.Copy)
            ins.then_inc(offsets_ready, 1)
            if offsets_b is not None:
                act.wait_ge(offsets_spread, 1)
                for i in range(2):
                    for g in range(3):
                        act.activation(offsets_b[:, i, g * 512:g * 512 + width[g]],
                                       s.ps[[0, 1, 2, 5, 6, 7][3 * i + g]][:, 0:width[g]], ACT.Copy)


def mask_banks(s, t):
    lead, tail = ((5, 6), (7, 0))[t % 2]
    return s.ps[lead][:, :].bitcast(BF16), s.ps[tail][:, :].bitcast(BF16)


class EdgeWeights:
    KP = NT // 2
    SLOTS = 4

    def __init__(self, nc, s, scope, tag, units, width, attention, source02, offsets, off_places, in_psum,
                 lo=None):
        self.in_psum = in_psum
        self.s, self.units, self.attention, self.source02 = s, units, attention, source02
        self.offsets, self.off_places = offsets, off_places
        self.steps = len(units) * self.KP
        self.hi = sbuf(nc, scope, f"{tag}_p_hi", [P, 2, NT, width], F16)
        self.lo = sbuf(nc, scope, f"{tag}_p_lo", [P, 2, NT, width], F16) if lo is None else lo
        self.work = sbuf(nc, scope, f"{tag}_work", [P, self.SLOTS, 2, width], F32)
        self.offsets_spread = semaphore(nc, scope, f"{tag}_offsets_spread")
        self.upper_ready = semaphore(nc, scope, f"{tag}_upper_ready")
        self.score_ready = semaphore(nc, scope, f"{tag}_score_ready")
        self.exp_ready = semaphore(nc, scope, f"{tag}_exp_ready")
        self.weight_ready = semaphore(nc, scope, f"{tag}_weight_ready")
        self.hi_ready = semaphore(nc, scope, f"{tag}_hi_ready")
        self.lo_ready = semaphore(nc, scope, f"{tag}_lo_ready")

    def place(self, n):
        u, q = divmod(n, self.KP)
        j, (at, w) = self.units[u]
        return u, 2 * q, j, at, w, self.work[:, n % self.SLOTS, :, 0:w]

    def spread(self, pe, u):
        j, (at, w) = self.units[u]
        if u >= 2:
            pe.wait_ge(self.score_ready, NT * (u - 1))
        for i in range(2):
            ins = pe.matmul(self.off_places(u)[i], self.s.sel[:, 2 * j + i, :],
                            self.offsets[:, at:at + w], start=True, stop=True)
        ins.then_inc(self.offsets_spread, 1)

    def act_upper(self, act, n):
        u, k, j, at, w, work = self.place(n)
        if k == 0 and self.in_psum:
            act.wait_ge(self.offsets_spread, u + 1)
        if n >= self.SLOTS:
            act.wait_ge(self.lo_ready, n - self.SLOTS + 1)
        for i in range(2):
            act.activation(work[:, i, :], self.off_places(u)[0], ACT.Identity,
                           bias=self.attention[:, k + i, j:j + 1]).then_inc(self.upper_ready, 1)

    def dve_score(self, dve, n):
        u, k, j, at, w, work = self.place(n)
        for i in range(2):
            dve.wait_ge(self.upper_ready, 2 * n + i + 1)
            dve.scalar_tensor_tensor(out=work[:, i, :], in0=self.off_places(u)[1],
                                     scalar=self.source02[:, k + i, j:j + 1], in1=work[:, i, :],
                                     op0=ALU.add, op1=ALU.max).then_inc(self.score_ready, 1)

    def act_exp(self, act, n):
        work = self.place(n)[-1]
        act.wait_ge(self.score_ready, 2 * n + 2)
        act.activation(work, work, ACT.Exp).then_inc(self.exp_ready, 1)

    def dve_weight(self, dve, n):
        u, k, j, at, w, work = self.place(n)
        dve.wait_ge(self.exp_ready, n + 1)
        dve.scalar_tensor_tensor(out=work, in0=work, scalar=1.0, in1=self.s.CT[:, k:k + 2, at:at + w],
                                 op0=ALU.min, op1=ALU.mult).then_inc(self.weight_ready, 1)

    def act_hi(self, act, n, used, per_unit):
        u, k, j, at, w, work = self.place(n)
        act.wait_ge(self.weight_ready, n + 1)
        if u >= 2:
            act.wait_ge(used, per_unit * (u - 1))
        act.activation(self.hi[:, u % 2, k:k + 2, 0:w], work, ACT.Copy).then_inc(self.hi_ready, 1)

    def pool_lo(self, pool, n):
        u, k, j, at, w, work = self.place(n)
        pool.wait_ge(self.hi_ready, n + 1)
        pool.tensor_tensor(self.lo[:, u % 2, k:k + 2, 0:w], work, self.hi[:, u % 2, k:k + 2, 0:w], ALU.subtract
                           ).then_inc(self.lo_ready, 1)


def aggregate_heads(nc, s, attention, source02, offsets, h_hi, h_lo, bias, scratch_hi, scratch_lo):
    units = [(j, block) for j in range(HEADS) for block in BLOCKS]
    HCC = HID // P
    chunks = len(units) * HCC
    with ExitStack() as scope:
        sb = lambda name, shape, dtype: sbuf(nc, scope, f"g1_{name}", shape, dtype)
        sem = lambda name: semaphore(nc, scope, f"g1_{name}")

        def off_places(u):
            return [s.ps[2 * (u % 2) + i][:, 0:units[u][1][1]] for i in range(2)]

        DEN, AGG = s.ps[4], (s.ps[5], s.ps[6], s.ps[7])
        spare = s.x1[:, :, :].rearrange("p t d -> p (t d)").bitcast(F16)[:, 0:2 * NT * 512]
        weights = EdgeWeights(nc, s, scope, "g1", units, 512, attention, source02, offsets, off_places,
                              True, lo=spare.rearrange("p (a t w) -> p a t w", a=2, t=NT))
        inverse = sb("inverse", [P, 2, 512], F32)
        value = sb("value", [P, 2, 512], F32)
        expd = sb("expd", [P, 2, 512], F32)
        out_hi = sb("out_hi", [P, 2, 512], F16)
        out_lo = sb("out_lo", [P, 2, 512], F16)
        b1 = sb("b1", [P, HC], F32)
        b1_loaded = sem("b1_loaded")
        den_summed = sem("den_summed")
        inverse_ready = sem("inverse_ready")
        summed = sem("summed")
        scaled = sem("scaled")
        exp2_ready = sem("exp2_ready")
        relu_ready = sem("relu_ready")
        elu_ready = sem("elu_ready")
        out_hi_ready = sem("out_hi_ready")
        out_lo_ready = sem("out_lo_ready")
        stored = [sem(f"stored{i}") for i in range(2)]
        block = scope.enter_context(nc.Block())

        def width(c):
            return units[c // HCC][1][1]

        slot_after = {u * EdgeWeights.KP + i + 2: (u - 1) * HCC + i for u in range(1, len(units)) for i in range(HCC)}
        last_slots = range((len(units) - 1) * HCC, chunks + 2)

        @block.sync
        def _(sp):
            with nc.allow_non_contiguous_dma(reason="one short vector per partition"):
                sp.dma_start(b1[:, :], bias.rearrange("(c p) -> p c", p=P)).then_inc(b1_loaded, 16)
            for n in range(chunks):
                (j, (at, w)), c = units[n // HCC], n % HCC
                sp.wait_ge(out_lo_ready, n + 1)
                sp.dma_start(scratch_hi[j * HCC + c, :, at:at + w], out_hi[:, n % 2, 0:w]).then_inc(stored[n % 2], 16)
                sp.dma_start(scratch_lo[j * HCC + c, :, at:at + w], out_lo[:, n % 2, 0:w]).then_inc(stored[n % 2], 16)
            for i in range(2):
                sp.wait_ge(stored[i], 32 * (chunks // 2))

        @block.scalar
        def _(act):
            def finish(slot):
                if 0 <= slot - 1 < chunks:
                    n = slot - 1
                    w = width(n)
                    act.wait_ge(elu_ready, n + 1)
                    if n >= 2:
                        act.wait_ge(stored[n % 2], 32 * (n // 2))
                    act.activation(out_hi[:, n % 2, 0:w], value[:, n % 2, 0:w], ACT.Copy, bias=-1.0
                                   ).then_inc(out_hi_ready, 1)
                if slot < chunks:
                    n = slot
                    w = width(n)
                    col = units[n // HCC][0] * HCC + n % HCC
                    act.wait_ge(scaled, n + 1)
                    act.activation(expd[:, n % 2, 0:w], value[:, n % 2, 0:w], ACT.Exp, bias=b1[:, col:col + 1]
                                   ).then_inc(exp2_ready, 1)
                    act.wait_ge(exp2_ready, n + 1)
                    act.activation(value[:, n % 2, 0:w], value[:, n % 2, 0:w], ACT.Relu, bias=b1[:, col:col + 1]
                                   ).then_inc(relu_ready, 1)

            act.wait_ge(b1_loaded, 16)
            for n in range(weights.steps + 2):
                if n < weights.steps:
                    weights.act_upper(act, n)
                if 0 <= n - 1 < weights.steps:
                    weights.act_exp(act, n - 1)
                if 0 <= n - 2:
                    weights.act_hi(act, n - 2, summed, HCC)
                if n in slot_after:
                    finish(slot_after[n])
            for slot in last_slots:
                finish(slot)

        @block.vector
        def _(dve):
            def finish(slot):
                if 0 <= slot - 2 < chunks:
                    n = slot - 2
                    w = width(n)
                    dve.wait_ge(out_hi_ready, n + 1)
                    dve.scalar_tensor_tensor(out=out_lo[:, n % 2, 0:w], in0=value[:, n % 2, 0:w], scalar=1.0,
                                             in1=out_hi[:, n % 2, 0:w], op0=ALU.subtract, op1=ALU.subtract
                                             ).then_inc(out_lo_ready, 1)
                if 0 <= slot - 1 < chunks:
                    n = slot - 1
                    w = width(n)
                    dve.wait_ge(relu_ready, n + 1)
                    dve.scalar_tensor_tensor(out=value[:, n % 2, 0:w], in0=expd[:, n % 2, 0:w], scalar=1.0,
                                             in1=value[:, n % 2, 0:w], op0=ALU.min, op1=ALU.add).then_inc(elu_ready, 1)
                if slot < chunks:
                    n = slot
                    w = width(n)
                    u = n // HCC
                    if n % HCC == 0:
                        dve.wait_ge(den_summed, u + 1)
                        dve.reciprocal(inverse[:, u % 2, 0:w], DEN[:, 0:w]).then_inc(inverse_ready, 1)
                        dve.wait_ge(inverse_ready, u + 1)
                    dve.wait_ge(summed, n + 1)
                    if n >= 2:
                        dve.wait_ge(out_lo_ready, n - 1)
                    dve.tensor_tensor(value[:, n % 2, 0:w], AGG[n % 3][:, 0:w], inverse[:, u % 2, 0:w],
                                      ALU.mult).then_inc(scaled, 1)

            for n in range(weights.steps + 1):
                if n < weights.steps:
                    weights.dve_score(dve, n)
                if n >= 1:
                    weights.dve_weight(dve, n - 1)
                if n in slot_after:
                    finish(slot_after[n])
            for slot in last_slots:
                finish(slot)

        @block.gpsimd
        def _(pool):
            for n in range(weights.steps):
                weights.pool_lo(pool, n)

        @block.tensor
        def _(pe):
            weights.spread(pe, 0)
            weights.spread(pe, 1)
            for u, (j, (at, w)) in enumerate(units):
                pe.wait_ge(weights.lo_ready, EdgeWeights.KP * (u + 1))
                if u + 2 < len(units):
                    weights.spread(pe, u + 2)
                p_hi, p_lo = weights.hi[:, u % 2, :, 0:w], weights.lo[:, u % 2, :, 0:w]
                if u >= 1:
                    pe.wait_ge(inverse_ready, u)
                for k in range(NT):
                    pe.matmul(DEN[:, 0:w], s.ones16[:, :], p_hi[:, k, :], start=(k == 0), stop=False)
                    ins = pe.matmul(DEN[:, 0:w], s.ones16[:, :], p_lo[:, k, :], start=False, stop=(k == NT - 1))
                ins.then_inc(den_summed, 1)
                for c in range(HCC):
                    n = u * HCC + c
                    if n >= 3:
                        pe.wait_ge(scaled, n - 2)
                    cols = slice((j * HCC + c) * P, (j * HCC + c + 1) * P)
                    for k in range(NT):
                        ins = pair_product(pe, AGG[n % 3][:, 0:w], h_hi[:, k, cols], h_lo[:, k, cols],
                                           p_hi[:, k, :], p_lo[:, k, :], k == 0, k == NT - 1)
                    ins.then_inc(summed, 1)


def project_hidden(nc, s, weights, att_src, att_dst, scratch_hi, scratch_lo, h_hi, h_lo, attention):
    KQ = 2
    with ExitStack() as scope:
        sb = lambda name, shape, dtype: sbuf(nc, scope, f"p2_{name}", shape, dtype)
        sem = lambda name: semaphore(nc, scope, f"p2_{name}")
        w32 = sb("w32", [P, 2, KQ, D], F32)
        w_hi = sb("w_hi", [P, HC, D], F16)
        w_lo = sb("w_lo", [P, HC, D], F16)
        x_hi = sb("x_hi", [P, 2, HC, 256], F16)
        x_lo = sb("x_lo", [P, 2, HC, 256], F16)
        att = sb("att", [P, 2, D], F32)
        product = sb("product", [P, 2, DHALF], F32)
        halves = sb("halves", [P, NT, 2, 2], F32)
        w_loaded = [sem(f"w_loaded{i}") for i in range(2)]
        x_loaded = [sem(f"x_loaded{i}") for i in range(2)]
        att_loaded = sem("att_loaded")
        w_hi_ready = sem("w_hi_ready")
        w_lo_ready = sem("w_lo_ready")
        summed = sem("summed")
        hi_ready = sem("hi_ready")
        lo_ready = sem("lo_ready")
        scored = sem("scored")
        block = scope.enter_context(nc.Block())
        blocks = [(at, min(256, N - at)) for at in range(0, N, 256)]

        @block.sync
        def _(sp):
            for q in range(HC // KQ):
                if q >= 2:
                    sp.wait_ge(w_lo_ready, q - 1)
                sp.dma_start(w32[:, q % 2, :, :], weights[q * KQ * P:(q + 1) * KQ * P, :]
                             .rearrange("(k p) n -> p k n", p=P)).then_inc(w_loaded[q % 2], 16)

        @block.gpsimd
        def _(pool):
            for i, vector in enumerate((att_src, att_dst)):
                pool.dma_start(att[:, i, :], vector[0:1, :].to_broadcast([P, D])).then_inc(att_loaded, 16)
            for b, (at, w) in enumerate(blocks):
                if b >= 2:
                    pool.wait_ge(summed, 4 * (b - 1))
                for tile, dram in ((x_hi, scratch_hi), (x_lo, scratch_lo)):
                    pool.dma_start(tile[:, b % 2, :, 0:w], dram[:, :, at:at + w].rearrange("c p n -> p c n")
                                   ).then_inc(x_loaded[b % 2], 16)

        @block.scalar
        def _(act):
            for q in range(HC // KQ):
                act.wait_ge(w_loaded[q % 2], 16 * (q // 2 + 1))
                act.activation(w_hi[:, q * KQ:(q + 1) * KQ, :], w32[:, q % 2, :, :], ACT.Copy, scale=WSCALE
                               ).then_inc(w_hi_ready, 1)
            for n in range(2 * NT):
                t, half = divmod(n, 2)
                r, cols = rows(t), slice(half * DHALF, (half + 1) * DHALF)
                act.wait_ge(summed, n + 1)
                act.activation(h_hi[0:r, t, cols], s.ps[n % 6][0:r, 0:DHALF], ACT.Copy, scale=1 / WSCALE
                               ).then_inc(hi_ready, 1)

        @block.vector
        def _(dve):
            for q in range(HC // KQ):
                dve.wait_ge(w_hi_ready, q + 1)
                ks = slice(q * KQ, (q + 1) * KQ)
                dve.scalar_tensor_tensor(out=w_lo[:, ks, :], in0=w32[:, q % 2, :, :], scalar=WSCALE,
                                         in1=w_hi[:, ks, :], op0=ALU.mult, op1=ALU.subtract).then_inc(w_lo_ready, 1)
            dve.memset(h_hi[:, :, D:D + 2], 0.0)
            dve.memset(h_lo[:, :, D:D + 2], 0.0)
            dve.memset(h_hi[96:P, NT - 1, 0:D], 0.0)
            dve.memset(h_lo[96:P, NT - 1, 0:D], 0.0)
            dve.memset(halves[:, :, :, :], 0.0).then_inc(scored, 1)
            dve.wait_ge(att_loaded, 32)
            dve.wait_ge(scored, 1)
            dve.memset(h_hi[:, :, D:D + 1], 1.0)
            for n in range(2 * NT):
                t, half = divmod(n, 2)
                r, cols = rows(t), slice(half * DHALF, (half + 1) * DHALF)
                dve.wait_ge(hi_ready, n + 1)
                if n >= 1:
                    dve.wait_ge(lo_ready, n)
                for i in range(2):
                    dve.tensor_tensor_reduce(out=product[0:r, i, :], in0=s.ps[n % 6][0:r, 0:DHALF],
                                             in1=att[0:r, i, cols], scale=1 / WSCALE, scalar=0.0, op0=ALU.mult,
                                             op1=ALU.add, accum_out=halves[0:r, t, i, half:half + 1])
                dve.scalar_tensor_tensor(out=h_lo[0:r, t, cols], in0=s.ps[n % 6][0:r, 0:DHALF], scalar=1 / WSCALE,
                                         in1=h_hi[0:r, t, cols], op0=ALU.mult, op1=ALU.subtract).then_inc(lo_ready, 1)
            dve.wait_ge(lo_ready, 2 * NT)
            dve.tensor_tensor(attention[:, :, 0:2], halves[:, :, :, 0], halves[:, :, :, 1], ALU.add)

        @block.tensor
        def _(pe):
            pe.wait_ge(w_lo_ready, HC // KQ)
            pe.wait_ge(scored, 1)
            for n in range(2 * NT):
                t, half = divmod(n, 2)
                r, cols = rows(t), slice(half * DHALF, (half + 1) * DHALF)
                b, at = t // 2, (t % 2) * P
                pe.wait_ge(x_loaded[b % 2], 32 * (b // 2 + 1))
                if n >= 6:
                    pe.wait_ge(lo_ready, n - 5)
                for k in range(HC):
                    ins = pair_product(pe, s.ps[n % 6][0:r, 0:DHALF], x_hi[:, b % 2, k, at:at + r],
                                       x_lo[:, b % 2, k, at:at + r], w_hi[:, k, cols], w_lo[:, k, cols],
                                       k == 0, k == HC - 1)
                ins.then_inc(summed, 1)


def aggregate_nodes(nc, s, attention, source02, offsets_b, h_hi, h_lo, x_dram, bias, x1):
    units = [(0, (at, min(256, N - at))) for at in range(0, N, 256)]
    with ExitStack() as scope:
        sb = lambda name, shape, dtype: sbuf(nc, scope, f"g2_{name}", shape, dtype)
        sem = lambda name: semaphore(nc, scope, f"g2_{name}")

        def off_places(u):
            at, w = units[u][1]
            return [offsets_b[:, i, at:at + w] for i in range(2)]

        weights = EdgeWeights(nc, s, scope, "g2", units, 256, attention, source02, None, off_places, False)
        b2 = sb("b2", [P, D], F32)
        inverse = sb("inverse", [P, NT], F32)
        loaded = sem("loaded")
        pads_zeroed = sem("pads_zeroed")
        based = sem("based")
        summed = sem("summed")
        inverse_ready = sem("inverse_ready")
        added = sem("added")
        block = scope.enter_context(nc.Block())

        @block.sync
        def _(sp):
            sp.dma_start(b2[:, :], bias.rearrange("(a d) -> a d", a=1).to_broadcast([P, D])).then_inc(loaded, 16)
            sp.wait_ge(pads_zeroed, 1)
            load_nodes(sp, x1, x_dram, loaded)

        @block.scalar
        def _(act):
            for n in range(weights.steps + 2):
                if n < weights.steps:
                    weights.act_upper(act, n)
                if 0 <= n - 1 < weights.steps:
                    weights.act_exp(act, n - 1)
                if 0 <= n - 2:
                    weights.act_hi(act, n - 2, summed, 2)

        @block.vector
        def _(dve):
            def finish(t):
                r = rows(t)
                lead, tail = s.ps[2 + 2 * (t % 3)], s.ps[3 + 2 * (t % 3)]
                dve.wait_ge(summed, t + 1)
                dve.reciprocal(inverse[0:r, t:t + 1], tail[0:r, DHALF:DHALF + 1]).then_inc(inverse_ready, 1)
                dve.wait_ge(inverse_ready, t + 1)
                for half, bank in ((0, lead), (1, tail)):
                    cols = slice(half * DHALF, (half + 1) * DHALF)
                    dve.scalar_tensor_tensor(out=x1[0:r, t, cols], in0=bank[0:r, 0:DHALF],
                                             scalar=inverse[0:r, t:t + 1], in1=x1[0:r, t, cols], op0=ALU.mult,
                                             op1=ALU.add).then_inc(added, 1)

            dve.memset(x1[96:P, NT - 1, :], 0.0).then_inc(pads_zeroed, 1)
            for n in range(weights.steps + 1):
                if n < weights.steps:
                    weights.dve_score(dve, n)
                if n >= 1:
                    weights.dve_weight(dve, n - 1)
                if n == 0:
                    dve.wait_ge(loaded, 48)
                    for t in range(NT):
                        dve.tensor_tensor(x1[0:rows(t), t, :], x1[0:rows(t), t, :], b2[0:rows(t), :], ALU.add
                                          ).then_inc(based, 1)
                    dve.wait_ge(based, NT)
                u, q = divmod(n, EdgeWeights.KP)
                if 1 <= u < len(units) and q in (2, 4):
                    finish(2 * (u - 1) + q // 2 - 1)
            finish(NT - 2)
            finish(NT - 1)

        @block.gpsimd
        def _(pool):
            for n in range(weights.steps):
                weights.pool_lo(pool, n)

        @block.tensor
        def _(pe):
            for t in range(NT):
                u, at = t // 2, (t % 2) * P
                r = rows(t)
                if t % 2 == 0:
                    pe.wait_ge(weights.lo_ready, EdgeWeights.KP * (u + 1))
                if t >= 3:
                    pe.wait_ge(added, 2 * (t - 2))
                lead, tail = s.ps[2 + 2 * (t % 3)], s.ps[3 + 2 * (t % 3)]
                for half, bank in ((0, lead), (1, tail)):
                    cols = slice(half * DHALF, (half + 1) * DHALF + half)
                    out = bank[0:r, 0:DHALF + half]
                    for k in range(NT):
                        ins = pair_product(pe, out, weights.hi[:, u % 2, k, at:at + r],
                                           weights.lo[:, u % 2, k, at:at + r], h_hi[:, k, cols], h_lo[:, k, cols],
                                           k == 0, k == NT - 1)
                ins.then_inc(summed, 1)


def attend(nc, s, xt, w_qkv, out_hi, out_lo):
    SLOTS = len(BLOCKS) * NT
    WIDTH = [512, 512, NPAD - 1024]
    scale = float(HD) ** -0.5
    jobs = [("qk", m, g) for m in range(2) for g in range(3)] + [("v", 2, g) for g in range(3)]
    QKV_JOBS = len(jobs)
    jobs += [("max", hd, t, g) for hd in range(2) for t in range(NT) for g in range(3)]
    MAX_JOBS = len(jobs) - QKV_JOBS
    jobs += [("row", hd, g) for hd in range(2) for g in range(3)]
    JOBS = len(jobs)
    plan = [[] for _ in range(SLOTS)]
    for n in range(QKV_JOBS):
        plan[n].append(n)
    for n in range(MAX_JOBS):
        plan[QKV_JOBS + n * 17 // MAX_JOBS].append(QKV_JOBS + n)
    for n in range(6):
        plan[27 + n // 3].append(QKV_JOBS + MAX_JOBS + n)
    act_jobs = [n for n, job in enumerate(jobs) if job[0] != "max"]
    SPLIT_SLOT = 12
    with ExitStack() as scope:
        sb = lambda name, shape, dtype: sbuf(nc, scope, f"a_{name}", shape, dtype)
        sem = lambda name: semaphore(nc, scope, f"a_{name}")
        w32 = sb("w32", [P, 2, DC, P], F32)
        w_hi = sb("w_hi", [P, 3, DC, P], F16)
        w_lo = sb("w_lo", [P, 3, DC, P], F16)
        q1, q2, k1, k2 = (sb(name, [P, 2, 2, NPAD], F16) for name in ("q1", "q2", "k1", "k2"))
        v_hi = sb("v_hi", [P, 2, NT, P], F16)
        v_lo = sb("v_lo", [P, 2, NT, P], F16)
        maxima = sb("maxima", [P, 2 * NT, 3], F32)
        minus_max = sb("minus_max", [P, 2 * NT], F32)
        row_hi = sb("row_hi", [1, 512], F16)
        work = sb("work", [P, 3, 2, 512], F32)
        p_hi = sb("p_hi", [P, 3, 2, 512], F16)
        p_lo = sb("p_lo", [P, 3, 2, 512], F16)
        inverse = sb("inverse", [P, 512], F32)
        value = sb("value", [P, 2, 512], F32)
        w_loaded = [sem(f"w_loaded{i}") for i in range(2)]
        zeroed = sem("zeroed")
        constants_ready = sem("constants_ready")
        w_hi_ready = sem("w_hi_ready")
        w_lo_ready = sem("w_lo_ready")
        job_product = sem("job_product")
        job_act = sem("job_act")
        job_dve = sem("job_dve")
        maxima_ready = sem("maxima_ready")
        scores_ready = sem("scores_ready")
        exp_ready = sem("exp_ready")
        hi_ready = sem("hi_ready")
        lo_ready = sem("lo_ready")
        pv_done = sem("pv_done")
        inverse_ready = sem("inverse_ready")
        value_ready = sem("value_ready")
        out_hi_ready = sem("out_hi_ready")
        out_lo_ready = sem("out_lo_ready")
        ACC, DEN = s.ps[4], s.ps[5]
        blocks_done = PAIRS * len(BLOCKS)
        block = scope.enter_context(nc.Block())

        def slot(n):
            i, r = divmod(n, SLOTS)
            b, k = divmod(r, NT)
            return i, b, k, BLOCKS[b][0], BLOCKS[b][1], rows(k)

        def job_bank(i, n):
            return s.ps[6 + (i * JOBS + n) % 2]

        def act_count(i, n):
            return i * len(act_jobs) + sum(m <= n for m in act_jobs)

        def finish_hi(act, nb):
            i, b = divmod(nb, len(BLOCKS))
            at, w = BLOCKS[b]
            act.wait_ge(value_ready, nb + 1)
            act.activation(out_hi[:, i, at:at + w], value[:, nb % 2, 0:w], ACT.Copy).then_inc(out_hi_ready, 1)

        def finish_value(dve, nb):
            w = BLOCKS[nb % len(BLOCKS)][1]
            dve.wait_ge(pv_done, NT * (nb + 1))
            dve.reciprocal(inverse[:, 0:w], DEN[:, 0:w]).then_inc(inverse_ready, 1)
            dve.wait_ge(inverse_ready, nb + 1)
            dve.tensor_tensor(value[:, nb % 2, 0:w], ACC[:, 0:w], inverse[:, 0:w], ALU.mult).then_inc(value_ready, 1)

        def finish_lo(dve, nb):
            i, b = divmod(nb, len(BLOCKS))
            at, w = BLOCKS[b]
            dve.wait_ge(out_hi_ready, nb + 1)
            dve.tensor_tensor(out_lo[:, i, at:at + w], value[:, nb % 2, 0:w], out_hi[:, i, at:at + w], ALU.subtract
                              ).then_inc(out_lo_ready, 1)

        @block.sync
        def _(sp):
            for n in range(3 * PAIRS):
                i, m = divmod(n, 3)
                if n >= 2:
                    sp.wait_ge(w_lo_ready, n - 1)
                sp.dma_start(w32[:, n % 2, :, :], w_qkv[:, m * D + i * P:m * D + (i + 1) * P]
                             .rearrange("(k p) n -> p k n", p=P)).then_inc(w_loaded[n % 2], 16)

        @block.gpsimd
        def _(pool):
            pool.memset(q2[:, :, :, :], 0.0).then_inc(zeroed, 1)
            pool.memset(k2[:, :, :, :], 0.0).then_inc(zeroed, 1)
            pool.memset(maxima[:, :, :], 0.0).then_inc(zeroed, 1)
            pool.wait_ge(zeroed, 3)
            for hd, b in ((0, 64), (1, 0)):
                pool.memset(k2[b:b + 1, :, hd, :], 1.0)
                ins = pool.memset(k2[b + 32:b + 33, :, hd, :], 1.0)
            ins.then_inc(constants_ready, 1)

        @block.scalar
        def _(act):
            def split(i):
                for m in range(3):
                    n = 3 * i + m
                    act.wait_ge(w_loaded[n % 2], 16 * (n // 2 + 1))
                    if i >= 1:
                        act.wait_ge(job_product, (i - 1) * JOBS + QKV_JOBS)
                    act.activation(w_hi[:, m, :, :], w32[:, n % 2, :, :], ACT.Copy, scale=WSCALE).then_inc(w_hi_ready, 1)

            def job(i, n):
                kind, *what = jobs[n]
                if kind == "max":
                    return
                bank = job_bank(i, n)
                act.wait_ge(job_product, i * JOBS + n + 1)
                if kind == "qk":
                    m, g = what
                    first = (q1, k1)[m]
                    w = WIDTH[g]
                    act.activation(first[0:64, i % 2, 0, g * 512:g * 512 + w], bank[0:64, 0:w], ACT.Copy,
                                   scale=1 / WSCALE)
                    ins = act.activation(first[64:P, i % 2, 1, g * 512:g * 512 + w], bank[64:P, 0:w], ACT.Copy,
                                         scale=1 / WSCALE)
                elif kind == "v":
                    g = what[1]
                    tiles = slice(4 * g, min(4 * g + 4, NT))
                    ins = act.activation(v_hi[:, i % 2, tiles, :].rearrange("p t n -> p (t n)"), bank[:, 0:WIDTH[g]],
                                         ACT.Copy, scale=1 / WSCALE)
                else:
                    hd, g = what
                    w, b = WIDTH[g], (64, 0)[hd]
                    if hd + g > 0:
                        act.wait_ge(job_dve, i * JOBS + n)
                    act.activation(row_hi[0:1, 0:w], bank[0:1, 0:w], ACT.Copy)
                    ins = act.activation(q2[b:b + 1, i % 2, hd, g * 512:g * 512 + w], bank[0:1, 0:w], ACT.Copy)
                ins.then_inc(job_act, 1)

            act.wait_ge(zeroed, 3)
            split(0)
            for n in range(JOBS):
                job(0, n)
            split(1)
            for n in range(PAIRS * SLOTS):
                i, b, k, at, w, r = slot(n)
                act.wait_ge(scores_ready, n + 1)
                if n >= 3:
                    act.wait_ge(lo_ready, n - 2)
                for hd in range(2):
                    ins = act.activation(work[0:r, n % 3, hd, 0:w], s.ps[2 * (n % 2) + hd][0:r, 0:w], ACT.Exp,
                                         scale=scale)
                ins.then_inc(exp_ready, 1)
                act.wait_ge(exp_ready, n + 1)
                if n >= 3:
                    act.wait_ge(pv_done, n - 2)
                act.activation(p_hi[0:r, n % 3, :, 0:w], work[0:r, n % 3, :, 0:w], ACT.Copy).then_inc(hi_ready, 1)
                if k == 1 and n > 1:
                    finish_hi(act, n // NT - 1)
                if i + 1 < PAIRS:
                    for j in plan[n % SLOTS]:
                        job(i + 1, j)
                    if n % SLOTS == SPLIT_SLOT and i + 2 < PAIRS:
                        split(i + 2)
            finish_hi(act, blocks_done - 1)

        @block.vector
        def _(dve):
            def split(i):
                for m in range(3):
                    n = 3 * i + m
                    dve.wait_ge(w_hi_ready, n + 1)
                    dve.scalar_tensor_tensor(out=w_lo[:, m, :, :], in0=w32[:, n % 2, :, :], scalar=WSCALE,
                                             in1=w_hi[:, m, :, :], op0=ALU.mult, op1=ALU.subtract
                                             ).then_inc(w_lo_ready, 1)

            def job(i, n):
                kind, *what = jobs[n]
                bank = job_bank(i, n)
                if kind == "qk":
                    m, g = what
                    w = WIDTH[g]
                    cols = slice(g * 512, g * 512 + w)
                    first = (q1, k1)[m]
                    dve.wait_ge(job_act, act_count(i, n))
                    for hd, (a, b) in enumerate(((0, 64), (64, 0))):
                        hi = first[a:a + 64, i % 2, hd, cols]
                        lo = q2[a:a + 64, i % 2, hd, cols] if m == 0 else k1[b:b + 64, i % 2, hd, cols]
                        again = q1[b:b + 64, i % 2, hd, cols] if m == 0 else k2[a:a + 64, i % 2, hd, cols]
                        dve.scalar_tensor_tensor(out=lo, in0=bank[a:a + 64, 0:w], scalar=1 / WSCALE, in1=hi,
                                                 op0=ALU.mult, op1=ALU.subtract)
                        ins = dve.tensor_copy(again, hi)
                elif kind == "v":
                    g = what[1]
                    tiles = slice(4 * g, min(4 * g + 4, NT))
                    dve.wait_ge(job_act, act_count(i, n))
                    ins = dve.scalar_tensor_tensor(
                        out=v_lo[:, i % 2, tiles, :].rearrange("p t n -> p (t n)"), in0=bank[:, 0:WIDTH[g]],
                        scalar=1 / WSCALE, in1=v_hi[:, i % 2, tiles, :].rearrange("p t n -> p (t n)"),
                        op0=ALU.mult, op1=ALU.subtract)
                elif kind == "max":
                    hd, t, g = what
                    dve.wait_ge(job_product, i * JOBS + n + 1)
                    ins = dve.tensor_reduce(maxima[0:rows(t), hd * NT + t, g:g + 1], bank[0:rows(t), 0:BLOCKS[g][1]],
                                            AX.X, ALU.max)
                else:
                    hd, g = what
                    w, b = WIDTH[g], (64, 0)[hd]
                    dve.wait_ge(job_act, act_count(i, n))
                    ins = dve.tensor_tensor(q2[b + 32:b + 33, i % 2, hd, g * 512:g * 512 + w], bank[0:1, 0:w],
                                            row_hi[0:1, 0:w], ALU.subtract)
                ins.then_inc(job_dve, 1)
                if n == QKV_JOBS + MAX_JOBS - 1:
                    dve.wait_ge(job_dve, i * JOBS + n + 1)
                    dve.tensor_reduce(minus_max[:, :], maxima[:, :, :], AX.X, ALU.max).then_inc(maxima_ready, 1)
                    dve.wait_ge(maxima_ready, 2 * i + 1)
                    dve.tensor_scalar(minus_max[:, :], minus_max[:, :], -1.0, None, ALU.mult).then_inc(maxima_ready, 1)

            dve.wait_ge(constants_ready, 1)
            split(0)
            for n in range(JOBS):
                job(0, n)
            split(1)
            for n in range(PAIRS * SLOTS):
                i, b, k, at, w, r = slot(n)
                if k == 1 and n > 1:
                    finish_value(dve, n // NT - 1)
                dve.wait_ge(hi_ready, n + 1)
                dve.tensor_tensor(p_lo[0:r, n % 3, :, 0:w], work[0:r, n % 3, :, 0:w], p_hi[0:r, n % 3, :, 0:w],
                                  ALU.subtract).then_inc(lo_ready, 1)
                if k == 1 and n > 1:
                    finish_lo(dve, n // NT - 1)
                if i + 1 < PAIRS:
                    for j in plan[n % SLOTS]:
                        job(i + 1, j)
                    if n % SLOTS == SPLIT_SLOT and i + 2 < PAIRS:
                        split(i + 2)
            finish_value(dve, blocks_done - 1)
            finish_lo(dve, blocks_done - 1)

        @block.tensor
        def _(pe):
            xt_hi, xt_lo = xt

            def job(i, n):
                kind, *what = jobs[n]
                bank = job_bank(i, n)
                if i * JOBS + n >= 2:
                    pe.wait_ge(job_dve, i * JOBS + n - 1)
                if kind == "qk":
                    m, g = what
                    w = WIDTH[g]
                    if g == 0:
                        pe.wait_ge(w_lo_ready, 3 * i + m + 1)
                    for k in range(DC):
                        cols = slice(g * 512, g * 512 + w)
                        ins = pair_product(pe, bank[:, 0:w], w_hi[:, m, k, :], w_lo[:, m, k, :], xt_hi[:, k, cols],
                                           xt_lo[:, k, cols], k == 0, k == DC - 1)
                elif kind == "v":
                    g = what[1]
                    if g == 0:
                        pe.wait_ge(w_lo_ready, 3 * i + 3)
                    for t in range(4 * g, min(4 * g + 4, NT)):
                        for k in range(DC):
                            nodes = slice(t * P, (t + 1) * P)
                            ins = pair_product(pe, bank[:, (t % 4) * P:(t % 4 + 1) * P], xt_hi[:, k, nodes],
                                               xt_lo[:, k, nodes], w_hi[:, 2, k, :], w_lo[:, 2, k, :], k == 0,
                                               k == DC - 1)
                elif kind == "max":
                    hd, t, g = what
                    at, w = BLOCKS[g]
                    if n == QKV_JOBS:
                        pe.wait_ge(job_dve, i * JOBS + QKV_JOBS)
                    ins = pe.matmul(bank[0:rows(t), 0:w], q1[:, i % 2, hd, t * P:t * P + rows(t)],
                                    k1[:, i % 2, hd, at:at + w], start=True, stop=True)
                else:
                    hd, g = what
                    pe.wait_ge(maxima_ready, 2 * i + 2)
                    for t in range(4 * g, min(4 * g + 4, NT)):
                        ins = pe.matmul(bank[0:1, (t % 4) * P:(t % 4 + 1) * P],
                                        minus_max[:, hd * NT + t:hd * NT + t + 1], s.ident[:, :], start=True, stop=True)
                ins.then_inc(job_product, 1)

            def scores(n):
                i, b, k, at, w, r = slot(n)
                if n % SLOTS == 0:
                    pe.wait_ge(job_dve, (i + 1) * JOBS)
                if n >= 2:
                    pe.wait_ge(exp_ready, n - 1)
                for hd in range(2):
                    out = s.ps[2 * (n % 2) + hd][0:r, 0:w]
                    keys = slice(k * P, k * P + r)
                    pe.matmul(out, k1[:, i % 2, hd, keys], q1[:, i % 2, hd, at:at + w], start=True, stop=False)
                    ins = pe.matmul(out, k2[:, i % 2, hd, keys], q2[:, i % 2, hd, at:at + w], start=False, stop=True)
                ins.then_inc(scores_ready, 1)

            def values(n):
                i, b, k, at, w, r = slot(n)
                pe.wait_ge(lo_ready, n + 1)
                if k == 0 and n >= NT:
                    pe.wait_ge(value_ready, n // NT)
                for v, p, first, last in ((v_hi, p_hi, True, False), (v_hi, p_lo, False, False), (v_lo, p_hi, False, True)):
                    for hd in range(2):
                        dims = slice(hd * HD, (hd + 1) * HD)
                        pe.matmul(ACC[dims, 0:w], v[0:r, i % 2, k, dims], p[0:r, n % 3, hd, 0:w],
                                  start=(first and k == 0), stop=(last and k == NT - 1))
                for p, first in ((p_hi, True), (p_lo, False)):
                    for hd in range(2):
                        dims = slice(hd * HD, (hd + 1) * HD)
                        ins = pe.matmul(DEN[dims, 0:w], s.ones16[0:r, 0:HD], p[0:r, n % 3, hd, 0:w],
                                        start=(first and k == 0), stop=(not first and k == NT - 1))
                ins.then_inc(pv_done, 1)

            pe.wait_ge(constants_ready, 1)
            for n in range(JOBS):
                job(0, n)
            scores(0)
            for n in range(PAIRS * SLOTS):
                i = n // SLOTS
                if n + 1 < PAIRS * SLOTS:
                    scores(n + 1)
                if i + 1 < PAIRS:
                    for j in plan[n % SLOTS]:
                        job(i + 1, j)
                if n >= 1:
                    values(n - 1)
            values(PAIRS * SLOTS - 1)


def project_out(nc, s, xt, w_proj, x2):
    with ExitStack() as scope:
        w32 = sbuf(nc, scope, "o_w32", [P, DC, D], F32)
        w_hi = sbuf(nc, scope, "o_w_hi", [P, DC, D], F16)
        w_lo = sbuf(nc, scope, "o_w_lo", [P, DC, D], F16)
        w_loaded = semaphore(nc, scope, "o_w_loaded")
        w_hi_ready = semaphore(nc, scope, "o_w_hi_ready")
        w_lo_ready = semaphore(nc, scope, "o_w_lo_ready")
        summed = semaphore(nc, scope, "o_summed")
        added = semaphore(nc, scope, "o_added")
        block = scope.enter_context(nc.Block())

        @block.sync
        def _(sp):
            sp.dma_start(w32[:, :, :], w_proj.rearrange("(k p) n -> p k n", p=P)).then_inc(w_loaded, 16)

        @block.scalar
        def _(act):
            act.wait_ge(w_loaded, 16)
            for k in range(DC):
                act.activation(w_hi[:, k, :], w32[:, k, :], ACT.Copy, scale=WSCALE).then_inc(w_hi_ready, 1)

        @block.vector
        def _(dve):
            for k in range(DC):
                dve.wait_ge(w_hi_ready, k + 1)
                dve.scalar_tensor_tensor(out=w_lo[:, k, :], in0=w32[:, k, :], scalar=WSCALE, in1=w_hi[:, k, :],
                                         op0=ALU.mult, op1=ALU.subtract).then_inc(w_lo_ready, 1)
            for n in range(2 * NT):
                t, half = divmod(n, 2)
                place = x2[0:rows(t), t, half * DHALF:(half + 1) * DHALF]
                dve.wait_ge(summed, n + 1)
                dve.scalar_tensor_tensor(out=place, in0=s.ps[n % 4][0:rows(t), 0:DHALF], scalar=1 / WSCALE, in1=place,
                                         op0=ALU.mult, op1=ALU.add).then_inc(added, 1)

        @block.tensor
        def _(pe):
            for n in range(2 * NT):
                t, half = divmod(n, 2)
                nodes = slice(t * P, t * P + rows(t))
                cols = slice(half * DHALF, (half + 1) * DHALF)
                if n >= 4:
                    pe.wait_ge(added, n - 3)
                for k in range(DC):
                    if n == 0:
                        pe.wait_ge(w_lo_ready, k + 1)
                    ins = pair_product(pe, s.ps[n % 4][0:rows(t), 0:DHALF], xt[0][:, k, nodes], xt[1][:, k, nodes],
                                       w_hi[:, k, cols], w_lo[:, k, cols], k == 0, k == DC - 1)
                ins.then_inc(summed, 1)


def route(nc, s, xt, w_router, gates, residual, x1_dram):
    with ExitStack() as scope:
        sb = lambda name, shape, dtype: sbuf(nc, scope, f"r_{name}", shape, dtype)
        sem = lambda name: semaphore(nc, scope, f"r_{name}")
        w32 = sb("w32", [P, DC, EXPERTS], F32)
        w_hi = sb("w_hi", [P, DC, EXPERTS], F16)
        w_lo = sb("w_lo", [P, DC, EXPERTS], F16)
        logits = sb("logits", [P, NT, EXPERTS], F32)
        above = sb("above", [P, NT, EXPERTS, EXPERTS], F32)
        equal = sb("equal", [P, NT, EXPERTS, EXPERTS], F32)
        lower = sb("lower", [P, EXPERTS, EXPERTS], F32)
        rank = sb("rank", [P, NT, EXPERTS], F32)
        largest = sb("largest", [P, NT], F32)
        total = sb("total", [P, NT], F32)
        x1 = sb("x1", [P, NT, D], F32)
        loaded = sem("loaded")
        x1_loaded = sem("x1_loaded")
        lower_ready = sem("lower_ready")
        split = sem("split")
        summed = sem("summed")
        dve_step = sem("dve_step")
        shifted = sem("shifted")
        exp_ready = sem("exp_ready")
        block = scope.enter_context(nc.Block())

        @block.sync
        def _(sp):
            with nc.allow_non_contiguous_dma(reason="eight columns"):
                sp.dma_start(w32[:, :, :], w_router.rearrange("(k p) n -> p k n", p=P)).then_inc(loaded, 16)
            load_nodes(sp, x1, x1_dram, x1_loaded)

        @block.gpsimd
        def _(pool):
            pool.memset(lower[:, :, :], 1.0).then_inc(lower_ready, 1)
            pool.wait_ge(lower_ready, 1)
            pool.affine_select(out=lower[:, :, :], in_=lower[:, :, :], compare_op=ALU.is_gt, fill=0.0, base=0,
                               pattern=[[1, EXPERTS], [-1, EXPERTS]], channel_multiplier=0).then_inc(lower_ready, 1)

        @block.vector
        def _(dve):
            steps = [0]

            def link(ins):
                steps[0] += 1
                ins.then_inc(dve_step, 1)
                dve.wait_ge(dve_step, steps[0])

            four = [P, NT, EXPERTS, EXPERTS]
            dve.wait_ge(loaded, 16)
            link(dve.tensor_scalar(w_hi[:, :, :], w32[:, :, :], WSCALE, None, ALU.mult))
            dve.scalar_tensor_tensor(out=w_lo[:, :, :], in0=w32[:, :, :], scalar=WSCALE, in1=w_hi[:, :, :],
                                     op0=ALU.mult, op1=ALU.subtract).then_inc(split, 1)
            dve.wait_ge(summed, 1)
            link(dve.tensor_scalar(logits[:, :, :].rearrange("p t e -> p (t e)"), s.ps[0][:, 0:NT * EXPERTS],
                                   1 / WSCALE, None, ALU.mult))
            mine = logits[:, :, :].unsqueeze(3).to_broadcast(four)
            other = logits[:, :, :].unsqueeze(2).to_broadcast(four)
            dve.tensor_tensor(above[:, :, :, :], other, mine, ALU.is_gt)
            link(dve.tensor_tensor(equal[:, :, :, :], other, mine, ALU.is_equal))
            dve.wait_ge(lower_ready, 2)
            link(dve.tensor_tensor(equal[:, :, :, :], equal[:, :, :, :],
                                   lower[:, :, :].unsqueeze(1).to_broadcast(four), ALU.mult))
            link(dve.tensor_tensor(above[:, :, :, :], above[:, :, :, :], equal[:, :, :, :], ALU.add))
            dve.tensor_reduce(rank[:, :, :], above[:, :, :, :], AX.X, ALU.add)
            link(dve.tensor_reduce(largest[:, :], logits[:, :, :], AX.X, ALU.max))
            dve.tensor_tensor(logits[:, :, :], logits[:, :, :],
                              largest[:, :].unsqueeze(2).to_broadcast([P, NT, EXPERTS]), ALU.subtract
                              ).then_inc(shifted, 1)
            dve.wait_ge(exp_ready, 1)
            link(dve.scalar_tensor_tensor(out=gates[:, :, :], in0=rank[:, :, :], scalar=2.0, in1=gates[:, :, :],
                                          op0=ALU.is_lt, op1=ALU.mult))
            link(dve.tensor_reduce(total[:, :], gates[:, :, :], AX.X, ALU.add))
            link(dve.reciprocal(total[:, :], total[:, :]))
            dve.scalar_tensor_tensor(out=gates[:, :, :], in0=gates[:, :, :], scalar=1 / WSCALE,
                                     in1=total[:, :].unsqueeze(2).to_broadcast([P, NT, EXPERTS]), op0=ALU.mult,
                                     op1=ALU.mult)
            dve.wait_ge(x1_loaded, 32)
            for t in range(NT):
                dve.tensor_tensor(residual[0:rows(t), t, :], residual[0:rows(t), t, :], x1[0:rows(t), t, :], ALU.add)

        @block.scalar
        def _(act):
            act.wait_ge(shifted, 1)
            act.activation(gates[:, :, :], logits[:, :, :], ACT.Exp).then_inc(exp_ready, 1)

        @block.tensor
        def _(pe):
            pe.wait_ge(split, 1)
            for t in range(NT):
                nodes = slice(t * P, (t + 1) * P)
                for k in range(DC):
                    ins = pair_product(pe, s.ps[0][:, t * EXPERTS:(t + 1) * EXPERTS], xt[0][:, k, nodes],
                                       xt[1][:, k, nodes], w_hi[:, k, :], w_lo[:, k, :], k == 0, k == DC - 1)
            ins.then_inc(summed, 1)


def experts(nc, s, xt, w1, w2, gates, result, out):
    with ExitStack() as scope:
        sb = lambda name, shape, dtype: sbuf(nc, scope, f"x_{name}", shape, dtype)
        sem = lambda name: semaphore(nc, scope, f"x_{name}")
        a32 = sb("a32", [P, DC, FF], F32)
        b32 = sb("b32", [P, FC, D], F32)
        a_hi, a_lo = sb("a_hi", [P, 2, DC, FF], F16), sb("a_lo", [P, 2, DC, FF], F16)
        b_hi, b_lo = sb("b_hi", [P, 2, FC, D], F16), sb("b_lo", [P, 2, FC, D], F16)
        hidden = sb("hidden", [P, 3, 512], F32)
        h_hi, h_lo = sb("h_hi", [P, 2, FC, NPAD], F16), sb("h_lo", [P, 2, FC, NPAD], F16)
        a_loaded, b_loaded = sem("a_loaded"), sem("b_loaded")
        a_hi_ready, a_lo_ready = sem("a_hi_ready"), sem("a_lo_ready")
        b_hi_ready, b_lo_ready = sem("b_hi_ready"), sem("b_lo_ready")
        up_summed = sem("up_summed")
        gelu_ready = sem("gelu_ready")
        h_hi_ready = sem("h_hi_ready")
        h_lo_ready = sem("h_lo_ready")
        down_summed = sem("down_summed")
        added = sem("added")
        stored = sem("stored")
        UP = FC * len(BLOCKS)
        DOWN = 2 * NT
        ups = [(f, g) for g in range(len(BLOCKS)) for f in range(FC)]
        block = scope.enter_context(nc.Block())

        @block.sync
        def _(sp):
            for e in range(EXPERTS):
                if e >= 1:
                    sp.wait_ge(a_lo_ready, e)
                sp.dma_start(a32[:, :, :], w1[e].rearrange("(k p) n -> p k n", p=P)).then_inc(a_loaded, 16)
                if e >= 1:
                    sp.wait_ge(b_lo_ready, e)
                sp.dma_start(b32[:, :, :], w2[e].rearrange("(k p) n -> p k n", p=P)).then_inc(b_loaded, 16)
            for t in range(NT):
                sp.wait_ge(added, (EXPERTS - 1) * DOWN + 2 * (t + 1))
                sp.dma_start(out[t * P:t * P + rows(t), :], result[0:rows(t), t, :]).then_inc(stored, 16)
            sp.wait_ge(stored, 16 * NT)

        @block.scalar
        def _(act):
            def split(e):
                act.wait_ge(a_loaded, 16 * (e + 1))
                if e >= 2:
                    act.wait_ge(up_summed, UP * (e - 1))
                act.activation(a_hi[:, e % 2, :, :], a32[:, :, :], ACT.Copy, scale=WSCALE).then_inc(a_hi_ready, 1)
                act.wait_ge(b_loaded, 16 * (e + 1))
                if e >= 2:
                    act.wait_ge(down_summed, DOWN * (e - 1))
                act.activation(b_hi[:, e % 2, :, :], b32[:, :, :], ACT.Copy, scale=WSCALE).then_inc(b_hi_ready, 1)

            split(0)
            for e in range(EXPERTS):
                for c, (f, g) in enumerate(ups):
                    n = e * UP + c
                    at, w = BLOCKS[g]
                    act.wait_ge(up_summed, n + 1)
                    if n >= 3:
                        act.wait_ge(h_lo_ready, n - 2)
                    act.activation(hidden[:, n % 3, 0:w], s.ps[n % 4][:, 0:w], ACT.Gelu, scale=1 / WSCALE
                                   ).then_inc(gelu_ready, 1)
                    act.wait_ge(gelu_ready, n + 1)
                    if e >= 2:
                        act.wait_ge(down_summed, DOWN * (e - 1))
                    act.activation(h_hi[:, e % 2, f, at:at + w], hidden[:, n % 3, 0:w], ACT.Copy).then_inc(h_hi_ready, 1)
                if e + 1 < EXPERTS:
                    split(e + 1)

        @block.vector
        def _(dve):
            def split(e):
                dve.wait_ge(a_hi_ready, e + 1)
                dve.scalar_tensor_tensor(out=a_lo[:, e % 2, :, :], in0=a32[:, :, :], scalar=WSCALE,
                                         in1=a_hi[:, e % 2, :, :], op0=ALU.mult, op1=ALU.subtract).then_inc(a_lo_ready, 1)
                dve.wait_ge(b_hi_ready, e + 1)
                dve.scalar_tensor_tensor(out=b_lo[:, e % 2, :, :], in0=b32[:, :, :], scalar=WSCALE,
                                         in1=b_hi[:, e % 2, :, :], op0=ALU.mult, op1=ALU.subtract).then_inc(b_lo_ready, 1)

            def up(e):
                for c, (f, g) in enumerate(ups):
                    n = e * UP + c
                    at, w = BLOCKS[g]
                    dve.wait_ge(h_hi_ready, n + 1)
                    dve.tensor_tensor(h_lo[:, e % 2, f, at:at + w], hidden[:, n % 3, 0:w],
                                      h_hi[:, e % 2, f, at:at + w], ALU.subtract).then_inc(h_lo_ready, 1)

            split(0)
            up(0)
            for e in range(EXPERTS):
                if e + 1 < EXPERTS:
                    split(e + 1)
                for c in range(DOWN):
                    t, half = divmod(c, 2)
                    n = e * DOWN + c
                    r = rows(t)
                    place = result[0:r, t, half * DHALF:(half + 1) * DHALF]
                    dve.wait_ge(down_summed, n + 1)
                    if e >= 1:
                        dve.wait_ge(added, n - DOWN + 1)
                    dve.scalar_tensor_tensor(out=place, in0=s.ps[4 + n % 4][0:r, 0:DHALF],
                                             scalar=gates[0:r, t, e:e + 1], in1=place, op0=ALU.mult, op1=ALU.add
                                             ).then_inc(added, 1)
                if e + 1 < EXPERTS:
                    up(e + 1)

        @block.tensor
        def _(pe):
            for e in range(EXPERTS):
                pe.wait_ge(a_lo_ready, e + 1)
                for c, (f, g) in enumerate(ups):
                    n = e * UP + c
                    at, w = BLOCKS[g]
                    if n >= 4:
                        pe.wait_ge(gelu_ready, n - 3)
                    for k in range(DC):
                        cols = slice(f * P, (f + 1) * P)
                        ins = pair_product(pe, s.ps[n % 4][:, 0:w], a_hi[:, e % 2, k, cols], a_lo[:, e % 2, k, cols],
                                           xt[0][:, k, at:at + w], xt[1][:, k, at:at + w], k == 0, k == DC - 1)
                    ins.then_inc(up_summed, 1)
                pe.wait_ge(b_lo_ready, e + 1)
                for c in range(DOWN):
                    t, half = divmod(c, 2)
                    n = e * DOWN + c
                    r = rows(t)
                    pe.wait_ge(h_lo_ready, e * UP + FC * (t // 4 + 1))
                    if n >= 4:
                        pe.wait_ge(added, n - 3)
                    for f in range(FC):
                        cols = slice(half * DHALF, (half + 1) * DHALF)
                        ins = pair_product(pe, s.ps[4 + n % 4][0:r, 0:DHALF], h_hi[:, e % 2, f, t * P:t * P + r],
                                           h_lo[:, e % 2, f, t * P:t * P + r], b_hi[:, e % 2, f, cols],
                                           b_lo[:, e % 2, f, cols], f == 0, f == FC - 1)
                    ins.then_inc(down_summed, 1)


def ffn(nc, s, a, out):
    x1_dram = nc.dram_tensor("x1_kept", (N, D), F32, kind="Internal").ap()
    with ExitStack() as scope:
        xt = [sbuf(nc, scope, f"fxt_{i}", [P, DC, NPAD], F16) for i in ("hi", "lo")]
        norm_transpose(nc, s, "n1", s.x1, s.x1, xt, twice=True, gain=a["L0_ffn_ln1_g"], bias=a["L0_ffn_ln1_b"],
                       keep=x1_dram)
        with ExitStack() as inner:
            heads_t = [sbuf(nc, inner, f"heads_{i}", [P, DC, NPAD], F16) for i in ("hi", "lo")]
            attend(nc, s, xt, a["L0_ffn_Wqkv"], *heads_t)
            project_out(nc, s, heads_t, a["L0_ffn_Wproj"], s.x1)
        with ExitStack() as inner:
            normed = sbuf(nc, inner, "normed", [P, NT, D], F32)
            norm_transpose(nc, s, "n2", s.x1, normed, xt, gain=a["L0_ffn_ln2_g"], bias=a["L0_ffn_ln2_b"])
        gates = sbuf(nc, scope, "gates", [P, NT, EXPERTS], F32)
        route(nc, s, xt, a["L0_ffn_Wrouter"], gates, s.x1, x1_dram)
        experts(nc, s, xt, a["L0_ffn_W1"], a["L0_ffn_W2"], gates, s.x1, out)


def setup(nc, s, scope):
    s.ps = [scope.enter_context(nc.psum_tensor(f"bank{i}", [P, 512], F32)) for i in range(8)]
    s.ident = sbuf(nc, scope, "ident", [P, P], F32)
    s.ident_bf = sbuf(nc, scope, "ident_bf", [P, P], BF16)
    s.ones = sbuf(nc, scope, "ones", [P, P], F32)
    s.ones16 = sbuf(nc, scope, "ones16", [P, P], F16)
    s.sel = sbuf(nc, scope, "sel", [8, 8, P], F32)
    s.x1 = sbuf(nc, scope, "x1", [P, NT, D], F32)
    constants(nc, s)


def gnn(nc, s, a):
    hidden_hi = nc.dram_tensor("hidden_hi", (HC, P, N), F16, kind="Internal").ap()
    hidden_lo = nc.dram_tensor("hidden_lo", (HC, P, N), F16, kind="Internal").ap()
    with ExitStack() as scope:
        s.CT = sbuf(nc, scope, "CT", [P, NT, CT_COLS], U16)
        attention = sbuf(nc, scope, "attention", [P, NT, 8], F32)
        source02 = sbuf(nc, scope, "source02", [P, NT, HEADS], F32)
        offsets = sbuf(nc, scope, "offsets", [8, NPAD], F32)
        count_edges(nc, s)
        with ExitStack() as layer:
            h_hi = sbuf(nc, layer, "h_hi", [P, NT, HEADS * HID], F16)
            h_lo = sbuf(nc, layer, "h_lo", [P, NT, HEADS * HID], F16)
            with ExitStack() as inner:
                xt = [sbuf(nc, inner, f"xt_{i}", [P, DC, NPAD], F16) for i in ("hi", "lo")]
                norm_transpose(nc, s, "n0", s.x1, s.x1, xt, load=a["x"])
                project_nodes(nc, s, "p1", xt, a["L0_gnn_W1"], a["L0_gnn_att_src1"], a["L0_gnn_att_dst1"], HEADS,
                              h_hi, h_lo, attention)
            edge_maxima(nc, s, "m1", HEADS, attention, source02, offsets)
            aggregate_heads(nc, s, attention, source02, offsets, h_hi, h_lo, a["L0_gnn_b1"], hidden_hi, hidden_lo)
        h_hi = sbuf(nc, scope, "h2_hi", [P, NT, D + 2], F16)
        h_lo = sbuf(nc, scope, "h2_lo", [P, NT, D + 2], F16)
        project_hidden(nc, s, a["L0_gnn_W2"], a["L0_gnn_att_src2"], a["L0_gnn_att_dst2"], hidden_hi, hidden_lo,
                       h_hi, h_lo, attention)
        offsets_b = sbuf(nc, scope, "offsets_b", [P, 2, NPAD], F32)
        edge_maxima(nc, s, "m2", 1, attention, source02, offsets, offsets_b)
        aggregate_nodes(nc, s, attention, source02, offsets_b, h_hi, h_lo, a["x"], a["L0_gnn_b2"], s.x1)


def program(nc, a, out):
    with ExitStack() as scope:
        s = State()
        State.used.clear()
        setup(nc, s, scope)
        s.src, s.dst = a["src"], a["dst"]
        gnn(nc, s, a)
        clear_semaphores(nc)
        ffn(nc, s, a, out)


_INS = ["x", "src", "dst"] + ["L0_gnn_" + n for n in ("W1", "att_src1", "att_dst1", "b1", "W2", "att_src2",
        "att_dst2", "b2")] + ["L0_ffn_" + n for n in ("Wqkv", "Wproj", "Wrouter", "W1", "W2", "ln1_g", "ln1_b",
        "ln2_g", "ln2_b")]


def kernel(**inputs):
    import concourse.bacc as _bacc
    from concourse.bass_utils import run_bass_kernel_spmd as _run

    nc = _bacc.Bacc("TRN2", target_bir_lowering=False, num_devices=1)
    arrays, args = {}, {}
    for name in _INS:
        arrays[f"in_{name}"] = np.ascontiguousarray(inputs[name])
        args[name] = nc.dram_tensor(f"in_{name}", arrays[f"in_{name}"].shape, DT.from_np(arrays[f"in_{name}"].dtype),
                                    kind="ExternalInput").ap()
    out = nc.dram_tensor("out_0", (N, D), F32, kind="ExternalOutput").ap()
    program(nc, args, out)
    r = _run(nc, [arrays], core_ids=[0])
    return r.results[0]["out_0"]
```

```python
from contextlib import ExitStack

import numpy as np
import concourse.bass as bass
from concourse import mybir

DT = mybir.dt
F32, F16, BF16, I32, U16 = DT.float32, DT.float16, DT.bfloat16, DT.int32, DT.uint16
ALU = mybir.AluOpType
ACT = mybir.ActivationFunctionType
AX = mybir.AxisListType

P = 128
N = 1250
NT = -(-N // P)
NPAD = NT * P
LAST = N - (NT - 1) * P
D = 768
DC = D // P
HID, HEADS = 512, 4
HC = HID * HEADS // P
EDGES = 40000
FF, EXPERTS = 384, 8
FC = FF // P
ATT_HEADS, HD = 12, 64
PAIRS = ATT_HEADS // 2
EPS = 1e-5
SLOPE = 0.2
WSCALE = 64.0
NO_EDGE = -1e30
BLOCKS = [(0, 512), (512, 512), (1024, N - 1024)]
DHALF = D // 2


def rows(t):
    return P if t < NT - 1 else LAST


class State:
    used = []


def sbuf(nc, scope, name, shape, dtype):
    return scope.enter_context(nc.sbuf_tensor(name, shape, dtype))


def semaphore(nc, scope, name):
    sem = scope.enter_context(nc.semaphore(name))
    State.used.append(sem)
    return sem


def pair_product(pe, out, lhs_hi, lhs_lo, rhs_hi, rhs_lo, first, last):
    pe.matmul(out, lhs_hi, rhs_hi, start=first, stop=False)
    pe.matmul(out, lhs_hi, rhs_lo, start=False, stop=False)
    return pe.matmul(out, lhs_lo, rhs_hi, start=False, stop=last)


def load_nodes(eng, tile, dram, sem):
    full = (NT - 1) * P
    eng.dma_start(tile[:, 0:NT - 1, :], dram[0:full, :].rearrange("(t p) d -> p t d", p=P)).then_inc(sem, 16)
    eng.dma_start(tile[0:LAST, NT - 1, :], dram[full:N, :]).then_inc(sem, 16)


def clear_semaphores(nc):
    with nc.Block() as block:

        @block.gpsimd
        def _(pool):
            for sem in State.used:
                pool.sem_clear(sem)
    State.used.clear()


def constants(nc, s):
    with ExitStack() as scope:
        zeroed = semaphore(nc, scope, "c_zeroed")
        ident_done = semaphore(nc, scope, "c_ident_done")
        block = scope.enter_context(nc.Block())

        @block.gpsimd
        def _(pool):
            pool.memset(s.ident[:, :], 0.0).then_inc(zeroed, 1)
            pool.wait_ge(zeroed, 1)
            pool.affine_select(out=s.ident[:, :], in_=s.ident[:, :], compare_op=ALU.not_equal, fill=1.0,
                               base=0, pattern=[[-1, P]], channel_multiplier=1).then_inc(ident_done, 1)

        @block.vector
        def _(dve):
            dve.memset(s.ones[:, :], 1.0)
            dve.memset(s.ones16[:, :], 1.0)
            dve.wait_ge(ident_done, 1)
            dve.tensor_copy(s.ident_bf[:, :], s.ident[:, :])
            dve.tensor_copy(s.ident16[:, :], s.ident[:, :])
            dve.tensor_copy(s.sel[:, :, :], s.ident[0:8, 0:8].unsqueeze(2).to_broadcast([8, 8, P]))


def norm_transpose(nc, s, tag, x, out_norm, xt, twice=False, gain=None, bias=None, loaded=None,
                   keep=None, ahead=None):
    xt_hi, xt_lo = xt
    with ExitStack() as scope:
        sb = lambda name, shape, dtype: sbuf(nc, scope, f"{tag}_{name}", shape, dtype)
        sem = lambda name: semaphore(nc, scope, f"{tag}_{name}")
        stats = sb("stats", [P, NT, 2, 6], F32)
        moments = sb("moments", [P, NT, 2], F32)
        variance = sb("variance", [P, NT], F32)
        deviation = sb("deviation", [P, NT], F32)
        inverse = sb("inverse", [P, NT], F32)
        scratch = sb("scratch", [P, NT, D], F32) if twice else None
        affine = gain is not None
        if affine:
            gb = sb("gain_bias", [P, 2, DC], F32)
            shifted = sb("shifted", [P, 4, 512], F32)
        kept = sem("kept")
        gb_loaded = sem("gb_loaded")
        dve_step = sem("dve_step")
        variance_ready = sem("variance_ready")
        deviation_ready = sem("deviation_ready")
        normed = sem("normed")
        turned = sem("turned")
        shifted_ready = sem("shifted_ready")
        hi_ready = sem("hi_ready")
        lo_ready = sem("lo_ready")
        groups = [(c, g) for c in range(DC) for g in range(3)]
        width = [512, 512, NPAD - 1024]
        final = scratch if twice else out_norm
        passes = 2 if twice else 1
        block = scope.enter_context(nc.Block())

        @block.sync
        def _(sp):
            if ahead is not None:
                ahead(sp)
            if keep is not None:
                full = (NT - 1) * P
                sp.dma_start(keep[0:full, :].rearrange("(t p) d -> p t d", p=P), x[:, 0:NT - 1, :]).then_inc(kept, 16)
                sp.dma_start(keep[full:N, :], x[0:LAST, NT - 1, :]).then_inc(kept, 16)
                sp.wait_ge(kept, 32)
            if affine:
                with nc.allow_non_contiguous_dma(reason="one short vector per partition"):
                    sp.dma_start(gb[:, 0, :], gain.rearrange("(c p) -> p c", p=P)).then_inc(gb_loaded, 16)
                    sp.dma_start(gb[:, 1, :], bias.rearrange("(c p) -> p c", p=P)).then_inc(gb_loaded, 16)

        @block.vector
        def _(dve):
            steps = [0]

            def link(ins):
                steps[0] += 1
                ins.then_inc(dve_step, 1)
                dve.wait_ge(dve_step, steps[0])

            if loaded is not None:
                dve.wait_ge(loaded, 32)
            for n in range(passes):
                src = x if n == 0 else out_norm
                dst = out_norm if n == 0 else scratch
                for t in range(NT):
                    for half in range(2):
                        ins = dve.bn_stats(stats[:, t, half, :], src[:, t, half * DHALF:(half + 1) * DHALF])
                link(ins)
                for t in range(NT):
                    ins = dve.bn_aggr(moments[:, t, :], stats[:, t, :, :].rearrange("p a b -> p (a b)"))
                link(ins)
                dve.tensor_scalar(variance[:, :], moments[:, :, 1], EPS, None, ALU.add).then_inc(variance_ready, 1)
                dve.wait_ge(deviation_ready, n + 1)
                link(dve.reciprocal(inverse[:, :], deviation[:, :]))
                if keep is not None and n == 0:
                    dve.wait_ge(kept, 32)
                for t in range(NT):
                    ins = dve.tensor_scalar(dst[:, t, :], src[:, t, :], moments[:, t, 0:1], inverse[:, t:t + 1],
                                            ALU.subtract, ALU.mult)
                    if n == passes - 1:
                        ins.then_inc(normed, 1)
                if n < passes - 1:
                    link(ins)
            if affine:
                dve.wait_ge(gb_loaded, 32)
            for n in range(len(groups) + 1):
                if affine and n < len(groups):
                    c, g = groups[n]
                    w = width[g]
                    dve.wait_ge(turned, n + 1)
                    dve.tensor_scalar(shifted[:, n % 4, 0:w], s.ps[n % 4][:, 0:w], gb[:, 0, c:c + 1],
                                      gb[:, 1, c:c + 1], ALU.mult, ALU.add).then_inc(shifted_ready, 1)
                m = n - 1
                if m >= 0:
                    c, g = groups[m]
                    w = width[g]
                    cols = slice(g * 512, g * 512 + w)
                    whole = shifted[:, m % 4, 0:w] if affine else s.ps[m % 4][:, 0:w]
                    dve.wait_ge(hi_ready, m + 1)
                    dve.tensor_tensor(xt_lo[:, c, cols], whole, xt_hi[:, c, cols], ALU.subtract).then_inc(lo_ready, 1)

        @block.scalar
        def _(act):
            for n in range(passes):
                act.wait_ge(variance_ready, n + 1)
                act.activation(deviation[:, :], variance[:, :], ACT.Sqrt).then_inc(deviation_ready, 1)
            for n, (c, g) in enumerate(groups):
                w = width[g]
                cols = slice(g * 512, g * 512 + w)
                if affine:
                    act.wait_ge(shifted_ready, n + 1)
                    whole = shifted[:, n % 4, 0:w]
                else:
                    act.wait_ge(turned, n + 1)
                    whole = s.ps[n % 4][:, 0:w]
                act.activation(xt_hi[:, c, cols], whole, ACT.Copy).then_inc(hi_ready, 1)

        @block.tensor
        def _(pe):
            for n, (c, g) in enumerate(groups):
                pe.wait_ge(normed, min(4 * g + 4, NT))
                if n >= 4:
                    pe.wait_ge(lo_ready, n - 3)
                for t in range(4 * g, min(4 * g + 4, NT)):
                    ins = pe.transpose(s.ps[n % 4][:, (t % 4) * P:(t % 4 + 1) * P],
                                       final[:, t, c * P:(c + 1) * P], s.ident[:, :])
                ins.then_inc(turned, 1)


TILE_E = 125
GROUP = 10
TILES_E = EDGES // TILE_E
GROUPS_E = TILES_E // GROUP
WIN = 64
KEYS = NT * WIN
CT_COLS = NPAD + WIN


def count_edges(nc, s, x, x_loaded):
    POOL_TILES = (1, 3, 4, 6, 8, 9)
    chunks = [(0, P), (P, P), (2 * P, TILES_E - 2 * P)]
    with ExitStack() as scope:
        sb = lambda name, shape, dtype: sbuf(nc, scope, f"e_{name}", shape, dtype)
        sem = lambda name: semaphore(nc, scope, f"e_{name}")
        src_i = sb("src_i", [P, 3, TILE_E], I32)
        dst_i = sb("dst_i", [P, 3, TILE_E], I32)
        part_i = sb("part_i", [P, 2, 3, TILE_E], I32)
        part_f = sb("part_f", [P, 3, 3, TILE_E], F32)
        extent = sb("extent", [P, 6], F32)
        least = sb("least", [1, GROUPS_E], F32)
        greatest = sb("greatest", [1, GROUPS_E], F32)
        span = sb("span", [1, GROUPS_E + 1], F32)
        window_i = sb("window_i", [1, GROUPS_E + 1, 2], I32)
        span_i = sb("span_i", [1, GROUPS_E + 1], I32)
        base = sb("base", [P, GROUPS_E], F32)
        table = sb("table", [P, GROUPS_E, 4, GROUP], F32)
        inside = sb("inside", [P, GROUPS_E, GROUP], F32)
        mine = sb("mine", [P, 4, GROUP], F32)
        test = sb("test", [P, GROUP], F32)
        iota_i = sb("iota_i", [P, KEYS], I32)
        iota = sb("iota", [P, KEYS], F16)
        one_key = sb("one_key", [P, GROUP, KEYS], F16)
        one_src = sb("one_src", [P, GROUP, P], F16)
        loaded = sem("loaded")
        iota_ready = sem("iota_ready")
        pads_zeroed = sem("pads_zeroed")
        dve_step = sem("dve_step")
        parts_ready = sem("parts_ready")
        parts_turned = sem("parts_turned")
        extent_ready = sem("extent_ready")
        extent_turned = sem("extent_turned")
        least_ready = sem("least_ready")
        base_turned = sem("base_turned")
        windows_ready = sem("windows_ready")
        group_step = sem("group_step")
        keys_made = sem("keys_made")
        key_onehots = sem("key_onehots")
        src_onehots = sem("src_onehots")
        first_used = sem("first_used")
        first_summed = sem("first_summed")
        first_added = sem("first_added")
        visit_step = sem("visit_step")
        onehots_ready = sem("onehots_ready")
        slots_used = sem("slots_used")
        piece_added = sem("piece_added")
        block = scope.enter_context(nc.Block())

        def first_banks(g):
            return (s.ps[6], s.ps[7]) if g % 2 == 0 else (s.ps[1], s.ps[5])

        @block.sync
        def _(sp):
            for dst_tile, dram in ((src_i, s.src), (dst_i, s.dst)):
                sp.dma_start(dst_tile[:, 0:2, :], dram[0:2 * P * TILE_E].rearrange("(a p e) -> p a e", a=2, e=TILE_E)
                             ).then_inc(loaded, 16)
                sp.dma_start(dst_tile[0:chunks[2][1], 2, :], dram[2 * P * TILE_E:EDGES].rearrange("(p e) -> p e", e=TILE_E)
                             ).then_inc(loaded, 16)
            sp.wait_ge(pads_zeroed, 1)
            load_nodes(sp, s.x1, x, x_loaded)

        @block.gpsimd
        def _(pool):
            pool.iota(iota_i[:, :], pattern=[[1, KEYS]], base=0, channel_multiplier=0).then_inc(iota_ready, 1)
            pool.wait_ge(keys_made, 1)
            for n in range(TILES_E):
                g, j = divmod(n, GROUP)
                if j not in POOL_TILES:
                    continue
                if n >= GROUP:
                    pool.wait_ge(first_used, n - GROUP + 1)
                pool.tensor_scalar(one_src[0:TILE_E, j, :], iota[0:TILE_E, 0:P], table[0:TILE_E, g, 1, j:j + 1], None,
                                   ALU.is_equal).then_inc(src_onehots, 1)

        @block.vector
        def _(dve):
            steps = [0]

            def link(ins):
                steps[0] += 1
                ins.then_inc(dve_step, 1)
                dve.wait_ge(dve_step, steps[0])

            dve.memset(s.x1[96:P, NT - 1, :], 0.0).then_inc(pads_zeroed, 1)
            dve.memset(s.CT[:, :, :], 0)
            link(dve.memset(extent[:, :], 0.0))
            dve.wait_ge(iota_ready, 1)
            dve.tensor_copy(iota[:, :], iota_i[:, :])
            dve.wait_ge(loaded, 64)
            for a, (_, k) in enumerate(chunks):
                dve.tensor_scalar(part_i[0:k, 0, a, :], src_i[0:k, a, :], 7, 6, ALU.logical_shift_right,
                                  ALU.logical_shift_left)
                dve.tensor_scalar(part_i[0:k, 1, a, :], src_i[0:k, a, :], P - 1, None, ALU.bitwise_and)
                ins = dve.tensor_copy(part_f[0:k, 2, a, :], dst_i[0:k, a, :])
            link(ins)
            for a, (_, k) in enumerate(chunks):
                dve.tensor_reduce(extent[0:k, a:a + 1], part_f[0:k, 2, a, :], AX.X, ALU.min)
                ins = dve.tensor_reduce(extent[0:k, 3 + a:4 + a], part_f[0:k, 2, a, :], AX.X, ALU.max)
            ins.then_inc(extent_ready, 1)
            for a, (_, k) in enumerate(chunks):
                ins = dve.tensor_copy(part_f[0:k, 0:2, a, :], part_i[0:k, :, a, :])
            ins.then_inc(parts_ready, 1)
            dve.wait_ge(extent_turned, 1)
            dve.tensor_reduce(least[:, :], s.ps[0][0:1, 0:TILES_E].rearrange("p (g t) -> p g t", t=GROUP), AX.X,
                              ALU.min).then_inc(least_ready, 1)
            link(dve.tensor_reduce(greatest[:, :], s.ps[1][0:1, 0:TILES_E].rearrange("p (g t) -> p g t", t=GROUP),
                                   AX.X, ALU.max))
            link(dve.tensor_tensor(span[:, 0:GROUPS_E], greatest[:, :], least[:, :], ALU.subtract))
            link(dve.tensor_reduce(span[:, GROUPS_E:GROUPS_E + 1], span[:, 0:GROUPS_E], AX.X, ALU.max))
            link(dve.tensor_copy(span_i[:, :], span[:, :]))
            link(dve.tensor_scalar(span_i[:, :], span_i[:, :], 6, None, ALU.logical_shift_right))
            dve.tensor_copy(window_i[:, 0:GROUPS_E, 1], span_i[:, 0:GROUPS_E]).then_inc(windows_ready, 1)
            dve.tensor_scalar(window_i[:, GROUPS_E, 1:2], span_i[:, GROUPS_E:GROUPS_E + 1], 1, None, ALU.min
                              ).then_inc(windows_ready, 1)
            dve.tensor_copy(window_i[:, 0:GROUPS_E, 0], least[:, 0:GROUPS_E]).then_inc(windows_ready, 1)
            dve.wait_ge(base_turned, 1)
            link(dve.tensor_copy(base[:, :], s.ps[0][:, 400:400 + GROUPS_E]))
            dve.wait_ge(parts_turned, 3)
            turned = [s.ps[2 + i][0:TILE_E, 0:TILES_E].rearrange("p (g t) -> p g t", t=GROUP) for i in range(3)]
            dve.tensor_copy(table[0:TILE_E, :, 2, :], turned[0])
            dve.tensor_copy(table[0:TILE_E, :, 1, :], turned[1])
            rel = table[0:TILE_E, :, 3, :]
            key = table[0:TILE_E, :, 0, :]
            link(dve.tensor_tensor(rel, turned[2],
                                   base[0:TILE_E, :].unsqueeze(2).to_broadcast([TILE_E, GROUPS_E, GROUP]),
                                   ALU.subtract))
            link(dve.scalar_tensor_tensor(out=key, in0=table[0:TILE_E, :, 2, :], scalar=1.0, in1=rel,
                                          op0=ALU.add, op1=ALU.add))
            link(dve.scalar_tensor_tensor(out=key, in0=rel, scalar=float(WIN), in1=key, op0=ALU.is_lt, op1=ALU.mult))
            dve.tensor_scalar(key, key, 1.0, None, ALU.subtract).then_inc(keys_made, 1)
            def add_piece(g):
                column = dve.value_load(window_i[0:1, g:g + 1, 0], min_val=0, max_val=N - 1)
                dve.wait_ge(first_summed, g + 1)
                if g >= 1:
                    dve.wait_ge(first_added, 2 * g)
                for half in range(2):
                    piece = s.CT[:, half * NT // 2:(half + 1) * NT // 2, bass.ds(column, WIN)]
                    dve.tensor_tensor(piece, piece, first_banks(g)[half][:, 0:KEYS // 2]
                                      .rearrange("p (c w) -> p c w", w=WIN), ALU.add).then_inc(first_added, 1)

            dve.wait_ge(windows_ready, 3)
            dve.wait_ge(keys_made, 1)
            for g in range(GROUPS_E):
                for j in range(GROUP):
                    n = g * GROUP + j
                    if n >= GROUP:
                        dve.wait_ge(first_used, n - GROUP + 1)
                    dve.tensor_scalar(one_key[0:TILE_E, j, :], iota[0:TILE_E, :], table[0:TILE_E, g, 0, j:j + 1], None,
                                      ALU.is_equal).then_inc(key_onehots, 1)
                    if j not in POOL_TILES:
                        dve.tensor_scalar(one_src[0:TILE_E, j, :], iota[0:TILE_E, 0:P], table[0:TILE_E, g, 1, j:j + 1],
                                          None, ALU.is_equal).then_inc(key_onehots, 1)
                    if j == 3 and g >= 1:
                        add_piece(g - 1)
            add_piece(GROUPS_E - 1)
            dve.wait_ge(first_added, 2 * GROUPS_E)
            dve.wait_ge(first_used, TILES_E)
            dve.wait_ge(src_onehots, GROUPS_E * len(POOL_TILES))
            dve.memset(test[:, 0:1], 0.0).then_inc(piece_added, 1)
            dve.memset(test[:, 1:2], 0.0).then_inc(slots_used, GROUP)
            dve.memset(test[:, 2:3], 0.0).then_inc(visit_step, 1)
            dve.memset(test[:, 4:5], 0.0).then_inc(group_step, 1)
            STEPS = 7
            ones_column = s.ones[:, 0:1]
            E_ = TILE_E
            more = dve.value_load(window_i[0:1, GROUPS_E:GROUPS_E + 1, 1], min_val=0, max_val=1)
            with dve.If(more > 0):
                visit = dve.alloc_register("e_dve_visit")
                window_start = dve.alloc_register("e_window_start")
                dve.reg_mov(visit, 0)
                with dve.Fori(0, GROUPS_E) as g:
                    first = dve.value_load(window_i[0:1, bass.ds(g, 1), 0], min_val=0, max_val=N - 1)
                    windows = dve.value_load(window_i[0:1, bass.ds(g, 1), 1], min_val=0, max_val=N // WIN)
                    dve.wait_ge(visit_step, dve.snap(visit) * STEPS + 1)
                    dve.wait_ge(group_step, g + 1)
                    dve.tensor_copy(mine[0:E_, :, :], table[0:E_, bass.ds(g, 1), :, :]
                                    .rearrange("p g k t -> p (g k) t")).then_inc(group_step, 1)
                    dve.reg_mov(window_start, first)
                    with dve.If(windows > 0), dve.Fori(0, windows):
                        v = dve.snap(visit)
                        dve.reg_add(window_start, window_start, WIN)
                        dve.wait_ge(group_step, g + 2)
                        dve.wait_ge(visit_step, v * STEPS + 1)
                        rel_m, key_m, high_m = mine[0:E_, 3, :], mine[0:E_, 0, :], mine[0:E_, 2, :]
                        dve.tensor_scalar(rel_m, rel_m, float(WIN), None, ALU.subtract).then_inc(visit_step, 1)
                        dve.wait_ge(visit_step, v * STEPS + 2)
                        dve.scalar_tensor_tensor(out=key_m, in0=high_m, scalar=1.0, in1=rel_m, op0=ALU.add,
                                                 op1=ALU.add).then_inc(visit_step, 1)
                        dve.wait_ge(visit_step, v * STEPS + 3)
                        dve.scalar_tensor_tensor(out=key_m, in0=rel_m, scalar=float(WIN), in1=key_m, op0=ALU.is_lt,
                                                 op1=ALU.mult).then_inc(visit_step, 1)
                        dve.wait_ge(visit_step, v * STEPS + 4)
                        dve.scalar_tensor_tensor(out=key_m, in0=rel_m, scalar=0.0, in1=key_m, op0=ALU.is_ge,
                                                 op1=ALU.mult).then_inc(visit_step, 1)
                        dve.wait_ge(visit_step, v * STEPS + 5)
                        dve.tensor_scalar(key_m, key_m, 1.0, None, ALU.subtract).then_inc(visit_step, 1)
                        dve.wait_ge(visit_step, v * STEPS + 6)
                        for j in range(GROUP):
                            dve.wait_ge(slots_used, v * GROUP + (j + 1))
                            dve.tensor_scalar(one_key[0:E_, j, :], iota[0:E_, :], mine[0:E_, 0, j:j + 1], None,
                                              ALU.is_equal)
                            dve.tensor_scalar(one_src[0:E_, j, :], iota[0:E_, 0:P], mine[0:E_, 1, j:j + 1], None,
                                              ALU.is_equal).then_inc(onehots_ready, 1)
                        dve.wait_ge(slots_used, v * GROUP + 2 * GROUP)
                        column = dve.snap(window_start, min_val=0, max_val=N - 1)
                        for half in range(2):
                            piece = s.CT[:, half * NT // 2:(half + 1) * NT // 2, bass.ds(column, WIN)]
                            dve.tensor_tensor(piece, piece, s.ps[6 + half][:, 0:KEYS // 2]
                                              .rearrange("p (c w) -> p c w", w=WIN), ALU.add).then_inc(visit_step, 1)
                        dve.nop().then_inc(piece_added, 1)
                        dve.reg_add(visit, visit, 1)
                dve.wait_ge(visit_step, dve.snap(visit) * STEPS + 1)
                dve.tensor_scalar(test[:, 3:4], ones_column, 1.0, None, ALU.mult)
            for t in range(NT):
                loop = s.CT[:, t, t * P:t * P + rows(t)]
                ins = dve.tensor_tensor(loop, loop, s.ident[:, 0:rows(t)], ALU.add)
            link(ins)

        @block.tensor
        def _(pe):
            pe.wait_ge(extent_ready, 1)
            for a in range(6):
                ins = pe.transpose(s.ps[a // 3][0:1, (a % 3) * P:(a % 3 + 1) * P], extent[:, a:a + 1], s.ident[:, :])
            ins.then_inc(extent_turned, 1)
            pe.wait_ge(least_ready, 1)
            pe.matmul(s.ps[0][:, 400:400 + GROUPS_E], s.ones[0:1, :], least[0:1, 0:GROUPS_E], start=True,
                      stop=True).then_inc(base_turned, 1)
            pe.wait_ge(parts_ready, 1)
            for i in range(3):
                for a, (at, k) in enumerate(chunks):
                    ins = pe.transpose(s.ps[2 + i][0:TILE_E, at:at + k], part_f[0:k, i, a, :], s.ident[0:k, 0:k])
                ins.then_inc(parts_turned, 1)
            for g in range(GROUPS_E):
                if g >= 2:
                    pe.wait_ge(first_added, 2 * (g - 1))
                for j in range(GROUP):
                    mine_too = sum(i <= j for i in POOL_TILES)
                    pe.wait_ge(key_onehots, g * (2 * GROUP - len(POOL_TILES)) + 2 * (j + 1) - mine_too)
                    if j in POOL_TILES:
                        pe.wait_ge(src_onehots, g * len(POOL_TILES) + mine_too)
                    for half in range(2):
                        ins = pe.matmul(first_banks(g)[half][:, 0:KEYS // 2], one_src[0:TILE_E, j, :],
                                        one_key[0:TILE_E, j, half * KEYS // 2:(half + 1) * KEYS // 2],
                                        start=(j == 0), stop=(j == GROUP - 1))
                    ins.then_inc(first_used, 1)
                pe.wait_ge(first_used, (g + 1) * GROUP)
                pe.nop().then_inc(first_summed, 1)
            pe.wait_ge(windows_ready, 3)
            more = pe.value_load(window_i[0:1, GROUPS_E:GROUPS_E + 1, 1], min_val=0, max_val=1)
            with pe.If(more > 0):
                visit = pe.alloc_register("e_pe_visit")
                pe.reg_mov(visit, 0)
                with pe.Fori(0, GROUPS_E) as g:
                    windows = pe.value_load(window_i[0:1, bass.ds(g, 1), 1], min_val=0, max_val=N // WIN)
                    with pe.If(windows > 0), pe.Fori(0, windows):
                        v = pe.snap(visit)
                        pe.wait_ge(piece_added, v + 1)
                        for j in range(GROUP):
                            pe.wait_ge(onehots_ready, v * GROUP + (j + 1))
                            for half in range(2):
                                ins = pe.matmul(s.ps[6 + half][:, 0:KEYS // 2], one_src[0:TILE_E, j, :],
                                                one_key[0:TILE_E, j, half * KEYS // 2:(half + 1) * KEYS // 2],
                                                start=(j == 0), stop=(j == GROUP - 1))
                            ins.then_inc(slots_used, 1)
                        pe.reg_add(visit, visit, 1)


def load_head(eng, w32, weights, j, cols, sem):
    eng.dma_start(w32[:, :, :], weights[:, j * cols:(j + 1) * cols].rearrange("(k p) n -> p k n", p=P)
                  ).then_inc(sem, 16)


def project_nodes(nc, s, tag, xt, weights, w32, w_loaded, att_src, att_dst, heads, h_hi, h_lo, attention, load_xt=None):
    cols = weights.shape[1] // heads
    kc = weights.shape[0] // P
    xt_hi, xt_lo = xt
    with ExitStack() as scope:
        sb = lambda name, shape, dtype: sbuf(nc, scope, f"{tag}_{name}", shape, dtype)
        sem = lambda name: semaphore(nc, scope, f"{tag}_{name}")
        split_w = s.x1[:, :, :].rearrange("p t d -> p (t d)").bitcast(F16)[:, 0:4 * kc * cols].rearrange(
            "p (i a k n) -> p i a k n", i=2, a=2, k=kc)
        w_hi, w_lo = split_w[:, 0], split_w[:, 1]
        att = sb("att", [P, 2, 2, cols], F32)
        product = s.x1[:, :, :].rearrange("p t d -> p (t d)")[:, 2 * kc * cols:2 * (kc + 1) * cols].rearrange(
            "p (i n) -> p i n", i=2)
        att_loaded = [sem(f"att_loaded{i}") for i in range(2)]
        w_hi_ready = sem("w_hi_ready")
        w_lo_ready = sem("w_lo_ready")
        summed = sem("summed")
        hi_ready = sem("hi_ready")
        lo_ready = sem("lo_ready")
        block = scope.enter_context(nc.Block())

        @block.sync
        def _(sp):
            for j in range(heads):
                if j >= 1:
                    sp.wait_ge(w_lo_ready, j)
                    load_head(sp, w32, weights, j, cols, w_loaded)
                if j >= 2:
                    sp.wait_ge(lo_ready, NT * (j - 1))
                for i, vector in enumerate((att_src, att_dst)):
                    sp.dma_start(att[:, j % 2, i, :], vector[j:j + 1, :].to_broadcast([P, cols])
                                 ).then_inc(att_loaded[j % 2], 16)

        @block.scalar
        def _(act):
            def split(j):
                act.wait_ge(w_loaded, 16 * (j + 1))
                if j >= 2:
                    act.wait_ge(summed, NT * (j - 1))
                act.activation(w_hi[:, j % 2, :, :], w32[:, :, :], ACT.Copy, scale=WSCALE).then_inc(w_hi_ready, 1)

            split(0)
            for j in range(heads):
                if j + 1 < heads:
                    act.wait_ge(w_lo_ready, j + 1)
                    split(j + 1)
                for t in range(NT):
                    n = j * NT + t
                    act.wait_ge(summed, n + 1)
                    act.activation(h_hi[:, t, j * cols:(j + 1) * cols], s.ps[n % 4][:, 0:cols], ACT.Copy,
                                   scale=1 / WSCALE).then_inc(hi_ready, 1)

        @block.vector
        def _(dve):
            def split(j):
                dve.wait_ge(w_hi_ready, j + 1)
                dve.scalar_tensor_tensor(out=w_lo[:, j % 2, :, :], in0=w32[:, :, :], scalar=WSCALE,
                                         in1=w_hi[:, j % 2, :, :], op0=ALU.mult, op1=ALU.subtract
                                         ).then_inc(w_lo_ready, 1)

            split(0)
            for j in range(heads):
                if j + 1 < heads:
                    split(j + 1)
                dve.wait_ge(att_loaded[j % 2], 32 * (j // 2 + 1))
                for t in range(NT):
                    n = j * NT + t
                    dve.wait_ge(hi_ready, n + 1)
                    for i in range(2):
                        if n >= 1:
                            dve.wait_ge(lo_ready, n)
                        dve.tensor_tensor_reduce(out=product[:, i, :], in0=s.ps[n % 4][:, 0:cols],
                                                 in1=att[:, j % 2, i, :], scale=1 / WSCALE, scalar=0.0, op0=ALU.mult,
                                                 op1=ALU.add, accum_out=attention[:, t, i * heads + j:i * heads + j + 1])
                    dve.scalar_tensor_tensor(out=h_lo[:, t, j * cols:(j + 1) * cols], in0=s.ps[n % 4][:, 0:cols],
                                             scalar=1 / WSCALE, in1=h_hi[:, t, j * cols:(j + 1) * cols],
                                             op0=ALU.mult, op1=ALU.subtract).then_inc(lo_ready, 1)

        @block.tensor
        def _(pe):
            for j in range(heads):
                pe.wait_ge(w_lo_ready, j + 1)
                for t in range(NT):
                    n = j * NT + t
                    if n >= 4:
                        pe.wait_ge(lo_ready, n - 3)
                    for k in range(kc):
                        ins = pair_product(pe, s.ps[n % 4][:, 0:cols], xt_hi[:, k, t * P:(t + 1) * P],
                                           xt_lo[:, k, t * P:(t + 1) * P], w_hi[:, j % 2, k, :],
                                           w_lo[:, j % 2, k, :], k == 0, k == kc - 1)
                    ins.then_inc(summed, 1)


def edge_maxima(nc, s, tag, heads, attention, source02, offsets, offsets_b=None):
    with ExitStack() as scope:
        sb = lambda name, shape, dtype: sbuf(nc, scope, f"{tag}_{name}", shape, dtype)
        sem = lambda name: semaphore(nc, scope, f"{tag}_{name}")
        mask_t = sb("mask_t", [P, NT, N], BF16)
        mask = sb("mask", [P, 2, NPAD], BF16)
        att_rows = sb("att_rows", [8, NPAD], F32)
        att_b = s.x1[:, :, :].rearrange("p t d -> p (t d)")[:, 0:heads * NPAD].rearrange("p (j n) -> p j n", j=heads)
        shifted = sb("shifted", [P, NPAD], F32)
        greatest = sb("greatest", [P, NT, heads], F32)
        maximum = sb("maximum", [P, NT, heads], F32)
        rest = sb("rest", [P, NT, 8], F32)
        dve_step = sem("dve_step")
        mask_ready = sem("mask_ready")
        rows_turned = sem("rows_turned")
        rows_ready = sem("rows_ready")
        spread = sem("spread")
        spread_copied = sem("spread_copied")
        mask_turned = sem("mask_turned")
        mask_copied = sem("mask_copied")
        tile_done = sem("tile_done")
        rest_ready = sem("rest_ready")
        rest_turned = sem("rest_turned")
        rest_copied = sem("rest_copied")
        offsets_ready = sem("offsets_ready")
        offsets_spread = sem("offsets_spread")
        width = [512, 512, NPAD - 1024]
        spreads = [(j, g) for j in range(heads) for g in range(3)]
        block = scope.enter_context(nc.Block())

        @block.vector
        def _(dve):
            steps = [0]

            def link(ins):
                steps[0] += 1
                ins.then_inc(dve_step, 1)
                dve.wait_ge(dve_step, steps[0])

            dve.tensor_scalar(mask_t[:, :, :], s.CT[:, :, 0:N], 0.0, NO_EDGE, ALU.is_equal, ALU.mult
                              ).then_inc(mask_ready, 1)
            dve.memset(greatest[:, :, :], 0.0)
            dve.memset(rest[:, :, :], 0.0)
            link(dve.tensor_scalar(source02[:, :, 0:heads], attention[:, :, 0:heads], SLOPE, None, ALU.mult))
            dve.wait_ge(spread_copied, len(spreads))
            for t in range(NT):
                dve.wait_ge(mask_copied, t + 1)
                for j in range(heads):
                    r = rows(t)
                    ins = dve.tensor_tensor_reduce(out=shifted[0:r, :], in0=mask[0:r, t % 2, :], in1=att_b[0:r, j, :],
                                                   scale=1.0, scalar=NO_EDGE * 2, op0=ALU.add, op1=ALU.max,
                                                   accum_out=greatest[0:r, t, j:j + 1])
                    link(ins)
                dve.nop().then_inc(tile_done, 1)
            dest = attention[:, :, heads:2 * heads]
            link(dve.tensor_tensor(maximum[:, :, :], greatest[:, :, :], dest, ALU.add))
            link(dve.scalar_tensor_tensor(out=maximum[:, :, :], in0=maximum[:, :, :], scalar=SLOPE,
                                          in1=maximum[:, :, :], op0=ALU.mult, op1=ALU.max))
            pairs = rest[:, :, :].rearrange("p t (j i) -> p t j i", i=2)
            dve.tensor_tensor(pairs[:, :, 0:heads, 0], dest, maximum[:, :, :], ALU.subtract)
            dve.scalar_tensor_tensor(out=pairs[:, :, 0:heads, 1], in0=dest, scalar=SLOPE, in1=maximum[:, :, :],
                                     op0=ALU.mult, op1=ALU.subtract).then_inc(rest_ready, 1)

        @block.tensor
        def _(pe):
            k = 2 * heads
            for t in range(NT):
                ins = pe.transpose(s.ps[t // 4][0:k, (t % 4) * P:(t % 4 + 1) * P], attention[:, t, 0:k], s.ident[:, :])
            ins.then_inc(rows_turned, 1)
            pe.wait_ge(rows_ready, 1)
            for n, (j, g) in enumerate(spreads):
                if n >= 2:
                    pe.wait_ge(spread_copied, n - 1)
                pe.matmul(s.ps[3 + n % 2][:, 0:width[g]], s.sel[0:k, j, :], att_rows[0:k, g * 512:g * 512 + width[g]],
                          start=True, stop=True).then_inc(spread, 1)
            pe.wait_ge(mask_ready, 1)
            for t in range(NT):
                if t >= 1:
                    if t >= 2:
                        pe.wait_ge(mask_copied, t - 1)
                lead, tail = mask_banks(s, t)
                for c in range(NT):
                    out = lead[0:rows(t), c * P:(c + 1) * P] if c < 8 else tail[0:rows(t), (c - 8) * P:(c - 7) * P]
                    ins = pe.transpose(out, mask_t[:, c, t * P:t * P + rows(t)], s.ident_bf[:, :])
                ins.then_inc(mask_turned, 1)
            pe.wait_ge(rest_ready, 1)
            for t in range(NT):
                ins = pe.transpose(s.ps[1 + t // 4][0:8, (t % 4) * P:(t % 4 + 1) * P], rest[:, t, :], s.ident[:, :])
            ins.then_inc(rest_turned, 1)
            if offsets_b is not None:
                pe.wait_ge(offsets_ready, 1)
                for i in range(2):
                    for g in range(3):
                        ins = pe.matmul(s.ps[[0, 1, 2, 5, 6, 7][3 * i + g]][:, 0:width[g]], s.sel[:, i, :],
                                        offsets[:, g * 512:g * 512 + width[g]], start=True, stop=True)
                ins.then_inc(offsets_spread, 1)

        @block.scalar
        def _(act):
            k = 2 * heads
            act.wait_ge(rows_turned, 1)
            for g in range(3):
                ins = act.activation(att_rows[0:k, g * 512:g * 512 + width[g]], s.ps[g][0:k, 0:width[g]], ACT.Copy)
            ins.then_inc(rows_ready, 1)
            for n, (j, g) in enumerate(spreads):
                act.wait_ge(spread, n + 1)
                act.activation(att_b[:, j, g * 512:g * 512 + width[g]], s.ps[3 + n % 2][:, 0:width[g]], ACT.Copy
                               ).then_inc(spread_copied, 1)
            for t in range(NT):
                act.wait_ge(mask_turned, t + 1)
                if t >= 2:
                    act.wait_ge(tile_done, t - 1)
                lead, tail = mask_banks(s, t)
                r = rows(t)
                act.activation(mask[0:r, t % 2, 0:1024], lead[0:r, :], ACT.Copy)
                act.activation(mask[0:r, t % 2, 1024:NPAD], tail[0:r, 0:NPAD - 1024], ACT.Copy).then_inc(mask_copied, 1)
            act.wait_ge(rest_turned, 1)
            for g in range(3):
                ins = act.activation(offsets[:, g * 512:g * 512 + width[g]], s.ps[1 + g][0:8, 0:width[g]], ACT.Copy)
            ins.then_inc(offsets_ready, 1)
            if offsets_b is not None:
                act.wait_ge(offsets_spread, 1)
                for i in range(2):
                    for g in range(3):
                        act.activation(offsets_b[:, i, g * 512:g * 512 + width[g]],
                                       s.ps[[0, 1, 2, 5, 6, 7][3 * i + g]][:, 0:width[g]], ACT.Copy)


def mask_banks(s, t):
    lead, tail = ((5, 6), (7, 0))[t % 2]
    return s.ps[lead][:, :].bitcast(BF16), s.ps[tail][:, :].bitcast(BF16)


class EdgeWeights:
    KP = NT // 2
    SLOTS = 4

    def __init__(self, nc, s, scope, tag, units, width, attention, source02, offsets, off_places, in_psum,
                 lo=None):
        self.in_psum = in_psum
        self.s, self.units, self.attention, self.source02 = s, units, attention, source02
        self.offsets, self.off_places = offsets, off_places
        self.steps = len(units) * self.KP
        self.hi = sbuf(nc, scope, f"{tag}_p_hi", [P, 2, NT, width], F16)
        self.lo = sbuf(nc, scope, f"{tag}_p_lo", [P, 2, NT, width], F16) if lo is None else lo
        self.work = sbuf(nc, scope, f"{tag}_work", [P, self.SLOTS, 2, width], F32)
        self.offsets_spread = semaphore(nc, scope, f"{tag}_offsets_spread")
        self.upper_ready = semaphore(nc, scope, f"{tag}_upper_ready")
        self.score_ready = semaphore(nc, scope, f"{tag}_score_ready")
        self.exp_ready = semaphore(nc, scope, f"{tag}_exp_ready")
        self.weight_ready = semaphore(nc, scope, f"{tag}_weight_ready")
        self.hi_ready = semaphore(nc, scope, f"{tag}_hi_ready")
        self.lo_ready = semaphore(nc, scope, f"{tag}_lo_ready")

    def place(self, n):
        u, q = divmod(n, self.KP)
        j, (at, w) = self.units[u]
        return u, 2 * q, j, at, w, self.work[:, n % self.SLOTS, :, 0:w]

    def spread(self, pe, u):
        j, (at, w) = self.units[u]
        if u >= 2:
            pe.wait_ge(self.score_ready, NT * (u - 1))
        for i in range(2):
            ins = pe.matmul(self.off_places(u)[i], self.s.sel[:, 2 * j + i, :],
                            self.offsets[:, at:at + w], start=True, stop=True)
        ins.then_inc(self.offsets_spread, 1)

    def act_upper(self, act, n):
        u, k, j, at, w, work = self.place(n)
        if k == 0 and self.in_psum:
            act.wait_ge(self.offsets_spread, u + 1)
        if n >= self.SLOTS:
            act.wait_ge(self.lo_ready, n - self.SLOTS + 1)
        for i in range(2):
            act.activation(work[:, i, :], self.off_places(u)[0], ACT.Identity,
                           bias=self.attention[:, k + i, j:j + 1]).then_inc(self.upper_ready, 1)

    def dve_score(self, dve, n):
        u, k, j, at, w, work = self.place(n)
        for i in range(2):
            dve.wait_ge(self.upper_ready, 2 * n + i + 1)
            dve.scalar_tensor_tensor(out=work[:, i, :], in0=self.off_places(u)[1],
                                     scalar=self.source02[:, k + i, j:j + 1], in1=work[:, i, :],
                                     op0=ALU.add, op1=ALU.max).then_inc(self.score_ready, 1)

    def act_exp(self, act, n):
        work = self.place(n)[-1]
        act.wait_ge(self.score_ready, 2 * n + 2)
        act.activation(work, work, ACT.Exp).then_inc(self.exp_ready, 1)

    def dve_weight(self, dve, n):
        u, k, j, at, w, work = self.place(n)
        dve.wait_ge(self.exp_ready, n + 1)
        dve.scalar_tensor_tensor(out=work, in0=work, scalar=1.0, in1=self.s.CT[:, k:k + 2, at:at + w],
                                 op0=ALU.min, op1=ALU.mult).then_inc(self.weight_ready, 1)

    def act_hi(self, act, n, used, per_unit):
        u, k, j, at, w, work = self.place(n)
        act.wait_ge(self.weight_ready, n + 1)
        if u >= 2:
            act.wait_ge(used, per_unit * (u - 1))
        act.activation(self.hi[:, u % 2, k:k + 2, 0:w], work, ACT.Copy).then_inc(self.hi_ready, 1)

    def pool_lo(self, pool, n):
        u, k, j, at, w, work = self.place(n)
        pool.wait_ge(self.hi_ready, n + 1)
        pool.tensor_tensor(self.lo[:, u % 2, k:k + 2, 0:w], work, self.hi[:, u % 2, k:k + 2, 0:w], ALU.subtract
                           ).then_inc(self.lo_ready, 1)


def aggregate_heads(nc, s, attention, source02, offsets, h_hi, h_lo, bias, scratch_hi, scratch_lo, ahead):
    units = [(j, block) for j in range(HEADS) for block in BLOCKS]
    HCC = HID // P
    chunks = len(units) * HCC
    with ExitStack() as scope:
        sb = lambda name, shape, dtype: sbuf(nc, scope, f"g1_{name}", shape, dtype)
        sem = lambda name: semaphore(nc, scope, f"g1_{name}")

        def off_places(u):
            return [s.ps[2 * (u % 2) + i][:, 0:units[u][1][1]] for i in range(2)]

        DEN, AGG = s.ps[4], (s.ps[5], s.ps[6], s.ps[7])
        spare = s.x1[:, :, :].rearrange("p t d -> p (t d)").bitcast(F16)[:, 0:2 * NT * 512]
        weights = EdgeWeights(nc, s, scope, "g1", units, 512, attention, source02, offsets, off_places,
                              True, lo=spare.rearrange("p (a t w) -> p a t w", a=2, t=NT))
        inverse = sb("inverse", [P, 2, 512], F32)
        value = sb("value", [P, 2, 512], F32)
        expd = s.x1[:, :, :].rearrange("p t d -> p (t d)")[:, NT * 512:(NT + 2) * 512].rearrange("p (a w) -> p a w", a=2)
        out_hi = sb("out_hi", [P, 2, 512], F16)
        out_lo = sb("out_lo", [P, 2, 512], F16)
        b1 = sb("b1", [P, HC], F32)
        b1_loaded = sem("b1_loaded")
        den_summed = sem("den_summed")
        inverse_ready = sem("inverse_ready")
        summed = sem("summed")
        scaled = sem("scaled")
        exp2_ready = sem("exp2_ready")
        relu_ready = sem("relu_ready")
        elu_ready = sem("elu_ready")
        out_hi_ready = sem("out_hi_ready")
        out_lo_ready = sem("out_lo_ready")
        stored = [sem(f"stored{i}") for i in range(2)]
        block = scope.enter_context(nc.Block())

        def width(c):
            return units[c // HCC][1][1]

        due = (3, 4, 6, 7)
        slot_after = {u * EdgeWeights.KP + due[i]: (u - 1) * HCC + i for u in range(1, len(units)) for i in range(HCC)}

        def slots_left(steps):
            return range(sum(n < steps for n in slot_after), chunks + 2)

        @block.sync
        def _(sp):
            ahead(sp)
            with nc.allow_non_contiguous_dma(reason="one short vector per partition"):
                sp.dma_start(b1[:, :], bias.rearrange("(c p) -> p c", p=P)).then_inc(b1_loaded, 16)
            for n in range(chunks):
                (j, (at, w)), c = units[n // HCC], n % HCC
                sp.wait_ge(out_lo_ready, n + 1)
                sp.dma_start(scratch_hi[j * HCC + c, :, at:at + w], out_hi[:, n % 2, 0:w]).then_inc(stored[n % 2], 16)
                sp.dma_start(scratch_lo[j * HCC + c, :, at:at + w], out_lo[:, n % 2, 0:w]).then_inc(stored[n % 2], 16)
            for i in range(2):
                sp.wait_ge(stored[i], 32 * (chunks // 2))

        @block.scalar
        def _(act):
            def finish(slot):
                if 0 <= slot - 1 < chunks:
                    n = slot - 1
                    w = width(n)
                    act.wait_ge(elu_ready, n + 1)
                    if n >= 2:
                        act.wait_ge(stored[n % 2], 32 * (n // 2))
                    act.activation(out_hi[:, n % 2, 0:w], value[:, n % 2, 0:w], ACT.Copy, bias=-1.0
                                   ).then_inc(out_hi_ready, 1)
                if slot < chunks:
                    n = slot
                    w = width(n)
                    col = units[n // HCC][0] * HCC + n % HCC
                    act.wait_ge(scaled, n + 1)
                    act.activation(expd[:, n % 2, 0:w], value[:, n % 2, 0:w], ACT.Exp, bias=b1[:, col:col + 1]
                                   ).then_inc(exp2_ready, 1)
                    act.wait_ge(exp2_ready, n + 1)
                    act.activation(value[:, n % 2, 0:w], value[:, n % 2, 0:w], ACT.Relu, bias=b1[:, col:col + 1]
                                   ).then_inc(relu_ready, 1)

            act.wait_ge(b1_loaded, 16)
            for n in range(weights.steps + 2):
                if n < weights.steps:
                    weights.act_upper(act, n)
                if 0 <= n - 1 < weights.steps:
                    weights.act_exp(act, n - 1)
                if 0 <= n - 2:
                    weights.act_hi(act, n - 2, summed, HCC)
                if n in slot_after:
                    finish(slot_after[n])
            for slot in slots_left(weights.steps + 2):
                finish(slot)

        @block.vector
        def _(dve):
            def finish(slot):
                if 0 <= slot - 2 < chunks:
                    n = slot - 2
                    w = width(n)
                    dve.wait_ge(out_hi_ready, n + 1)
                    dve.scalar_tensor_tensor(out=out_lo[:, n % 2, 0:w], in0=value[:, n % 2, 0:w], scalar=1.0,
                                             in1=out_hi[:, n % 2, 0:w], op0=ALU.subtract, op1=ALU.subtract
                                             ).then_inc(out_lo_ready, 1)
                if 0 <= slot - 1 < chunks:
                    n = slot - 1
                    w = width(n)
                    dve.wait_ge(relu_ready, n + 1)
                    dve.scalar_tensor_tensor(out=value[:, n % 2, 0:w], in0=expd[:, n % 2, 0:w], scalar=1.0,
                                             in1=value[:, n % 2, 0:w], op0=ALU.min, op1=ALU.add).then_inc(elu_ready, 1)
                if slot < chunks:
                    n = slot
                    w = width(n)
                    u = n // HCC
                    if n % HCC == 0:
                        dve.wait_ge(den_summed, u + 1)
                        dve.reciprocal(inverse[:, u % 2, 0:w], DEN[:, 0:w]).then_inc(inverse_ready, 1)
                        dve.wait_ge(inverse_ready, u + 1)
                    dve.wait_ge(summed, n + 1)
                    if n >= 2:
                        dve.wait_ge(out_lo_ready, n - 1)
                    dve.tensor_tensor(value[:, n % 2, 0:w], AGG[n % 3][:, 0:w], inverse[:, u % 2, 0:w],
                                      ALU.mult).then_inc(scaled, 1)

            for n in range(weights.steps + 1):
                if n < weights.steps:
                    weights.dve_score(dve, n)
                if n >= 1:
                    weights.dve_weight(dve, n - 1)
                if n in slot_after:
                    finish(slot_after[n])
            for slot in slots_left(weights.steps + 1):
                finish(slot)

        @block.gpsimd
        def _(pool):
            for n in range(weights.steps):
                weights.pool_lo(pool, n)

        @block.tensor
        def _(pe):
            weights.spread(pe, 0)
            weights.spread(pe, 1)
            for u, (j, (at, w)) in enumerate(units):
                pe.wait_ge(weights.lo_ready, EdgeWeights.KP * (u + 1))
                if u + 2 < len(units):
                    weights.spread(pe, u + 2)
                p_hi, p_lo = weights.hi[:, u % 2, :, 0:w], weights.lo[:, u % 2, :, 0:w]
                if u >= 1:
                    pe.wait_ge(inverse_ready, u)
                for k in range(NT):
                    pe.matmul(DEN[:, 0:w], s.ones16[:, :], p_hi[:, k, :], start=(k == 0), stop=False)
                    ins = pe.matmul(DEN[:, 0:w], s.ones16[:, :], p_lo[:, k, :], start=False, stop=(k == NT - 1))
                ins.then_inc(den_summed, 1)
                for c in range(HCC):
                    n = u * HCC + c
                    if n >= 3:
                        pe.wait_ge(scaled, n - 2)
                    cols = slice((j * HCC + c) * P, (j * HCC + c + 1) * P)
                    for k in range(NT):
                        ins = pair_product(pe, AGG[n % 3][:, 0:w], h_hi[:, k, cols], h_lo[:, k, cols],
                                           p_hi[:, k, :], p_lo[:, k, :], k == 0, k == NT - 1)
                    ins.then_inc(summed, 1)


W2_SLOTS = 3


def load_w2(eng, w32, weights, q, sem):
    eng.dma_start(w32[:, q % W2_SLOTS, :], weights[q * P:(q + 1) * P, :]).then_inc(sem, 16)


def project_hidden(nc, s, weights, w32, w_loaded, att_src, att_dst, scratch_hi, scratch_lo, h_hi, h_lo, attention):
    with ExitStack() as scope:
        sb = lambda name, shape, dtype: sbuf(nc, scope, f"p2_{name}", shape, dtype)
        sem = lambda name: semaphore(nc, scope, f"p2_{name}")
        w_hi = sb("w_hi", [P, HC, D], F16)
        w_lo = sb("w_lo", [P, HC, D], F16)
        x_hi = sb("x_hi", [P, 2, HC, 256], F16)
        x_lo = sb("x_lo", [P, 2, HC, 256], F16)
        att = sb("att", [P, 2, D], F32)
        product = sb("product", [P, 2, DHALF], F32)
        halves = sb("halves", [P, NT, 2, 2], F32)
        x_loaded = [sem(f"x_loaded{i}") for i in range(2)]
        att_loaded = sem("att_loaded")
        w_hi_ready = sem("w_hi_ready")
        w_lo_ready = sem("w_lo_ready")
        summed = sem("summed")
        hi_ready = sem("hi_ready")
        lo_ready = sem("lo_ready")
        scored = sem("scored")
        block = scope.enter_context(nc.Block())
        blocks = [(at, min(256, N - at)) for at in range(0, N, 256)]

        @block.sync
        def _(sp):
            for q in range(W2_SLOTS, HC):
                sp.wait_ge(w_lo_ready, q - W2_SLOTS + 1)
                load_w2(sp, w32, weights, q, w_loaded[q % W2_SLOTS])

        @block.gpsimd
        def _(pool):
            for i, vector in enumerate((att_src, att_dst)):
                pool.dma_start(att[:, i, :], vector[0:1, :].to_broadcast([P, D])).then_inc(att_loaded, 16)
            for b, (at, w) in enumerate(blocks):
                if b >= 2:
                    pool.wait_ge(summed, 4 * (b - 1))
                for tile, dram in ((x_hi, scratch_hi), (x_lo, scratch_lo)):
                    pool.dma_start(tile[:, b % 2, :, 0:w], dram[:, :, at:at + w].rearrange("c p n -> p c n")
                                   ).then_inc(x_loaded[b % 2], 16)

        @block.scalar
        def _(act):
            for q in range(HC):
                act.wait_ge(w_loaded[q % W2_SLOTS], 16 * (q // W2_SLOTS + 1))
                act.activation(w_hi[:, q, :], w32[:, q % W2_SLOTS, :], ACT.Copy, scale=WSCALE).then_inc(w_hi_ready, 1)
            for n in range(2 * NT):
                t, half = divmod(n, 2)
                r, cols = rows(t), slice(half * DHALF, (half + 1) * DHALF)
                act.wait_ge(summed, n + 1)
                act.activation(h_hi[0:r, t, cols], s.ps[n % 6][0:r, 0:DHALF], ACT.Copy, scale=1 / WSCALE
                               ).then_inc(hi_ready, 1)

        @block.vector
        def _(dve):
            for q in range(HC):
                dve.wait_ge(w_hi_ready, q + 1)
                dve.scalar_tensor_tensor(out=w_lo[:, q, :], in0=w32[:, q % W2_SLOTS, :], scalar=WSCALE,
                                         in1=w_hi[:, q, :], op0=ALU.mult, op1=ALU.subtract).then_inc(w_lo_ready, 1)
            dve.memset(h_hi[:, :, D:D + 2], 0.0)
            dve.memset(h_lo[:, :, D:D + 2], 0.0)
            dve.memset(h_hi[96:P, NT - 1, 0:D], 0.0)
            dve.memset(h_lo[96:P, NT - 1, 0:D], 0.0)
            dve.memset(halves[:, :, :, :], 0.0).then_inc(scored, 1)
            dve.wait_ge(att_loaded, 32)
            dve.wait_ge(scored, 1)
            dve.memset(h_hi[:, :, D:D + 1], 1.0)
            for n in range(2 * NT):
                t, half = divmod(n, 2)
                r, cols = rows(t), slice(half * DHALF, (half + 1) * DHALF)
                dve.wait_ge(hi_ready, n + 1)
                if n >= 1:
                    dve.wait_ge(lo_ready, n)
                for i in range(2):
                    dve.tensor_tensor_reduce(out=product[0:r, i, :], in0=s.ps[n % 6][0:r, 0:DHALF],
                                             in1=att[0:r, i, cols], scale=1 / WSCALE, scalar=0.0, op0=ALU.mult,
                                             op1=ALU.add, accum_out=halves[0:r, t, i, half:half + 1])
                dve.scalar_tensor_tensor(out=h_lo[0:r, t, cols], in0=s.ps[n % 6][0:r, 0:DHALF], scalar=1 / WSCALE,
                                         in1=h_hi[0:r, t, cols], op0=ALU.mult, op1=ALU.subtract).then_inc(lo_ready, 1)
            dve.wait_ge(lo_ready, 2 * NT)
            dve.tensor_tensor(attention[:, :, 0:2], halves[:, :, :, 0], halves[:, :, :, 1], ALU.add)

        @block.tensor
        def _(pe):
            for b in range(2):
                pe.wait_ge(x_loaded[b], 32)
            for k in range(HC):
                pe.wait_ge(w_lo_ready, k + 1)
                for n in range(6):
                    t, half = divmod(n, 2)
                    cols = slice(half * DHALF, (half + 1) * DHALF)
                    b, at = t // 2, (t % 2) * P
                    ins = pair_product(pe, s.ps[n][:, 0:DHALF], x_hi[:, b, k, at:at + P], x_lo[:, b, k, at:at + P],
                                       w_hi[:, k, cols], w_lo[:, k, cols], k == 0, k == HC - 1)
                    if k == HC - 1:
                        ins.then_inc(summed, 1)
            for n in range(6, 2 * NT):
                t, half = divmod(n, 2)
                r, cols = rows(t), slice(half * DHALF, (half + 1) * DHALF)
                b, at = t // 2, (t % 2) * P
                pe.wait_ge(x_loaded[b % 2], 32 * (b // 2 + 1))
                pe.wait_ge(lo_ready, n - 5)
                for k in range(HC):
                    ins = pair_product(pe, s.ps[n % 6][0:r, 0:DHALF], x_hi[:, b % 2, k, at:at + r],
                                       x_lo[:, b % 2, k, at:at + r], w_hi[:, k, cols], w_lo[:, k, cols],
                                       k == 0, k == HC - 1)
                ins.then_inc(summed, 1)


def aggregate_nodes(nc, s, attention, source02, offsets_b, h_hi, h_lo, x_dram, bias, x1):
    units = [(0, (at, min(256, N - at))) for at in range(0, N, 256)]
    with ExitStack() as scope:
        sb = lambda name, shape, dtype: sbuf(nc, scope, f"g2_{name}", shape, dtype)
        sem = lambda name: semaphore(nc, scope, f"g2_{name}")

        def off_places(u):
            at, w = units[u][1]
            return [offsets_b[:, i, at:at + w] for i in range(2)]

        weights = EdgeWeights(nc, s, scope, "g2", units, 256, attention, source02, None, off_places, False)
        b2 = sb("b2", [P, D], F32)
        inverse = sb("inverse", [P, NT], F32)
        loaded = sem("loaded")
        pads_zeroed = sem("pads_zeroed")
        based = sem("based")
        summed = sem("summed")
        inverse_ready = sem("inverse_ready")
        added = sem("added")
        block = scope.enter_context(nc.Block())

        @block.sync
        def _(sp):
            sp.dma_start(b2[:, :], bias.rearrange("(a d) -> a d", a=1).to_broadcast([P, D])).then_inc(loaded, 16)
            sp.wait_ge(pads_zeroed, 1)
            load_nodes(sp, x1, x_dram, loaded)

        @block.scalar
        def _(act):
            for n in range(weights.steps + 2):
                if n < weights.steps:
                    weights.act_upper(act, n)
                if 0 <= n - 1 < weights.steps:
                    weights.act_exp(act, n - 1)
                if 0 <= n - 2:
                    weights.act_hi(act, n - 2, summed, 2)

        @block.vector
        def _(dve):
            def finish(t):
                r = rows(t)
                lead, tail = s.ps[2 + 2 * (t % 3)], s.ps[3 + 2 * (t % 3)]
                dve.wait_ge(summed, t + 1)
                dve.reciprocal(inverse[0:r, t:t + 1], tail[0:r, DHALF:DHALF + 1]).then_inc(inverse_ready, 1)
                dve.wait_ge(inverse_ready, t + 1)
                for half, bank in ((0, lead), (1, tail)):
                    cols = slice(half * DHALF, (half + 1) * DHALF)
                    dve.scalar_tensor_tensor(out=x1[0:r, t, cols], in0=bank[0:r, 0:DHALF],
                                             scalar=inverse[0:r, t:t + 1], in1=x1[0:r, t, cols], op0=ALU.mult,
                                             op1=ALU.add).then_inc(added, 1)

            dve.memset(x1[96:P, NT - 1, :], 0.0).then_inc(pads_zeroed, 1)
            for n in range(weights.steps + 1):
                if n < weights.steps:
                    weights.dve_score(dve, n)
                if n >= 1:
                    weights.dve_weight(dve, n - 1)
                if n == EdgeWeights.KP:
                    dve.wait_ge(loaded, 48)
                    for t in range(NT):
                        dve.tensor_tensor(x1[0:rows(t), t, :], x1[0:rows(t), t, :], b2[0:rows(t), :], ALU.add
                                          ).then_inc(based, 1)
                    dve.wait_ge(based, NT)
                u, q = divmod(n, EdgeWeights.KP)
                if 1 <= u < len(units) and q in (2, 4):
                    finish(2 * (u - 1) + q // 2 - 1)
            finish(NT - 2)
            finish(NT - 1)

        @block.gpsimd
        def _(pool):
            for n in range(weights.steps):
                weights.pool_lo(pool, n)

        @block.tensor
        def _(pe):
            for t in range(NT):
                u, at = t // 2, (t % 2) * P
                r = rows(t)
                if t % 2 == 0:
                    pe.wait_ge(weights.lo_ready, EdgeWeights.KP * (u + 1))
                if t >= 3:
                    pe.wait_ge(added, 2 * (t - 2))
                lead, tail = s.ps[2 + 2 * (t % 3)], s.ps[3 + 2 * (t % 3)]
                for half, bank in ((0, lead), (1, tail)):
                    cols = slice(half * DHALF, (half + 1) * DHALF + half)
                    out = bank[0:r, 0:DHALF + half]
                    for k in range(NT):
                        ins = pair_product(pe, out, weights.hi[:, u % 2, k, at:at + r],
                                           weights.lo[:, u % 2, k, at:at + r], h_hi[:, k, cols], h_lo[:, k, cols],
                                           k == 0, k == NT - 1)
                ins.then_inc(summed, 1)


def load_qkv(eng, w32, w_qkv, i, m, sem):
    eng.dma_start(w32[:, (3 * i + m) % 2, :, :], w_qkv[:, m * D + i * P:m * D + (i + 1) * P]
                  .rearrange("(k p) n -> p k n", p=P)).then_inc(sem, 16)


def attend(nc, s, xt, w_qkv, w32, w_loaded, out_hi, out_lo):
    SLOTS = len(BLOCKS) * NT
    WIDTH = [512, 512, NPAD - 1024]
    scale = float(HD) ** -0.5
    todo = [[("qk", m, g)] for m in range(2) for g in range(3)]
    QK_JOBS = len(todo)
    maxima_jobs = [("max", hd, t, g) for hd in range(2) for t in range(NT) for g in range(3)]
    WIDE_SLOTS = 2 * NT - QK_JOBS
    NARROW_SLOTS = NT - 4
    for n in range(WIDE_SLOTS):
        todo.append([maxima_jobs.pop(0) for _ in range(3)])
        if n % 4 == 1 and n < 12:
            todo[-1].insert(1, ("v", 2, n // 4))
    for n in range(NARROW_SLOTS):
        count = -(-len(maxima_jobs) // (NARROW_SLOTS - n))
        todo.append([maxima_jobs.pop(0) for _ in range(count)])
    todo += [[], [("row", 0)], [("row", 1), ("row", 2)], []]
    jobs = [job for slot_jobs in todo for job in slot_jobs]
    JOBS = len(jobs)
    plan = [[jobs.index(job) for job in slot_jobs] for slot_jobs in todo]
    LAST_MAX = max(n for n, job in enumerate(jobs) if job[0] == "max")
    LAST_V = max(n for n, job in enumerate(jobs) if job[0] == "v")
    act_jobs = [n for n, job in enumerate(jobs) if job[0] != "max"]
    SPLIT_SLOTS = {8: 0, 12: 1, 18: 2}
    RING = 4
    with ExitStack() as scope:
        sb = lambda name, shape, dtype: sbuf(nc, scope, f"a_{name}", shape, dtype)
        sem = lambda name: semaphore(nc, scope, f"a_{name}")
        w_hi = sb("w_hi", [P, 3, DC, P], F16)
        w_lo = sb("w_lo", [P, 3, DC, P], F16)
        q1, q2, k1, k2 = (sb(name, [P, 2, 2, NPAD], F16) for name in ("q1", "q2", "k1", "k2"))
        v_hi = sb("v_hi", [P, 2, NT, P], F16)
        v_lo = sb("v_lo", [P, 2, NT, P], F16)
        maxima = sb("maxima", [P, 2 * NT, 3], F32)
        greatest = sb("greatest", [P, 2, NT], F32)
        stack = sb("stack", [P, NT, P], F16)
        work = sb("work", [P, RING, 2, 512], F32)
        p_hi = sb("p_hi", [P, RING, 2, 512], F16)
        p_lo = sb("p_lo", [P, RING, 2, 512], F16)
        inverse = sb("inverse", [P, 512], F32)
        value = sb("value", [P, 2, 512], F32)
        zeroed = sem("zeroed")
        stacks_zeroed = sem("stacks_zeroed")
        constants_ready = sem("constants_ready")
        w_hi_ready = sem("w_hi_ready")
        w_lo_ready = sem("w_lo_ready")
        job_product = sem("job_product")
        job_act = sem("job_act")
        job_dve = sem("job_dve")
        maxima_ready = sem("maxima_ready")
        scores_ready = sem("scores_ready")
        exp_ready = sem("exp_ready")
        hi_ready = sem("hi_ready")
        lo_ready = [sem(f"lo_ready{i}") for i in range(2)]
        pv_done = sem("pv_done")
        den_copied = sem("den_copied")
        acc_copied = sem("acc_copied")
        inverse_ready = sem("inverse_ready")
        value_ready = sem("value_ready")
        out_hi_ready = sem("out_hi_ready")
        out_lo_ready = sem("out_lo_ready")
        ACC, DEN = s.ps[4], s.ps[5]
        blocks_done = PAIRS * len(BLOCKS)
        block = scope.enter_context(nc.Block())

        def slot(n):
            i, r = divmod(n, SLOTS)
            b, k = divmod(r, NT)
            return i, b, k, BLOCKS[b][0], BLOCKS[b][1], rows(k)

        def job_bank(i, n):
            return s.ps[6 + (i * JOBS + n) % 2]

        def act_count(i, n):
            return i * len(act_jobs) + sum(m <= n for m in act_jobs)

        def wait_lo(eng, n):
            eng.wait_ge(lo_ready[n % 2], n // 2 + 1)

        def split_weights(eng, n):
            i, b, k, at, w, r = slot(n)
            eng.wait_ge(hi_ready, n + 1)
            eng.tensor_tensor(p_lo[0:r, n % RING, :, 0:w], work[0:r, n % RING, :, 0:w], p_hi[0:r, n % RING, :, 0:w],
                              ALU.subtract).then_inc(lo_ready[n % 2], 1)

        def copy_den(act, nb):
            w = BLOCKS[nb % len(BLOCKS)][1]
            act.wait_ge(pv_done, NT * (nb + 1))
            if nb >= 1:
                act.wait_ge(value_ready, nb)
            act.activation(inverse[:, 0:w], DEN[:, 0:w], ACT.Copy).then_inc(den_copied, 1)

        def copy_acc(dve, nb):
            w = BLOCKS[nb % len(BLOCKS)][1]
            dve.wait_ge(pv_done, NT * (nb + 1))
            if nb >= 2:
                dve.wait_ge(out_lo_ready, nb - 1)
            dve.tensor_copy(value[:, nb % 2, 0:w], ACC[:, 0:w]).then_inc(acc_copied, 1)

        def finish_hi(act, nb):
            i, b = divmod(nb, len(BLOCKS))
            at, w = BLOCKS[b]
            act.wait_ge(value_ready, nb + 1)
            act.activation(out_hi[:, i, at:at + w], value[:, nb % 2, 0:w], ACT.Copy).then_inc(out_hi_ready, 1)

        def finish_value(dve, nb):
            w = BLOCKS[nb % len(BLOCKS)][1]
            dve.wait_ge(den_copied, nb + 1)
            dve.reciprocal(inverse[:, 0:w], inverse[:, 0:w]).then_inc(inverse_ready, 1)
            dve.wait_ge(inverse_ready, nb + 1)
            dve.wait_ge(acc_copied, nb + 1)
            dve.tensor_tensor(value[:, nb % 2, 0:w], value[:, nb % 2, 0:w], inverse[:, 0:w], ALU.mult
                              ).then_inc(value_ready, 1)

        def finish_lo(dve, nb):
            i, b = divmod(nb, len(BLOCKS))
            at, w = BLOCKS[b]
            dve.wait_ge(out_hi_ready, nb + 1)
            dve.tensor_tensor(out_lo[:, i, at:at + w], value[:, nb % 2, 0:w], out_hi[:, i, at:at + w], ALU.subtract
                              ).then_inc(out_lo_ready, 1)

        @block.sync
        def _(sp):
            for n in range(3 * PAIRS):
                i, m = divmod(n, 3)
                if n < 2:
                    continue
                sp.wait_ge(w_lo_ready, n - 1)
                load_qkv(sp, w32, w_qkv, i, m, w_loaded[n % 2])

        @block.gpsimd
        def _(pool):
            pool.memset(stack[:, :, :], 0.0).then_inc(zeroed, 1)
            pool.memset(maxima[:, :, :], 0.0).then_inc(zeroed, 1)
            pool.wait_ge(zeroed, 2)
            pool.wait_ge(stacks_zeroed, 2)
            for hd, b in ((0, 64), (1, 0)):
                pool.memset(k2[b:b + 1, :, hd, :], 1.0)
                ins = pool.memset(k2[b + 32:b + 33, :, hd, :], 1.0)
            ins.then_inc(constants_ready, 1)
            for n in range(1, PAIRS * SLOTS, 2):
                split_weights(pool, n)

        @block.scalar
        def _(act):
            def split(i, m):
                n = 3 * i + m
                act.wait_ge(w_loaded[n % 2], 16 * (n // 2 + 1))
                if i >= 1:
                    act.wait_ge(job_product, (i - 1) * JOBS + (QK_JOBS if m < 2 else LAST_V + 1))
                act.activation(w_hi[:, m, :, :], w32[:, n % 2, :, :], ACT.Copy, scale=WSCALE).then_inc(w_hi_ready, 1)

            def job(i, n):
                kind, *what = jobs[n]
                if kind == "max":
                    return
                bank = job_bank(i, n)
                act.wait_ge(job_product, i * JOBS + n + 1)
                if kind == "qk":
                    m, g = what
                    first = (q1, k1)[m]
                    w = WIDTH[g]
                    act.activation(first[0:64, i % 2, 0, g * 512:g * 512 + w], bank[0:64, 0:w], ACT.Copy,
                                   scale=1 / WSCALE)
                    ins = act.activation(first[64:P, i % 2, 1, g * 512:g * 512 + w], bank[64:P, 0:w], ACT.Copy,
                                         scale=1 / WSCALE)
                elif kind == "v":
                    g = what[1]
                    tiles = slice(4 * g, min(4 * g + 4, NT))
                    ins = act.activation(v_hi[:, i % 2, tiles, :].rearrange("p t n -> p (t n)"), bank[:, 0:WIDTH[g]],
                                         ACT.Copy, scale=1 / WSCALE)
                else:
                    g, = what
                    ins = act.activation(q2[64:97, i % 2, 0, g * 512:g * 512 + WIDTH[g]], bank[64:97, 0:WIDTH[g]],
                                         ACT.Copy)
                ins.then_inc(job_act, 1)

            for m in range(3):
                split(0, m)
            act.wait_ge(stacks_zeroed, 2)
            for n in range(JOBS):
                job(0, n)
            for m in range(3):
                split(1, m)
            for n in range(PAIRS * SLOTS):
                i, b, k, at, w, r = slot(n)
                act.wait_ge(scores_ready, n + 1)
                if n >= RING:
                    wait_lo(act, n - RING)
                for hd in range(2):
                    ins = act.activation(work[0:r, n % RING, hd, 0:w], s.ps[2 * (n % 2) + hd][0:r, 0:w], ACT.Exp,
                                         scale=scale)
                ins.then_inc(exp_ready, 1)
                if k == 2 and n > NT:
                    copy_den(act, n // NT - 1)
                act.wait_ge(exp_ready, n + 1)
                if n >= RING:
                    act.wait_ge(pv_done, n - RING + 1)
                act.activation(p_hi[0:r, n % RING, :, 0:w], work[0:r, n % RING, :, 0:w], ACT.Copy).then_inc(hi_ready, 1)
                if k == 5 and n > NT:
                    finish_hi(act, n // NT - 1)
                if i + 1 < PAIRS:
                    for j in plan[n % SLOTS]:
                        job(i + 1, j)
                    if n % SLOTS in SPLIT_SLOTS and i + 2 < PAIRS:
                        split(i + 2, SPLIT_SLOTS[n % SLOTS])
            copy_den(act, blocks_done - 1)
            finish_hi(act, blocks_done - 1)

        @block.vector
        def _(dve):
            def split(i, m):
                n = 3 * i + m
                dve.wait_ge(w_hi_ready, n + 1)
                dve.scalar_tensor_tensor(out=w_lo[:, m, :, :], in0=w32[:, n % 2, :, :], scalar=WSCALE,
                                         in1=w_hi[:, m, :, :], op0=ALU.mult, op1=ALU.subtract).then_inc(w_lo_ready, 1)

            def job(i, n):
                kind, *what = jobs[n]
                bank = job_bank(i, n)
                if kind == "qk":
                    m, g = what
                    w = WIDTH[g]
                    cols = slice(g * 512, g * 512 + w)
                    first = (q1, k1)[m]
                    dve.wait_ge(job_act, act_count(i, n))
                    for hd, (a, b) in enumerate(((0, 64), (64, 0))):
                        hi = first[a:a + 64, i % 2, hd, cols]
                        lo = q2[a:a + 64, i % 2, hd, cols] if m == 0 else k1[b:b + 64, i % 2, hd, cols]
                        again = q1[b:b + 64, i % 2, hd, cols] if m == 0 else k2[a:a + 64, i % 2, hd, cols]
                        dve.scalar_tensor_tensor(out=lo, in0=bank[a:a + 64, 0:w], scalar=1 / WSCALE, in1=hi,
                                                 op0=ALU.mult, op1=ALU.subtract)
                        ins = dve.tensor_copy(again, hi)
                elif kind == "v":
                    g = what[1]
                    tiles = slice(4 * g, min(4 * g + 4, NT))
                    dve.wait_ge(job_act, act_count(i, n))
                    ins = dve.scalar_tensor_tensor(
                        out=v_lo[:, i % 2, tiles, :].rearrange("p t n -> p (t n)"), in0=bank[:, 0:WIDTH[g]],
                        scalar=1 / WSCALE, in1=v_hi[:, i % 2, tiles, :].rearrange("p t n -> p (t n)"),
                        op0=ALU.mult, op1=ALU.subtract)
                elif kind == "max":
                    hd, t, g = what
                    dve.wait_ge(job_product, i * JOBS + n + 1)
                    ins = dve.tensor_reduce(maxima[0:rows(t), hd * NT + t, g:g + 1], bank[0:rows(t), 0:BLOCKS[g][1]],
                                            AX.X, ALU.max)
                else:
                    g, = what
                    dve.wait_ge(job_act, act_count(i, n))
                    ins = dve.tensor_copy(q2[0:33, i % 2, 1, g * 512:g * 512 + WIDTH[g]], bank[0:33, 0:WIDTH[g]])
                ins.then_inc(job_dve, 1)
                if n == LAST_MAX:
                    dve.wait_ge(job_dve, i * JOBS + n + 1)
                    dve.tensor_reduce(greatest[:, :, :].rearrange("p h t -> p (h t)"), maxima[:, :, :], AX.X, ALU.max
                                      ).then_inc(maxima_ready, 1)
                    dve.wait_ge(maxima_ready, 5 * i + 1)
                    for hd, b in ((0, 64), (1, 0)):
                        dve.tensor_scalar(stack[:, :, b], greatest[:, hd, :], -1.0, None, ALU.mult
                                          ).then_inc(maxima_ready, 1)
                    dve.wait_ge(maxima_ready, 5 * i + 3)
                    for hd, b in ((0, 64), (1, 0)):
                        dve.scalar_tensor_tensor(out=stack[:, :, b + 32], in0=greatest[:, hd, :], scalar=-1.0,
                                                 in1=stack[:, :, b], op0=ALU.mult, op1=ALU.subtract
                                                 ).then_inc(maxima_ready, 1)

            dve.memset(q2[:, :, :, :], 0.0).then_inc(stacks_zeroed, 1)
            dve.memset(k2[:, :, :, :], 0.0).then_inc(stacks_zeroed, 1)
            for m in range(3):
                split(0, m)
            dve.wait_ge(constants_ready, 1)
            for n in range(JOBS):
                job(0, n)
            for m in range(3):
                split(1, m)
            for n in range(PAIRS * SLOTS):
                i, b, k, at, w, r = slot(n)
                if k == 2 and n > NT:
                    copy_acc(dve, n // NT - 1)
                if n % 2 == 0:
                    split_weights(dve, n)
                if k == 3 and n > NT:
                    finish_value(dve, n // NT - 1)
                if k == 7 and n > NT:
                    finish_lo(dve, n // NT - 1)
                if i + 1 < PAIRS:
                    for j in plan[n % SLOTS]:
                        job(i + 1, j)
                    if n % SLOTS in SPLIT_SLOTS and i + 2 < PAIRS:
                        split(i + 2, SPLIT_SLOTS[n % SLOTS])
            copy_acc(dve, blocks_done - 1)
            finish_value(dve, blocks_done - 1)
            finish_lo(dve, blocks_done - 1)

        @block.tensor
        def _(pe):
            xt_hi, xt_lo = xt

            def job(i, n):
                kind, *what = jobs[n]
                bank = job_bank(i, n)
                if i * JOBS + n >= 2:
                    pe.wait_ge(job_dve, i * JOBS + n - 1)
                if kind == "qk":
                    m, g = what
                    w = WIDTH[g]
                    if g == 0:
                        pe.wait_ge(w_lo_ready, 3 * i + m + 1)
                    for k in range(DC):
                        cols = slice(g * 512, g * 512 + w)
                        ins = pair_product(pe, bank[:, 0:w], w_hi[:, m, k, :], w_lo[:, m, k, :], xt_hi[:, k, cols],
                                           xt_lo[:, k, cols], k == 0, k == DC - 1)
                elif kind == "v":
                    g = what[1]
                    if g == 0:
                        pe.wait_ge(w_lo_ready, 3 * i + 3)
                    for t in range(4 * g, min(4 * g + 4, NT)):
                        for k in range(DC):
                            nodes = slice(t * P, (t + 1) * P)
                            ins = pair_product(pe, bank[:, (t % 4) * P:(t % 4 + 1) * P], xt_hi[:, k, nodes],
                                               xt_lo[:, k, nodes], w_hi[:, 2, k, :], w_lo[:, 2, k, :], k == 0,
                                               k == DC - 1)
                elif kind == "max":
                    hd, t, g = what
                    at, w = BLOCKS[g]
                    if n == QK_JOBS:
                        pe.wait_ge(job_dve, i * JOBS + QK_JOBS)
                    ins = pe.matmul(bank[0:rows(t), 0:w], q1[:, i % 2, hd, t * P:t * P + rows(t)],
                                    k1[:, i % 2, hd, at:at + w], start=True, stop=True)
                else:
                    g, = what
                    pe.wait_ge(maxima_ready, 5 * i + 5)
                    for t in range(4 * g, min(4 * g + 4, NT)):
                        ins = pe.matmul(bank[:, (t % 4) * P:(t % 4 + 1) * P], stack[:, t, :], s.ident16[:, :],
                                        start=True, stop=True)
                ins.then_inc(job_product, 1)

            def scores(n):
                i, b, k, at, w, r = slot(n)
                if n % SLOTS == 0:
                    pe.wait_ge(job_dve, (i + 1) * JOBS)
                if n >= 2:
                    pe.wait_ge(exp_ready, n - 1)
                for hd in range(2):
                    out = s.ps[2 * (n % 2) + hd][0:r, 0:w]
                    keys = slice(k * P, k * P + r)
                    pe.matmul(out, k1[:, i % 2, hd, keys], q1[:, i % 2, hd, at:at + w], start=True, stop=False)
                    ins = pe.matmul(out, k2[:, i % 2, hd, keys], q2[:, i % 2, hd, at:at + w], start=False, stop=True)
                ins.then_inc(scores_ready, 1)

            def values(n):
                i, b, k, at, w, r = slot(n)
                wait_lo(pe, n)
                if k == 0 and n >= NT:
                    pe.wait_ge(acc_copied, n // NT)
                    pe.wait_ge(den_copied, n // NT)
                for v, p, first, last in ((v_hi, p_hi, True, False), (v_hi, p_lo, False, False), (v_lo, p_hi, False, True)):
                    for hd in range(2):
                        dims = slice(hd * HD, (hd + 1) * HD)
                        pe.matmul(ACC[dims, 0:w], v[0:r, i % 2, k, dims], p[0:r, n % RING, hd, 0:w],
                                  start=(first and k == 0), stop=(last and k == NT - 1))
                for p, first in ((p_hi, True), (p_lo, False)):
                    for hd in range(2):
                        dims = slice(hd * HD, (hd + 1) * HD)
                        ins = pe.matmul(DEN[dims, 0:w], s.ones16[0:r, 0:HD], p[0:r, n % RING, hd, 0:w],
                                        start=(first and k == 0), stop=(not first and k == NT - 1))
                ins.then_inc(pv_done, 1)

            for n in range(JOBS):
                job(0, n)
            scores(0)
            for n in range(PAIRS * SLOTS):
                i = n // SLOTS
                if n + 1 < PAIRS * SLOTS:
                    scores(n + 1)
                todo_now = plan[n % SLOTS] if i + 1 < PAIRS else []
                for j in todo_now[0:1]:
                    job(i + 1, j)
                if n >= 2:
                    values(n - 2)
                for j in todo_now[1:]:
                    job(i + 1, j)
            values(PAIRS * SLOTS - 2)
            values(PAIRS * SLOTS - 1)


def project_out(nc, s, xt, w_proj, x2):
    with ExitStack() as scope:
        w32 = sbuf(nc, scope, "o_w32", [P, DC, D], F32)
        w_hi = sbuf(nc, scope, "o_w_hi", [P, DC, D], F16)
        w_lo = sbuf(nc, scope, "o_w_lo", [P, DC, D], F16)
        w_loaded = [semaphore(nc, scope, f"o_w_loaded{i}") for i in range(DC)]
        w_hi_ready = semaphore(nc, scope, "o_w_hi_ready")
        w_lo_ready = semaphore(nc, scope, "o_w_lo_ready")
        summed = semaphore(nc, scope, "o_summed")
        added = semaphore(nc, scope, "o_added")
        block = scope.enter_context(nc.Block())

        @block.sync
        def _(sp):
            for k in range(DC):
                sp.dma_start(w32[:, k, :], w_proj[k * P:(k + 1) * P, :]).then_inc(w_loaded[k], 16)

        @block.scalar
        def _(act):
            for k in range(DC):
                act.wait_ge(w_loaded[k], 16)
                act.activation(w_hi[:, k, :], w32[:, k, :], ACT.Copy, scale=WSCALE).then_inc(w_hi_ready, 1)

        @block.vector
        def _(dve):
            for k in range(DC):
                dve.wait_ge(w_hi_ready, k + 1)
                dve.scalar_tensor_tensor(out=w_lo[:, k, :], in0=w32[:, k, :], scalar=WSCALE, in1=w_hi[:, k, :],
                                         op0=ALU.mult, op1=ALU.subtract).then_inc(w_lo_ready, 1)
            for n in range(2 * NT):
                t, half = divmod(n, 2)
                place = x2[0:rows(t), t, half * DHALF:(half + 1) * DHALF]
                dve.wait_ge(summed, n + 1)
                dve.scalar_tensor_tensor(out=place, in0=s.ps[n % 4][0:rows(t), 0:DHALF], scalar=1 / WSCALE, in1=place,
                                         op0=ALU.mult, op1=ALU.add).then_inc(added, 1)

        @block.tensor
        def _(pe):
            for n in range(2 * NT):
                t, half = divmod(n, 2)
                nodes = slice(t * P, t * P + rows(t))
                cols = slice(half * DHALF, (half + 1) * DHALF)
                if n >= 4:
                    pe.wait_ge(added, n - 3)
                for k in range(DC):
                    if n == 0:
                        pe.wait_ge(w_lo_ready, k + 1)
                    ins = pair_product(pe, s.ps[n % 4][0:rows(t), 0:DHALF], xt[0][:, k, nodes], xt[1][:, k, nodes],
                                       w_hi[:, k, cols], w_lo[:, k, cols], k == 0, k == DC - 1)
                ins.then_inc(summed, 1)


def route(nc, s, xt, w_router, gates, residual, x1_dram):
    with ExitStack() as scope:
        sb = lambda name, shape, dtype: sbuf(nc, scope, f"r_{name}", shape, dtype)
        sem = lambda name: semaphore(nc, scope, f"r_{name}")
        w32 = sb("w32", [P, DC, EXPERTS], F32)
        w_hi = sb("w_hi", [P, DC, EXPERTS], F16)
        w_lo = sb("w_lo", [P, DC, EXPERTS], F16)
        logits = sb("logits", [P, NT, EXPERTS], F32)
        above = sb("above", [P, NT, EXPERTS, EXPERTS], F32)
        equal = sb("equal", [P, NT, EXPERTS, EXPERTS], F32)
        lower = sb("lower", [P, EXPERTS, EXPERTS], F32)
        rank = sb("rank", [P, NT, EXPERTS], F32)
        largest = sb("largest", [P, NT], F32)
        total = sb("total", [P, NT], F32)
        x1 = sb("x1", [P, NT, D], F32)
        loaded = sem("loaded")
        x1_loaded = sem("x1_loaded")
        lower_ready = sem("lower_ready")
        split = sem("split")
        summed = sem("summed")
        dve_step = sem("dve_step")
        shifted = sem("shifted")
        exp_ready = sem("exp_ready")
        block = scope.enter_context(nc.Block())

        @block.sync
        def _(sp):
            with nc.allow_non_contiguous_dma(reason="eight columns"):
                sp.dma_start(w32[:, :, :], w_router.rearrange("(k p) n -> p k n", p=P)).then_inc(loaded, 16)
            load_nodes(sp, x1, x1_dram, x1_loaded)

        @block.gpsimd
        def _(pool):
            pool.memset(lower[:, :, :], 1.0).then_inc(lower_ready, 1)
            pool.wait_ge(lower_ready, 1)
            pool.affine_select(out=lower[:, :, :], in_=lower[:, :, :], compare_op=ALU.is_gt, fill=0.0, base=0,
                               pattern=[[1, EXPERTS], [-1, EXPERTS]], channel_multiplier=0).then_inc(lower_ready, 1)

        @block.vector
        def _(dve):
            steps = [0]

            def link(ins):
                steps[0] += 1
                ins.then_inc(dve_step, 1)
                dve.wait_ge(dve_step, steps[0])

            four = [P, NT, EXPERTS, EXPERTS]
            dve.wait_ge(loaded, 16)
            link(dve.tensor_scalar(w_hi[:, :, :], w32[:, :, :], WSCALE, None, ALU.mult))
            dve.scalar_tensor_tensor(out=w_lo[:, :, :], in0=w32[:, :, :], scalar=WSCALE, in1=w_hi[:, :, :],
                                     op0=ALU.mult, op1=ALU.subtract).then_inc(split, 1)
            dve.wait_ge(summed, 1)
            link(dve.tensor_scalar(logits[:, :, :].rearrange("p t e -> p (t e)"), s.ps[0][:, 0:NT * EXPERTS],
                                   1 / WSCALE, None, ALU.mult))
            mine = logits[:, :, :].unsqueeze(3).to_broadcast(four)
            other = logits[:, :, :].unsqueeze(2).to_broadcast(four)
            dve.tensor_tensor(above[:, :, :, :], other, mine, ALU.is_gt)
            link(dve.tensor_tensor(equal[:, :, :, :], other, mine, ALU.is_equal))
            dve.wait_ge(lower_ready, 2)
            link(dve.tensor_tensor(equal[:, :, :, :], equal[:, :, :, :],
                                   lower[:, :, :].unsqueeze(1).to_broadcast(four), ALU.mult))
            link(dve.tensor_tensor(above[:, :, :, :], above[:, :, :, :], equal[:, :, :, :], ALU.add))
            dve.tensor_reduce(rank[:, :, :], above[:, :, :, :], AX.X, ALU.add)
            link(dve.tensor_reduce(largest[:, :], logits[:, :, :], AX.X, ALU.max))
            dve.tensor_tensor(logits[:, :, :], logits[:, :, :],
                              largest[:, :].unsqueeze(2).to_broadcast([P, NT, EXPERTS]), ALU.subtract
                              ).then_inc(shifted, 1)
            dve.wait_ge(exp_ready, 1)
            link(dve.scalar_tensor_tensor(out=gates[:, :, :], in0=rank[:, :, :], scalar=2.0, in1=gates[:, :, :],
                                          op0=ALU.is_lt, op1=ALU.mult))
            link(dve.tensor_reduce(total[:, :], gates[:, :, :], AX.X, ALU.add))
            link(dve.reciprocal(total[:, :], total[:, :]))
            dve.scalar_tensor_tensor(out=gates[:, :, :], in0=gates[:, :, :], scalar=1 / WSCALE,
                                     in1=total[:, :].unsqueeze(2).to_broadcast([P, NT, EXPERTS]), op0=ALU.mult,
                                     op1=ALU.mult)
            dve.wait_ge(x1_loaded, 32)
            for t in range(NT):
                dve.tensor_tensor(residual[0:rows(t), t, :], residual[0:rows(t), t, :], x1[0:rows(t), t, :], ALU.add)

        @block.scalar
        def _(act):
            act.wait_ge(shifted, 1)
            act.activation(gates[:, :, :], logits[:, :, :], ACT.Exp).then_inc(exp_ready, 1)

        @block.tensor
        def _(pe):
            pe.wait_ge(split, 1)
            for t in range(NT):
                nodes = slice(t * P, (t + 1) * P)
                for k in range(DC):
                    ins = pair_product(pe, s.ps[0][:, t * EXPERTS:(t + 1) * EXPERTS], xt[0][:, k, nodes],
                                       xt[1][:, k, nodes], w_hi[:, k, :], w_lo[:, k, :], k == 0, k == DC - 1)
            ins.then_inc(summed, 1)


def load_expert(eng, a32, b32, w1, w2, e, a_loaded, b_loaded):
    if a_loaded is not None:
        eng.dma_start(a32[:, :, :], w1[e].rearrange("(k p) n -> p k n", p=P)).then_inc(a_loaded, 16)
    if b_loaded is not None:
        eng.dma_start(b32[:, :, :], w2[e].rearrange("(k p) n -> p k n", p=P)).then_inc(b_loaded, 16)


def experts(nc, s, xt, w1, w2, a32, b32, a_loaded, b_loaded, gates, result, out):
    with ExitStack() as scope:
        sb = lambda name, shape, dtype: sbuf(nc, scope, f"x_{name}", shape, dtype)
        sem = lambda name: semaphore(nc, scope, f"x_{name}")
        a_hi, a_lo = sb("a_hi", [P, 2, DC, FF], F16), sb("a_lo", [P, 2, DC, FF], F16)
        b_hi, b_lo = sb("b_hi", [P, 2, FC, D], F16), sb("b_lo", [P, 2, FC, D], F16)
        hidden = sb("hidden", [P, 3, 512], F32)
        h_hi, h_lo = sb("h_hi", [P, 2, FC, NPAD], F16), sb("h_lo", [P, 2, FC, NPAD], F16)
        a_hi_ready, a_lo_ready = sem("a_hi_ready"), sem("a_lo_ready")
        b_hi_ready, b_lo_ready = sem("b_hi_ready"), sem("b_lo_ready")
        up_summed = sem("up_summed")
        gelu_ready = sem("gelu_ready")
        h_hi_ready = sem("h_hi_ready")
        h_lo_ready = sem("h_lo_ready")
        down_summed = sem("down_summed")
        added = sem("added")
        stored = sem("stored")
        UP = FC * len(BLOCKS)
        DOWN = 2 * NT
        ups = [(f, g) for g in range(len(BLOCKS)) for f in range(FC)]
        block = scope.enter_context(nc.Block())

        @block.sync
        def _(sp):
            for e in range(1, EXPERTS):
                sp.wait_ge(a_lo_ready, e)
                load_expert(sp, a32, b32, w1, w2, e, a_loaded, None)
                sp.wait_ge(b_lo_ready, e)
                load_expert(sp, a32, b32, w1, w2, e, None, b_loaded)
            for t in range(NT):
                sp.wait_ge(added, (EXPERTS - 1) * DOWN + 2 * (t + 1))
                sp.dma_start(out[t * P:t * P + rows(t), :], result[0:rows(t), t, :]).then_inc(stored, 16)
            sp.wait_ge(stored, 16 * NT)

        @block.scalar
        def _(act):
            def split(e):
                act.wait_ge(a_loaded, 16 * (e + 1))
                if e >= 2:
                    act.wait_ge(up_summed, UP * (e - 1))
                act.activation(a_hi[:, e % 2, :, :], a32[:, :, :], ACT.Copy, scale=WSCALE).then_inc(a_hi_ready, 1)
                act.wait_ge(b_loaded, 16 * (e + 1))
                if e >= 2:
                    act.wait_ge(down_summed, DOWN * (e - 1))
                act.activation(b_hi[:, e % 2, :, :], b32[:, :, :], ACT.Copy, scale=WSCALE).then_inc(b_hi_ready, 1)

            split(0)
            for e in range(EXPERTS):
                for c, (f, g) in enumerate(ups):
                    n = e * UP + c
                    at, w = BLOCKS[g]
                    act.wait_ge(up_summed, n + 1)
                    if n >= 3:
                        act.wait_ge(h_lo_ready, n - 2)
                    act.activation(hidden[:, n % 3, 0:w], s.ps[n % 4][:, 0:w], ACT.Gelu, scale=1 / WSCALE
                                   ).then_inc(gelu_ready, 1)
                    act.wait_ge(gelu_ready, n + 1)
                    if e >= 2:
                        act.wait_ge(down_summed, DOWN * (e - 1))
                    act.activation(h_hi[:, e % 2, f, at:at + w], hidden[:, n % 3, 0:w], ACT.Copy).then_inc(h_hi_ready, 1)
                if e + 1 < EXPERTS:
                    split(e + 1)

        @block.vector
        def _(dve):
            def split(e):
                dve.wait_ge(a_hi_ready, e + 1)
                dve.scalar_tensor_tensor(out=a_lo[:, e % 2, :, :], in0=a32[:, :, :], scalar=WSCALE,
                                         in1=a_hi[:, e % 2, :, :], op0=ALU.mult, op1=ALU.subtract).then_inc(a_lo_ready, 1)
                dve.wait_ge(b_hi_ready, e + 1)
                dve.scalar_tensor_tensor(out=b_lo[:, e % 2, :, :], in0=b32[:, :, :], scalar=WSCALE,
                                         in1=b_hi[:, e % 2, :, :], op0=ALU.mult, op1=ALU.subtract).then_inc(b_lo_ready, 1)

            def up(e):
                for c, (f, g) in enumerate(ups):
                    n = e * UP + c
                    at, w = BLOCKS[g]
                    dve.wait_ge(h_hi_ready, n + 1)
                    dve.tensor_tensor(h_lo[:, e % 2, f, at:at + w], hidden[:, n % 3, 0:w],
                                      h_hi[:, e % 2, f, at:at + w], ALU.subtract).then_inc(h_lo_ready, 1)

            split(0)
            up(0)
            for e in range(EXPERTS):
                if e + 1 < EXPERTS:
                    split(e + 1)
                for c in range(DOWN):
                    t, half = divmod(c, 2)
                    n = e * DOWN + c
                    r = rows(t)
                    place = result[0:r, t, half * DHALF:(half + 1) * DHALF]
                    dve.wait_ge(down_summed, n + 1)
                    if e >= 1:
                        dve.wait_ge(added, n - DOWN + 1)
                    dve.scalar_tensor_tensor(out=place, in0=s.ps[4 + n % 4][0:r, 0:DHALF],
                                             scalar=gates[0:r, t, e:e + 1], in1=place, op0=ALU.mult, op1=ALU.add
                                             ).then_inc(added, 1)
                if e + 1 < EXPERTS:
                    up(e + 1)

        @block.tensor
        def _(pe):
            for e in range(EXPERTS):
                pe.wait_ge(a_lo_ready, e + 1)
                for c, (f, g) in enumerate(ups):
                    n = e * UP + c
                    at, w = BLOCKS[g]
                    if n >= 4:
                        pe.wait_ge(gelu_ready, n - 3)
                    for k in range(DC):
                        cols = slice(f * P, (f + 1) * P)
                        ins = pair_product(pe, s.ps[n % 4][:, 0:w], a_hi[:, e % 2, k, cols], a_lo[:, e % 2, k, cols],
                                           xt[0][:, k, at:at + w], xt[1][:, k, at:at + w], k == 0, k == DC - 1)
                    ins.then_inc(up_summed, 1)
                pe.wait_ge(b_lo_ready, e + 1)
                for c in range(DOWN):
                    t, half = divmod(c, 2)
                    n = e * DOWN + c
                    r = rows(t)
                    pe.wait_ge(h_lo_ready, e * UP + FC * (t // 4 + 1))
                    if n >= 4:
                        pe.wait_ge(added, n - 3)
                    for f in range(FC):
                        cols = slice(half * DHALF, (half + 1) * DHALF)
                        ins = pair_product(pe, s.ps[4 + n % 4][0:r, 0:DHALF], h_hi[:, e % 2, f, t * P:t * P + r],
                                           h_lo[:, e % 2, f, t * P:t * P + r], b_hi[:, e % 2, f, cols],
                                           b_lo[:, e % 2, f, cols], f == 0, f == FC - 1)
                    ins.then_inc(down_summed, 1)


def ffn(nc, s, a, out):
    x1_dram = nc.dram_tensor("x1_kept", (N, D), F32, kind="Internal").ap()
    with ExitStack() as scope:
        xt = [sbuf(nc, scope, f"fxt_{i}", [P, DC, NPAD], F16) for i in ("hi", "lo")]
        with ExitStack() as inner:
            heads_t = [sbuf(nc, inner, f"heads_{i}", [P, DC, NPAD], F16) for i in ("hi", "lo")]
            with ExitStack() as attention:
                qkv_w32 = sbuf(nc, attention, "qkv_w32", [P, 2, DC, P], F32)
                qkv_loaded = [semaphore(nc, attention, f"qkv_loaded{i}") for i in range(2)]

                def load_first_qkv(sp):
                    for m in range(2):
                        load_qkv(sp, qkv_w32, a["L0_ffn_Wqkv"], 0, m, qkv_loaded[m])

                norm_transpose(nc, s, "n1", s.x1, s.x1, xt, twice=True, gain=a["L0_ffn_ln1_g"],
                               bias=a["L0_ffn_ln1_b"], keep=x1_dram, ahead=load_first_qkv)
                attend(nc, s, xt, a["L0_ffn_Wqkv"], qkv_w32, qkv_loaded, *heads_t)
            project_out(nc, s, heads_t, a["L0_ffn_Wproj"], s.x1)
        a32 = sbuf(nc, scope, "a32", [P, DC, FF], F32)
        b32 = sbuf(nc, scope, "b32", [P, FC, D], F32)
        a_loaded, b_loaded = semaphore(nc, scope, "a_loaded"), semaphore(nc, scope, "b_loaded")
        with ExitStack() as inner:
            normed = sbuf(nc, inner, "normed", [P, NT, D], F32)
            norm_transpose(nc, s, "n2", s.x1, normed, xt, gain=a["L0_ffn_ln2_g"], bias=a["L0_ffn_ln2_b"],
                           ahead=lambda sp: load_expert(sp, a32, b32, a["L0_ffn_W1"], a["L0_ffn_W2"], 0, a_loaded,
                                                        b_loaded))
        gates = sbuf(nc, scope, "gates", [P, NT, EXPERTS], F32)
        route(nc, s, xt, a["L0_ffn_Wrouter"], gates, s.x1, x1_dram)
        experts(nc, s, xt, a["L0_ffn_W1"], a["L0_ffn_W2"], a32, b32, a_loaded, b_loaded, gates, s.x1, out)


def setup(nc, s, scope):
    s.ps = [scope.enter_context(nc.psum_tensor(f"bank{i}", [P, 512], F32)) for i in range(8)]
    s.ident = sbuf(nc, scope, "ident", [P, P], F32)
    s.ident_bf = sbuf(nc, scope, "ident_bf", [P, P], BF16)
    s.ident16 = sbuf(nc, scope, "ident16", [P, P], F16)
    s.ones = sbuf(nc, scope, "ones", [P, P], F32)
    s.ones16 = sbuf(nc, scope, "ones16", [P, P], F16)
    s.sel = sbuf(nc, scope, "sel", [8, 8, P], F32)
    s.x1 = sbuf(nc, scope, "x1", [P, NT, D], F32)
    constants(nc, s)


def gnn(nc, s, a):
    hidden_hi = nc.dram_tensor("hidden_hi", (HC, P, N), F16, kind="Internal").ap()
    hidden_lo = nc.dram_tensor("hidden_lo", (HC, P, N), F16, kind="Internal").ap()
    with ExitStack() as scope:
        s.CT = sbuf(nc, scope, "CT", [P, NT, CT_COLS], U16)
        attention = sbuf(nc, scope, "attention", [P, NT, 8], F32)
        source02 = sbuf(nc, scope, "source02", [P, NT, HEADS], F32)
        offsets = sbuf(nc, scope, "offsets", [8, NPAD], F32)
        x_loaded = semaphore(nc, scope, "x_loaded")
        count_edges(nc, s, a["x"], x_loaded)
        w2_32 = sbuf(nc, scope, "w2_32", [P, W2_SLOTS, D], F32)
        w2_loaded = [semaphore(nc, scope, f"w2_loaded{i}") for i in range(W2_SLOTS)]

        def load_first_w2(sp):
            for q in range(W2_SLOTS):
                load_w2(sp, w2_32, a["L0_gnn_W2"], q, w2_loaded[q])

        with ExitStack() as layer:
            h_hi = sbuf(nc, layer, "h_hi", [P, NT, HEADS * HID], F16)
            h_lo = sbuf(nc, layer, "h_lo", [P, NT, HEADS * HID], F16)
            with ExitStack() as inner:
                xt = [sbuf(nc, inner, f"xt_{i}", [P, DC, NPAD], F16) for i in ("hi", "lo")]
                w1_32 = sbuf(nc, inner, "w1_32", [P, DC, HID], F32)
                w1_loaded = semaphore(nc, inner, "w1_loaded")
                norm_transpose(nc, s, "n0", s.x1, s.x1, xt, loaded=x_loaded,
                               ahead=lambda sp: load_head(sp, w1_32, a["L0_gnn_W1"], 0, HID, w1_loaded))
                project_nodes(nc, s, "p1", xt, a["L0_gnn_W1"], w1_32, w1_loaded, a["L0_gnn_att_src1"], a["L0_gnn_att_dst1"], HEADS,
                              h_hi, h_lo, attention)
            edge_maxima(nc, s, "m1", HEADS, attention, source02, offsets)
            aggregate_heads(nc, s, attention, source02, offsets, h_hi, h_lo, a["L0_gnn_b1"], hidden_hi, hidden_lo,
                            load_first_w2)
        h_hi = sbuf(nc, scope, "h2_hi", [P, NT, D + 2], F16)
        h_lo = sbuf(nc, scope, "h2_lo", [P, NT, D + 2], F16)
        project_hidden(nc, s, a["L0_gnn_W2"], w2_32, w2_loaded, a["L0_gnn_att_src2"], a["L0_gnn_att_dst2"], hidden_hi, hidden_lo,
                       h_hi, h_lo, attention)
        offsets_b = sbuf(nc, scope, "offsets_b", [P, 2, NPAD], F32)
        edge_maxima(nc, s, "m2", 1, attention, source02, offsets, offsets_b)
        aggregate_nodes(nc, s, attention, source02, offsets_b, h_hi, h_lo, a["x"], a["L0_gnn_b2"], s.x1)


def program(nc, a, out):
    with ExitStack() as scope:
        s = State()
        State.used.clear()
        setup(nc, s, scope)
        s.src, s.dst = a["src"], a["dst"]
        gnn(nc, s, a)
        clear_semaphores(nc)
        ffn(nc, s, a, out)


_INS = ["x", "src", "dst"] + ["L0_gnn_" + n for n in ("W1", "att_src1", "att_dst1", "b1", "W2", "att_src2",
        "att_dst2", "b2")] + ["L0_ffn_" + n for n in ("Wqkv", "Wproj", "Wrouter", "W1", "W2", "ln1_g", "ln1_b",
        "ln2_g", "ln2_b")]


def kernel(**inputs):
    import concourse.bacc as _bacc
    from concourse.bass_utils import run_bass_kernel_spmd as _run

    nc = _bacc.Bacc("TRN2", target_bir_lowering=False, num_devices=1)
    arrays, args = {}, {}
    for name in _INS:
        arrays[f"in_{name}"] = np.ascontiguousarray(inputs[name])
        args[name] = nc.dram_tensor(f"in_{name}", arrays[f"in_{name}"].shape, DT.from_np(arrays[f"in_{name}"].dtype),
                                    kind="ExternalInput").ap()
    out = nc.dram_tensor("out_0", (N, D), F32, kind="ExternalOutput").ap()
    program(nc, args, out)
    r = _run(nc, [arrays], core_ids=[0])
    return r.results[0]["out_0"]
```

```python
from contextlib import ExitStack

import numpy as np
import concourse.bass as bass
from concourse import mybir

DT = mybir.dt
F32, F16, BF16, I32, U16 = DT.float32, DT.float16, DT.bfloat16, DT.int32, DT.uint16
ALU = mybir.AluOpType
ACT = mybir.ActivationFunctionType
AX = mybir.AxisListType

P = 128
N = 1250
NT = -(-N // P)
NPAD = NT * P
LAST = N - (NT - 1) * P
D = 768
DC = D // P
HID, HEADS = 512, 4
HC = HID * HEADS // P
EDGES = 40000
FF, EXPERTS = 384, 8
FC = FF // P
TOP = 2
SLOT_TILES = (TOP * N + EXPERTS * (P - 1)) // P
ATT_HEADS, HD = 12, 64
PAIRS = ATT_HEADS // 2
EPS = 1e-5
SLOPE = 0.2
WSCALE = 64.0
NO_EDGE = -1e30
WIDE = 2 * -(-N // 6)
BLOCKS = [(0, WIDE), (WIDE, (N - WIDE) // 2), (WIDE + (N - WIDE) // 2, N - WIDE - (N - WIDE) // 2)]
DHALF = D // 2


def rows(t):
    return P if t < NT - 1 else LAST


class State:
    used = []


def sbuf(nc, scope, name, shape, dtype):
    return scope.enter_context(nc.sbuf_tensor(name, shape, dtype))


def semaphore(nc, scope, name):
    sem = scope.enter_context(nc.semaphore(name))
    State.used.append(sem)
    return sem


def pair_product(pe, out, lhs_hi, lhs_lo, rhs_hi, rhs_lo, first, last):
    pe.matmul(out, lhs_hi, rhs_hi, start=first, stop=False)
    pe.matmul(out, lhs_hi, rhs_lo, start=False, stop=False)
    return pe.matmul(out, lhs_lo, rhs_hi, start=False, stop=last)


def load_nodes(eng, tile, dram, sem):
    full = (NT - 1) * P
    eng.dma_start(tile[:, 0:NT - 1, :], dram[0:full, :].rearrange("(t p) d -> p t d", p=P)).then_inc(sem, 16)
    eng.dma_start(tile[0:LAST, NT - 1, :], dram[full:N, :]).then_inc(sem, 16)


def clear_semaphores(nc):
    with nc.Block() as block:

        @block.gpsimd
        def _(pool):
            for sem in State.used:
                pool.sem_clear(sem)
    State.used.clear()


def constants(nc, s):
    with ExitStack() as scope:
        zeroed = semaphore(nc, scope, "c_zeroed")
        ident_done = semaphore(nc, scope, "c_ident_done")
        block = scope.enter_context(nc.Block())

        @block.gpsimd
        def _(pool):
            pool.memset(s.ident[:, :], 0.0).then_inc(zeroed, 1)
            pool.wait_ge(zeroed, 1)
            pool.affine_select(out=s.ident[:, :], in_=s.ident[:, :], compare_op=ALU.not_equal, fill=1.0,
                               base=0, pattern=[[-1, P]], channel_multiplier=1).then_inc(ident_done, 1)

        @block.vector
        def _(dve):
            dve.memset(s.ones[:, :], 1.0)
            dve.memset(s.ones16[:, :], 1.0)
            dve.wait_ge(ident_done, 1)
            dve.tensor_copy(s.ident_bf[:, :], s.ident[:, :])
            dve.tensor_copy(s.ident16[:, :], s.ident[:, :])


def norm_transpose(nc, s, tag, x, out_norm, xt, twice=False, gain=None, bias=None, loaded=None,
                   ahead=None, row_gain=None, row_bias=None, row_pair=None,
                   beside=None, x_stats=None):
    xt_hi, xt_lo = xt
    with ExitStack() as scope:
        sb = lambda name, shape, dtype: sbuf(nc, scope, f"{tag}_{name}", shape, dtype)
        sem = lambda name: semaphore(nc, scope, f"{tag}_{name}")
        stats = sb("stats", [P, NT, 2, 6], F32) if x_stats is None or twice else x_stats
        moments = sb("moments", [P, NT, 2], F32)
        variance = sb("variance", [P, NT], F32)
        deviation = sb("deviation", [P, NT], F32)
        inverse = sb("inverse", [P, NT], F32)
        scratch = sb("scratch", [P, NT, D], F32) if twice else None
        affine = gain is not None
        if affine:
            gb = sb("gain_bias", [P, 2, DC], F32)
            shifted = sb("shifted", [P, 4, 512], F32)
        if row_gain is not None:
            row_gb = sb("row_gain_bias", [P, 2, D], F32)
        row_gb_loaded = sem("row_gb_loaded")
        row_hi_ready = sem("row_hi_ready")
        gb_loaded = sem("gb_loaded")
        dve_step = sem("dve_step")
        variance_ready = sem("variance_ready")
        deviation_ready = sem("deviation_ready")
        normed = sem("normed")
        turned = sem("turned")
        shifted_ready = sem("shifted_ready")
        hi_ready = sem("hi_ready")
        lo_ready = sem("lo_ready")
        groups = [(c, g) for c in range(DC) for g in range(3)]
        width = [512, 512, NPAD - 1024]
        final = scratch if twice else out_norm
        passes = 2 if twice else 1
        block = scope.enter_context(nc.Block())

        @block.sync
        def _(sp):
            if row_gain is not None:
                for i, vector in enumerate((row_gain, row_bias)):
                    sp.dma_start(row_gb[:, i, :], vector.rearrange("(a d) -> a d", a=1).to_broadcast([P, D])
                                 ).then_inc(row_gb_loaded, 16)
            if ahead is not None:
                ahead(sp)
            if affine:
                with nc.allow_non_contiguous_dma(reason="one short vector per partition"):
                    sp.dma_start(gb[:, 0, :], gain.rearrange("(c p) -> p c", p=P)).then_inc(gb_loaded, 16)
                    sp.dma_start(gb[:, 1, :], bias.rearrange("(c p) -> p c", p=P)).then_inc(gb_loaded, 16)

        @block.vector
        def _(dve):
            steps = [0]

            def link(ins):
                steps[0] += 1
                ins.then_inc(dve_step, 1)
                dve.wait_ge(dve_step, steps[0])

            if loaded is not None:
                dve.wait_ge(loaded, 32)
            for n in range(passes):
                src = x if n == 0 else out_norm
                dst = out_norm if n == 0 else scratch
                these = stats if x_stats is None or n > 0 else x_stats
                if these is stats and (x_stats is None or n > 0):
                    for t in range(NT):
                        for half in range(2):
                            ins = dve.bn_stats(stats[:, t, half, :], src[:, t, half * DHALF:(half + 1) * DHALF])
                    link(ins)
                for t in range(NT):
                    ins = dve.bn_aggr(moments[:, t, :], these[:, t, :, :].rearrange("p a b -> p (a b)"))
                link(ins)
                dve.tensor_scalar(variance[:, :], moments[:, :, 1], EPS, None, ALU.add).then_inc(variance_ready, 1)
                dve.wait_ge(deviation_ready, n + 1)
                link(dve.reciprocal(inverse[:, :], deviation[:, :]))
                if row_gain is not None:
                    dve.wait_ge(row_gb_loaded, 32)
                    for t in range(NT):
                        ins = dve.scalar_tensor_tensor(out=dst[:, t, :], in0=src[:, t, :], scalar=moments[:, t, 0:1],
                                                       in1=row_gb[:, 0, :], op0=ALU.subtract, op1=ALU.mult)
                    link(ins)
                for t in range(NT):
                    if row_gain is not None:
                        ins = dve.scalar_tensor_tensor(out=dst[:, t, :], in0=dst[:, t, :], scalar=inverse[:, t:t + 1],
                                                       in1=row_gb[:, 1, :], op0=ALU.mult, op1=ALU.add)
                    else:
                        ins = dve.tensor_scalar(dst[:, t, :], src[:, t, :], moments[:, t, 0:1], inverse[:, t:t + 1],
                                                ALU.subtract, ALU.mult)
                    if n == passes - 1:
                        ins.then_inc(normed, 1)
                if n < passes - 1:
                    link(ins)
            for n, (c, g) in enumerate(groups):
                w = width[g]
                cols = slice(g * 512, g * 512 + w)
                whole = shifted[:, n % 4, 0:w] if affine else s.ps[n % 4][:, 0:w]
                dve.wait_ge(hi_ready, n + 1)
                dve.tensor_tensor(xt_lo[:, c, cols], whole, xt_hi[:, c, cols], ALU.subtract).then_inc(lo_ready, 1)

        @block.scalar
        def _(act):
            for n in range(passes):
                act.wait_ge(variance_ready, n + 1)
                act.activation(deviation[:, :], variance[:, :], ACT.Sqrt).then_inc(deviation_ready, 1)
            if beside is not None:
                beside.scale_split_hi(act, beside.AT_NORM[0])
            if affine:
                act.wait_ge(gb_loaded, 32)
            for n, (c, g) in enumerate(groups):
                w = width[g]
                cols = slice(g * 512, g * 512 + w)
                act.wait_ge(turned, n + 1)
                whole = s.ps[n % 4][:, 0:w]
                if affine:
                    if n >= 4:
                        act.wait_ge(lo_ready, n - 3)
                    act.activation(shifted[:, n % 4, 0:w], whole, ACT.Identity, scale=gb[:, 0, c:c + 1],
                                   bias=gb[:, 1, c:c + 1]).then_inc(shifted_ready, 1)
                    act.wait_ge(shifted_ready, n + 1)
                    whole = shifted[:, n % 4, 0:w]
                act.activation(xt_hi[:, c, cols], whole, ACT.Copy).then_inc(hi_ready, 1)
                if row_pair is not None and n < NT:
                    act.wait_ge(normed, n + 1)
                    act.activation(row_pair[:, n, 0, :], final[:, n, :], ACT.Copy).then_inc(row_hi_ready, 1)
            if beside is not None:
                beside.scale_split_hi(act, beside.AT_NORM[1])

        if row_pair is not None:
            @block.gpsimd
            def _(pool):
                beside.subtract_hi(pool, beside.AT_NORM[0])
                for t in range(NT):
                    pool.wait_ge(row_hi_ready, t + 1)
                    pool.tensor_tensor(row_pair[:, t, 1, :], final[:, t, :], row_pair[:, t, 0, :], ALU.subtract)
                beside.subtract_hi(pool, beside.AT_NORM[1])

        @block.tensor
        def _(pe):
            for n, (c, g) in enumerate(groups):
                pe.wait_ge(normed, min(4 * g + 4, NT))
                if n >= 4:
                    pe.wait_ge(lo_ready, n - 3)
                for t in range(4 * g, min(4 * g + 4, NT)):
                    ins = pe.transpose(s.ps[n % 4][:, (t % 4) * P:(t % 4 + 1) * P],
                                       final[:, t, c * P:(c + 1) * P], s.ident[:, :])
                ins.then_inc(turned, 1)


TILE_E = 125
GROUP = 10
TILES_E = EDGES // TILE_E
GROUPS_E = TILES_E // GROUP
WIN = 48
KEYS = NT * WIN
CT_COLS = NPAD + WIN


def count_edges(nc, s, x, x_loaded):
    POOL_TILES = (1, 3, 4, 6, 8, 9)
    chunks = [(0, P), (P, P), (2 * P, TILES_E - 2 * P)]
    with ExitStack() as scope:
        sb = lambda name, shape, dtype: sbuf(nc, scope, f"e_{name}", shape, dtype)
        sem = lambda name: semaphore(nc, scope, f"e_{name}")
        src_i = sb("src_i", [P, 3, TILE_E], I32)
        dst_i = sb("dst_i", [P, 3, TILE_E], I32)
        part_i = sb("part_i", [P, 2, 3, TILE_E], I32)
        part_f = sb("part_f", [P, 3, 3, TILE_E], F32)
        extent = sb("extent", [P, 6], F32)
        least = sb("least", [1, GROUPS_E], F32)
        greatest = sb("greatest", [1, GROUPS_E], F32)
        span = sb("span", [1, GROUPS_E + 1], F32)
        window_i = sb("window_i", [1, GROUPS_E + 1, 2], I32)
        span_i = sb("span_i", [1, GROUPS_E + 1], I32)
        base = sb("base", [P, GROUPS_E], F32)
        table = sb("table", [P, GROUPS_E, 4, GROUP], F32)
        mine = sb("mine", [P, 4, GROUP], F32)
        test = sb("test", [P, GROUP], F32)
        iota_i = sb("iota_i", [P, KEYS], I32)
        iota = sb("iota", [P, KEYS], F16)
        one_key = sb("one_key", [P, GROUP, KEYS], F16)
        one_src = sb("one_src", [P, GROUP, P], F16)
        loaded = sem("loaded")
        iota_ready = sem("iota_ready")
        pads_zeroed = sem("pads_zeroed")
        zeros = sb("zeros", [P, 2 * D], F16)
        zeros_ready = sem("zeros_ready")
        slots_zeroed = sem("slots_zeroed")
        dve_step = sem("dve_step")
        parts_ready = sem("parts_ready")
        parts_turned = sem("parts_turned")
        extent_ready = sem("extent_ready")
        extent_turned = sem("extent_turned")
        least_ready = sem("least_ready")
        base_turned = sem("base_turned")
        windows_ready = sem("windows_ready")
        group_step = sem("group_step")
        keys_made = sem("keys_made")
        key_onehots = sem("key_onehots")
        src_onehots = sem("src_onehots")
        first_used = sem("first_used")
        first_summed = sem("first_summed")
        first_added = sem("first_added")
        visit_step = sem("visit_step")
        onehots_ready = sem("onehots_ready")
        slots_used = sem("slots_used")
        piece_added = sem("piece_added")
        block = scope.enter_context(nc.Block())

        def first_banks(g):
            return (s.ps[6], s.ps[7]) if g % 2 == 0 else (s.ps[1], s.ps[5])

        @block.sync
        def _(sp):
            for dst_tile, dram in ((src_i, s.src), (dst_i, s.dst)):
                sp.dma_start(dst_tile[:, 0:2, :], dram[0:2 * P * TILE_E].rearrange("(a p e) -> p a e", a=2, e=TILE_E)
                             ).then_inc(loaded, 16)
                sp.dma_start(dst_tile[0:chunks[2][1], 2, :], dram[2 * P * TILE_E:EDGES].rearrange("(p e) -> p e", e=TILE_E)
                             ).then_inc(loaded, 16)
            sp.wait_ge(pads_zeroed, 1)
            load_nodes(sp, s.x1, x, x_loaded)
            sp.wait_ge(zeros_ready, 1)
            sp.dma_start(s.slot_rows.rearrange("(i p) d -> p i d", p=P),
                         zeros[:, :].unsqueeze(1).to_broadcast([P, SLOT_TILES, 2 * D])).then_inc(slots_zeroed, 16)
            sp.wait_ge(slots_zeroed, 16)

        @block.gpsimd
        def _(pool):
            pool.iota(iota_i[:, :], pattern=[[1, KEYS]], base=0, channel_multiplier=0).then_inc(iota_ready, 1)
            pool.memset(zeros[:, :], 0.0).then_inc(zeros_ready, 1)
            pool.wait_ge(keys_made, 1)
            for n in range(TILES_E):
                g, j = divmod(n, GROUP)
                if j not in POOL_TILES:
                    continue
                if n >= GROUP:
                    pool.wait_ge(first_used, n - GROUP + 1)
                pool.tensor_scalar(one_src[0:TILE_E, j, :], iota[0:TILE_E, 0:P], table[0:TILE_E, g, 1, j:j + 1], None,
                                   ALU.is_equal).then_inc(src_onehots, 1)

        @block.vector
        def _(dve):
            steps = [0]

            def link(ins):
                steps[0] += 1
                ins.then_inc(dve_step, 1)
                dve.wait_ge(dve_step, steps[0])

            dve.memset(s.x1[96:P, NT - 1, :], 0.0).then_inc(pads_zeroed, 1)
            dve.memset(s.CT[:, :, :], 0)
            dve.tensor_copy(s.sel[:, :, :], s.ident[0:8, 0:8].unsqueeze(2).to_broadcast([8, 8, P]))
            link(dve.memset(extent[:, :], 0.0))
            dve.wait_ge(iota_ready, 1)
            dve.tensor_copy(iota[:, :], iota_i[:, :])
            dve.wait_ge(loaded, 64)
            for a, (_, k) in enumerate(chunks):
                dve.tensor_scalar(part_i[0:k, 0, a, :], src_i[0:k, a, :], 7, None, ALU.logical_shift_right)
                dve.tensor_scalar(part_i[0:k, 1, a, :], src_i[0:k, a, :], P - 1, None, ALU.bitwise_and)
                ins = dve.tensor_copy(part_f[0:k, 2, a, :], dst_i[0:k, a, :])
            link(ins)
            for a, (_, k) in enumerate(chunks):
                dve.tensor_reduce(extent[0:k, a:a + 1], part_f[0:k, 2, a, :], AX.X, ALU.min)
                ins = dve.tensor_reduce(extent[0:k, 3 + a:4 + a], part_f[0:k, 2, a, :], AX.X, ALU.max)
            ins.then_inc(extent_ready, 1)
            for a, (_, k) in enumerate(chunks):
                dve.tensor_scalar(part_f[0:k, 0, a, :], part_i[0:k, 0, a, :], float(WIN), None, ALU.mult)
                ins = dve.tensor_copy(part_f[0:k, 1, a, :], part_i[0:k, 1, a, :])
            ins.then_inc(parts_ready, 1)
            dve.wait_ge(extent_turned, 1)
            dve.tensor_reduce(least[:, :], s.ps[0][0:1, 0:TILES_E].rearrange("p (g t) -> p g t", t=GROUP), AX.X,
                              ALU.min).then_inc(least_ready, 1)
            link(dve.tensor_reduce(greatest[:, :], s.ps[1][0:1, 0:TILES_E].rearrange("p (g t) -> p g t", t=GROUP),
                                   AX.X, ALU.max))
            link(dve.tensor_tensor(span[:, 0:GROUPS_E], greatest[:, :], least[:, :], ALU.subtract))
            link(dve.tensor_reduce(span[:, GROUPS_E:GROUPS_E + 1], span[:, 0:GROUPS_E], AX.X, ALU.max))
            link(dve.tensor_scalar(span_i[:, :], span[:, :], float(-(-2 ** 16 // WIN)), None, ALU.mult))
            link(dve.tensor_scalar(span_i[:, :], span_i[:, :], 16, None, ALU.logical_shift_right))
            dve.tensor_copy(window_i[:, 0:GROUPS_E, 1], span_i[:, 0:GROUPS_E]).then_inc(windows_ready, 1)
            dve.tensor_scalar(window_i[:, GROUPS_E, 1:2], span_i[:, GROUPS_E:GROUPS_E + 1], 1, None, ALU.min
                              ).then_inc(windows_ready, 1)
            dve.tensor_copy(window_i[:, 0:GROUPS_E, 0], least[:, 0:GROUPS_E]).then_inc(windows_ready, 1)
            dve.wait_ge(base_turned, 1)
            link(dve.tensor_copy(base[:, :], s.ps[0][:, 400:400 + GROUPS_E]))
            dve.wait_ge(parts_turned, 3)
            turned = [s.ps[2 + i][0:TILE_E, 0:TILES_E].rearrange("p (g t) -> p g t", t=GROUP) for i in range(3)]
            dve.tensor_copy(table[0:TILE_E, :, 2, :], turned[0])
            dve.tensor_copy(table[0:TILE_E, :, 1, :], turned[1])
            rel = table[0:TILE_E, :, 3, :]
            key = table[0:TILE_E, :, 0, :]
            link(dve.tensor_tensor(rel, turned[2],
                                   base[0:TILE_E, :].unsqueeze(2).to_broadcast([TILE_E, GROUPS_E, GROUP]),
                                   ALU.subtract))
            link(dve.scalar_tensor_tensor(out=key, in0=table[0:TILE_E, :, 2, :], scalar=1.0, in1=rel,
                                          op0=ALU.add, op1=ALU.add))
            link(dve.scalar_tensor_tensor(out=key, in0=rel, scalar=float(WIN), in1=key, op0=ALU.is_lt, op1=ALU.mult))
            dve.tensor_scalar(key, key, 1.0, None, ALU.subtract).then_inc(keys_made, 1)
            def add_piece(g):
                column = dve.value_load(window_i[0:1, g:g + 1, 0], min_val=0, max_val=N - 1)
                dve.wait_ge(first_summed, g + 1)
                if g >= 1:
                    dve.wait_ge(first_added, 2 * g)
                for half in range(2):
                    piece = s.CT[:, half * NT // 2:(half + 1) * NT // 2, bass.ds(column, WIN)]
                    dve.tensor_tensor(piece, piece, first_banks(g)[half][:, 0:KEYS // 2]
                                      .rearrange("p (c w) -> p c w", w=WIN), ALU.add).then_inc(first_added, 1)

            dve.wait_ge(windows_ready, 3)
            dve.wait_ge(keys_made, 1)
            for g in range(GROUPS_E):
                for j in range(GROUP):
                    n = g * GROUP + j
                    if n >= GROUP:
                        dve.wait_ge(first_used, n - GROUP + 1)
                    dve.tensor_scalar(one_key[0:TILE_E, j, :], iota[0:TILE_E, :], table[0:TILE_E, g, 0, j:j + 1], None,
                                      ALU.is_equal).then_inc(key_onehots, 1)
                    if j not in POOL_TILES:
                        dve.tensor_scalar(one_src[0:TILE_E, j, :], iota[0:TILE_E, 0:P], table[0:TILE_E, g, 1, j:j + 1],
                                          None, ALU.is_equal).then_inc(key_onehots, 1)
                    if j == 3 and g >= 1:
                        add_piece(g - 1)
            add_piece(GROUPS_E - 1)
            dve.wait_ge(first_added, 2 * GROUPS_E)
            dve.wait_ge(first_used, TILES_E)
            dve.wait_ge(src_onehots, GROUPS_E * len(POOL_TILES))
            dve.memset(test[:, 0:1], 0.0).then_inc(piece_added, 1)
            dve.memset(test[:, 1:2], 0.0).then_inc(slots_used, GROUP)
            dve.memset(test[:, 2:3], 0.0).then_inc(visit_step, 1)
            dve.memset(test[:, 4:5], 0.0).then_inc(group_step, 1)
            STEPS = 7
            ones_column = s.ones[:, 0:1]
            E_ = TILE_E
            more = dve.value_load(window_i[0:1, GROUPS_E:GROUPS_E + 1, 1], min_val=0, max_val=1)
            with dve.If(more > 0):
                visit = dve.alloc_register("e_dve_visit")
                window_start = dve.alloc_register("e_window_start")
                dve.reg_mov(visit, 0)
                with dve.Fori(0, GROUPS_E) as g:
                    first = dve.value_load(window_i[0:1, bass.ds(g, 1), 0], min_val=0, max_val=N - 1)
                    windows = dve.value_load(window_i[0:1, bass.ds(g, 1), 1], min_val=0, max_val=N // WIN)
                    dve.wait_ge(visit_step, dve.snap(visit) * STEPS + 1)
                    dve.wait_ge(group_step, g + 1)
                    dve.tensor_copy(mine[0:E_, :, :], table[0:E_, bass.ds(g, 1), :, :]
                                    .rearrange("p g k t -> p (g k) t")).then_inc(group_step, 1)
                    dve.reg_mov(window_start, first)
                    with dve.If(windows > 0), dve.Fori(0, windows):
                        v = dve.snap(visit)
                        dve.reg_add(window_start, window_start, WIN)
                        dve.wait_ge(group_step, g + 2)
                        dve.wait_ge(visit_step, v * STEPS + 1)
                        rel_m, key_m, high_m = mine[0:E_, 3, :], mine[0:E_, 0, :], mine[0:E_, 2, :]
                        dve.tensor_scalar(rel_m, rel_m, float(WIN), None, ALU.subtract).then_inc(visit_step, 1)
                        dve.wait_ge(visit_step, v * STEPS + 2)
                        dve.scalar_tensor_tensor(out=key_m, in0=high_m, scalar=1.0, in1=rel_m, op0=ALU.add,
                                                 op1=ALU.add).then_inc(visit_step, 1)
                        dve.wait_ge(visit_step, v * STEPS + 3)
                        dve.scalar_tensor_tensor(out=key_m, in0=rel_m, scalar=float(WIN), in1=key_m, op0=ALU.is_lt,
                                                 op1=ALU.mult).then_inc(visit_step, 1)
                        dve.wait_ge(visit_step, v * STEPS + 4)
                        dve.scalar_tensor_tensor(out=key_m, in0=rel_m, scalar=0.0, in1=key_m, op0=ALU.is_ge,
                                                 op1=ALU.mult).then_inc(visit_step, 1)
                        dve.wait_ge(visit_step, v * STEPS + 5)
                        dve.tensor_scalar(key_m, key_m, 1.0, None, ALU.subtract).then_inc(visit_step, 1)
                        dve.wait_ge(visit_step, v * STEPS + 6)
                        for j in range(GROUP):
                            dve.wait_ge(slots_used, v * GROUP + (j + 1))
                            dve.tensor_scalar(one_key[0:E_, j, :], iota[0:E_, :], mine[0:E_, 0, j:j + 1], None,
                                              ALU.is_equal)
                            dve.tensor_scalar(one_src[0:E_, j, :], iota[0:E_, 0:P], mine[0:E_, 1, j:j + 1], None,
                                              ALU.is_equal).then_inc(onehots_ready, 1)
                        dve.wait_ge(slots_used, v * GROUP + 2 * GROUP)
                        column = dve.snap(window_start, min_val=0, max_val=N - 1)
                        for half in range(2):
                            piece = s.CT[:, half * NT // 2:(half + 1) * NT // 2, bass.ds(column, WIN)]
                            dve.tensor_tensor(piece, piece, s.ps[6 + half][:, 0:KEYS // 2]
                                              .rearrange("p (c w) -> p c w", w=WIN), ALU.add).then_inc(visit_step, 1)
                        dve.nop().then_inc(piece_added, 1)
                        dve.reg_add(visit, visit, 1)
                dve.wait_ge(visit_step, dve.snap(visit) * STEPS + 1)
                dve.tensor_scalar(test[:, 3:4], ones_column, 1.0, None, ALU.mult)
            for t in range(NT):
                loop = s.CT[:, t, t * P:t * P + rows(t)]
                ins = dve.tensor_tensor(loop, loop, s.ident[:, 0:rows(t)], ALU.add)
            link(ins)

        @block.tensor
        def _(pe):
            pe.wait_ge(extent_ready, 1)
            for a in range(6):
                ins = pe.transpose(s.ps[a // 3][0:1, (a % 3) * P:(a % 3 + 1) * P], extent[:, a:a + 1], s.ident[:, :])
            ins.then_inc(extent_turned, 1)
            pe.wait_ge(least_ready, 1)
            pe.matmul(s.ps[0][:, 400:400 + GROUPS_E], s.ones[0:1, :], least[0:1, 0:GROUPS_E], start=True,
                      stop=True).then_inc(base_turned, 1)
            pe.wait_ge(parts_ready, 1)
            for i in range(3):
                for a, (at, k) in enumerate(chunks):
                    ins = pe.transpose(s.ps[2 + i][0:TILE_E, at:at + k], part_f[0:k, i, a, :], s.ident[0:k, 0:k])
                ins.then_inc(parts_turned, 1)
            for g in range(GROUPS_E):
                if g >= 2:
                    pe.wait_ge(first_added, 2 * (g - 1))
                for j in range(GROUP):
                    mine_too = sum(i <= j for i in POOL_TILES)
                    pe.wait_ge(key_onehots, g * (2 * GROUP - len(POOL_TILES)) + 2 * (j + 1) - mine_too)
                    if j in POOL_TILES:
                        pe.wait_ge(src_onehots, g * len(POOL_TILES) + mine_too)
                    for half in range(2):
                        ins = pe.matmul(first_banks(g)[half][:, 0:KEYS // 2], one_src[0:TILE_E, j, :],
                                        one_key[0:TILE_E, j, half * KEYS // 2:(half + 1) * KEYS // 2],
                                        start=(j == 0), stop=(j == GROUP - 1))
                    ins.then_inc(first_used, 1)
                pe.wait_ge(first_used, (g + 1) * GROUP)
                pe.nop().then_inc(first_summed, 1)
            pe.wait_ge(windows_ready, 3)
            more = pe.value_load(window_i[0:1, GROUPS_E:GROUPS_E + 1, 1], min_val=0, max_val=1)
            with pe.If(more > 0):
                visit = pe.alloc_register("e_pe_visit")
                pe.reg_mov(visit, 0)
                with pe.Fori(0, GROUPS_E) as g:
                    windows = pe.value_load(window_i[0:1, bass.ds(g, 1), 1], min_val=0, max_val=N // WIN)
                    with pe.If(windows > 0), pe.Fori(0, windows):
                        v = pe.snap(visit)
                        pe.wait_ge(piece_added, v + 1)
                        for j in range(GROUP):
                            pe.wait_ge(onehots_ready, v * GROUP + (j + 1))
                            for half in range(2):
                                ins = pe.matmul(s.ps[6 + half][:, 0:KEYS // 2], one_src[0:TILE_E, j, :],
                                                one_key[0:TILE_E, j, half * KEYS // 2:(half + 1) * KEYS // 2],
                                                start=(j == 0), stop=(j == GROUP - 1))
                            ins.then_inc(slots_used, 1)
                        pe.reg_add(visit, visit, 1)


def load_head(eng, w32, weights, j, cols, sem):
    eng.dma_start(w32[:, :, :], weights[:, j * cols:(j + 1) * cols].rearrange("(k p) n -> p k n", p=P)
                  ).then_inc(sem, 16)


def project_nodes(nc, s, tag, xt, weights, w32, w_loaded, att_src, att_dst, heads, h_hi, h_lo, attention, load_xt=None):
    cols = weights.shape[1] // heads
    kc = weights.shape[0] // P
    xt_hi, xt_lo = xt
    with ExitStack() as scope:
        sb = lambda name, shape, dtype: sbuf(nc, scope, f"{tag}_{name}", shape, dtype)
        sem = lambda name: semaphore(nc, scope, f"{tag}_{name}")
        split_w = s.x1[:, :, :].rearrange("p t d -> p (t d)").bitcast(F16)[:, 0:4 * kc * cols].rearrange(
            "p (i a k n) -> p i a k n", i=2, a=2, k=kc)
        w_hi, w_lo = split_w[:, 0], split_w[:, 1]
        att = sb("att", [P, 2, 2, cols], F32)
        product = s.x1[:, :, :].rearrange("p t d -> p (t d)")[:, 2 * kc * cols:2 * (kc + 1) * cols].rearrange(
            "p (i n) -> p i n", i=2)
        att_loaded = [sem(f"att_loaded{i}") for i in range(2)]
        w_hi_ready = sem("w_hi_ready")
        w_lo_ready = sem("w_lo_ready")
        summed = sem("summed")
        hi_ready = sem("hi_ready")
        lo_ready = sem("lo_ready")
        block = scope.enter_context(nc.Block())

        @block.sync
        def _(sp):
            for j in range(heads):
                if j >= 1:
                    sp.wait_ge(w_lo_ready, j)
                    load_head(sp, w32, weights, j, cols, w_loaded)
                if j >= 2:
                    sp.wait_ge(lo_ready, NT * (j - 1))
                for i, vector in enumerate((att_src, att_dst)):
                    sp.dma_start(att[:, j % 2, i, :], vector[j:j + 1, :].to_broadcast([P, cols])
                                 ).then_inc(att_loaded[j % 2], 16)

        @block.scalar
        def _(act):
            def split(j):
                act.wait_ge(w_loaded, 16 * (j + 1))
                if j >= 2:
                    act.wait_ge(summed, NT * (j - 1))
                act.activation(w_hi[:, j % 2, :, :], w32[:, :, :], ACT.Copy, scale=WSCALE).then_inc(w_hi_ready, 1)

            split(0)
            for j in range(heads):
                if j + 1 < heads:
                    act.wait_ge(w_lo_ready, j + 1)
                    split(j + 1)
                for t in range(NT):
                    n = j * NT + t
                    act.wait_ge(summed, n + 1)
                    act.activation(h_hi[:, t, j * cols:(j + 1) * cols], s.ps[n % 4][:, 0:cols], ACT.Copy,
                                   scale=1 / WSCALE).then_inc(hi_ready, 1)

        @block.vector
        def _(dve):
            def split(j):
                dve.wait_ge(w_hi_ready, j + 1)
                dve.scalar_tensor_tensor(out=w_lo[:, j % 2, :, :], in0=w32[:, :, :], scalar=WSCALE,
                                         in1=w_hi[:, j % 2, :, :], op0=ALU.mult, op1=ALU.subtract
                                         ).then_inc(w_lo_ready, 1)

            split(0)
            for j in range(heads):
                if j + 1 < heads:
                    split(j + 1)
                dve.wait_ge(att_loaded[j % 2], 32 * (j // 2 + 1))
                for t in range(NT):
                    n = j * NT + t
                    dve.wait_ge(hi_ready, n + 1)
                    for i in range(2):
                        if n >= 1:
                            dve.wait_ge(lo_ready, n)
                        dve.tensor_tensor_reduce(out=product[:, i, :], in0=s.ps[n % 4][:, 0:cols],
                                                 in1=att[:, j % 2, i, :], scale=1 / WSCALE, scalar=0.0, op0=ALU.mult,
                                                 op1=ALU.add, accum_out=attention[:, t, i * heads + j:i * heads + j + 1])
                    dve.scalar_tensor_tensor(out=h_lo[:, t, j * cols:(j + 1) * cols], in0=s.ps[n % 4][:, 0:cols],
                                             scalar=1 / WSCALE, in1=h_hi[:, t, j * cols:(j + 1) * cols],
                                             op0=ALU.mult, op1=ALU.subtract).then_inc(lo_ready, 1)

        @block.tensor
        def _(pe):
            for j in range(heads):
                pe.wait_ge(w_lo_ready, j + 1)
                for t in range(NT):
                    n = j * NT + t
                    if n >= 4:
                        pe.wait_ge(lo_ready, n - 3)
                    for k in range(kc):
                        ins = pair_product(pe, s.ps[n % 4][:, 0:cols], xt_hi[:, k, t * P:(t + 1) * P],
                                           xt_lo[:, k, t * P:(t + 1) * P], w_hi[:, j % 2, k, :],
                                           w_lo[:, j % 2, k, :], k == 0, k == kc - 1)
                    ins.then_inc(summed, 1)


def edge_maxima(nc, s, tag, heads, attention, source02, offsets, offsets_b=None):
    with ExitStack() as scope:
        sb = lambda name, shape, dtype: sbuf(nc, scope, f"{tag}_{name}", shape, dtype)
        sem = lambda name: semaphore(nc, scope, f"{tag}_{name}")
        mask_t = sb("mask_t", [P, NT, N], BF16)
        mask = sb("mask", [P, 2, NPAD], BF16)
        att_rows = sb("att_rows", [8, NPAD], F32)
        att_b = s.x1[:, :, :].rearrange("p t d -> p (t d)")[:, 0:heads * NPAD].rearrange("p (j n) -> p j n", j=heads)
        shifted = sb("shifted", [P, NPAD], F32)
        greatest = sb("greatest", [P, NT, heads], F32)
        maximum = sb("maximum", [P, NT, heads], F32)
        rest = sb("rest", [P, NT, 8], F32)
        dve_step = sem("dve_step")
        mask_ready = sem("mask_ready")
        rows_turned = sem("rows_turned")
        rows_ready = sem("rows_ready")
        spread = sem("spread")
        spread_copied = sem("spread_copied")
        mask_turned = sem("mask_turned")
        mask_copied = sem("mask_copied")
        tile_done = sem("tile_done")
        rest_ready = sem("rest_ready")
        rest_turned = sem("rest_turned")
        offsets_ready = sem("offsets_ready")
        offsets_spread = sem("offsets_spread")
        width = [512, 512, NPAD - 1024]
        act_masks = heads > 1
        spreads = [(j, g) for j in range(heads) for g in range(3)]
        block = scope.enter_context(nc.Block())

        @block.vector
        def _(dve):
            steps = [0]

            def link(ins):
                steps[0] += 1
                ins.then_inc(dve_step, 1)
                dve.wait_ge(dve_step, steps[0])

            def make_mask(t):
                cols = slice(t * P, min((t + 2) * P, N))
                dve.tensor_scalar(mask_t[:, :, cols], s.CT[:, :, cols], 0.0, None, ALU.is_equal
                                  ).then_inc(mask_ready, 1)

            if not act_masks:
                make_mask(0)
            dve.memset(greatest[:, :, :], 0.0)
            dve.memset(rest[:, :, :], 0.0)
            link(dve.tensor_scalar(source02[:, :, 0:heads], attention[:, :, 0:heads], SLOPE, None, ALU.mult))
            for t in range(NT):
                if not act_masks and t % 2 == 0 and t + 2 < NT:
                    make_mask(t + 2)
                dve.wait_ge(mask_copied, t + 1)
                for j in range(heads):
                    r = rows(t)
                    dve.wait_ge(spread_copied, 3 * (j + 1))
                    ins = dve.tensor_tensor_reduce(out=shifted[0:r, :], in0=mask[0:r, t % 2, :], in1=att_b[0:r, j, :],
                                                   scale=1.0, scalar=NO_EDGE * 2, op0=ALU.add, op1=ALU.max,
                                                   accum_out=greatest[0:r, t, j:j + 1])
                    link(ins)
                dve.nop().then_inc(tile_done, 1)
            dest = attention[:, :, heads:2 * heads]
            link(dve.tensor_tensor(maximum[:, :, :], greatest[:, :, :], dest, ALU.add))
            link(dve.scalar_tensor_tensor(out=maximum[:, :, :], in0=maximum[:, :, :], scalar=SLOPE,
                                          in1=maximum[:, :, :], op0=ALU.mult, op1=ALU.max))
            pairs = rest[:, :, :].rearrange("p t (j i) -> p t j i", i=2)
            dve.tensor_tensor(pairs[:, :, 0:heads, 0], dest, maximum[:, :, :], ALU.subtract)
            dve.scalar_tensor_tensor(out=pairs[:, :, 0:heads, 1], in0=dest, scalar=SLOPE, in1=maximum[:, :, :],
                                     op0=ALU.mult, op1=ALU.subtract).then_inc(rest_ready, 1)

        @block.tensor
        def _(pe):
            k = 2 * heads
            for t in range(NT):
                ins = pe.transpose(s.ps[t // 4][0:k, (t % 4) * P:(t % 4 + 1) * P], attention[:, t, 0:k], s.ident[:, :])
            ins.then_inc(rows_turned, 1)
            pe.wait_ge(rows_ready, 1)


            def spread_rows(first, last):
                for n in range(first, last):
                    j, g = spreads[n]
                    if n >= 2:
                        pe.wait_ge(spread_copied, n - 1)
                    pe.matmul(s.ps[3 + n % 2][:, 0:width[g]], s.sel[0:k, j, :],
                              att_rows[0:k, g * 512:g * 512 + width[g]], start=True, stop=True).then_inc(spread, 1)

            spread_rows(0, 3)
            for t in range(NT):
                if t == 1:
                    spread_rows(3, len(spreads))
                pe.wait_ge(mask_ready, t // 2 + 1)
                if t >= 2:
                    pe.wait_ge(mask_copied, t - 1)
                lead, tail = mask_banks(s, t)
                for c in range(NT):
                    out = lead[0:rows(t), c * P:(c + 1) * P] if c < 8 else tail[0:rows(t), (c - 8) * P:(c - 7) * P]
                    ins = pe.transpose(out, mask_t[:, c, t * P:t * P + rows(t)], s.ident_bf[:, :])
                ins.then_inc(mask_turned, 1)
            pe.wait_ge(rest_ready, 1)
            for t in range(NT):
                ins = pe.transpose(s.ps[1 + t // 4][0:8, (t % 4) * P:(t % 4 + 1) * P], rest[:, t, :], s.ident[:, :])
            ins.then_inc(rest_turned, 1)
            if offsets_b is not None:
                pe.wait_ge(offsets_ready, 1)
                for i in range(2):
                    for g in range(3):
                        ins = pe.matmul(s.ps[[0, 1, 2, 5, 6, 7][3 * i + g]][:, 0:width[g]], s.sel[:, i, :],
                                        offsets[:, g * 512:g * 512 + width[g]], start=True, stop=True)
                ins.then_inc(offsets_spread, 1)

        @block.scalar
        def _(act):
            k = 2 * heads

            def make_mask(t):
                cols = slice(t * P, min((t + 2) * P, N))
                act.activation(mask_t[:, :, cols], s.CT[:, :, cols], ACT.Relu, scale=-1.0, bias=s.ones[:, 0:1]
                               ).then_inc(mask_ready, 1)

            if act_masks:
                make_mask(0)
            act.wait_ge(rows_turned, 1)
            for g in range(3):
                ins = act.activation(att_rows[0:k, g * 512:g * 512 + width[g]], s.ps[g][0:k, 0:width[g]], ACT.Copy)
            ins.then_inc(rows_ready, 1)


            def copy_spread(first, last):
                for n in range(first, last):
                    j, g = spreads[n]
                    act.wait_ge(spread, n + 1)
                    act.activation(att_b[:, j, g * 512:g * 512 + width[g]], s.ps[3 + n % 2][:, 0:width[g]], ACT.Copy
                                   ).then_inc(spread_copied, 1)

            copy_spread(0, 3)
            for t in range(NT):
                if t == 1:
                    copy_spread(3, len(spreads))
                if act_masks and t % 2 == 1 and t + 1 < NT:
                    make_mask(t + 1)
                act.wait_ge(mask_turned, t + 1)
                if t >= 2:
                    act.wait_ge(tile_done, t - 1)
                lead, tail = mask_banks(s, t)
                r = rows(t)
                act.activation(mask[0:r, t % 2, 0:1024], lead[0:r, :], ACT.Copy, scale=NO_EDGE)
                act.activation(mask[0:r, t % 2, 1024:NPAD], tail[0:r, 0:NPAD - 1024], ACT.Copy, scale=NO_EDGE
                               ).then_inc(mask_copied, 1)
            act.wait_ge(rest_turned, 1)
            for g in range(3):
                ins = act.activation(offsets[:, g * 512:g * 512 + width[g]], s.ps[1 + g][0:8, 0:width[g]], ACT.Copy)
            ins.then_inc(offsets_ready, 1)
            if offsets_b is not None:
                act.wait_ge(offsets_spread, 1)
                for i in range(2):
                    for g in range(3):
                        act.activation(offsets_b[:, i, g * 512:g * 512 + width[g]],
                                       s.ps[[0, 1, 2, 5, 6, 7][3 * i + g]][:, 0:width[g]], ACT.Copy)


def mask_banks(s, t):
    lead, tail = ((5, 6), (7, 0))[t % 2]
    return s.ps[lead][:, :].bitcast(BF16), s.ps[tail][:, :].bitcast(BF16)


class EdgeWeights:
    KP = NT // 2
    SLOTS = 4

    def __init__(self, nc, s, scope, tag, units, width, attention, source02, offsets, off_places, in_psum,
                 lo=None):
        self.in_psum = in_psum
        self.s, self.units, self.attention, self.source02 = s, units, attention, source02
        self.offsets, self.off_places = offsets, off_places
        self.steps = len(units) * self.KP
        self.hi = sbuf(nc, scope, f"{tag}_p_hi", [P, 2, NT, width], F16)
        self.lo = sbuf(nc, scope, f"{tag}_p_lo", [P, 2, NT, width], F16) if lo is None else lo
        self.work = sbuf(nc, scope, f"{tag}_work", [P, self.SLOTS, 2, width], F32)
        self.offsets_spread = semaphore(nc, scope, f"{tag}_offsets_spread")
        self.upper_ready = semaphore(nc, scope, f"{tag}_upper_ready")
        self.score_ready = semaphore(nc, scope, f"{tag}_score_ready")
        self.exp_ready = semaphore(nc, scope, f"{tag}_exp_ready")
        self.weight_ready = semaphore(nc, scope, f"{tag}_weight_ready")
        self.hi_ready = semaphore(nc, scope, f"{tag}_hi_ready")
        self.lo_ready = semaphore(nc, scope, f"{tag}_lo_ready")

    def place(self, n):
        u, q = divmod(n, self.KP)
        j, (at, w) = self.units[u]
        return u, 2 * q, j, at, w, self.work[:, n % self.SLOTS, :, 0:w]

    def spread(self, pe, u):
        j, (at, w) = self.units[u]
        if u >= 2:
            pe.wait_ge(self.score_ready, NT * (u - 1))
        for i in range(2):
            ins = pe.matmul(self.off_places(u)[i], self.s.sel[:, 2 * j + i, :],
                            self.offsets[:, at:at + w], start=True, stop=True)
        ins.then_inc(self.offsets_spread, 1)

    def act_upper(self, act, n):
        u, k, j, at, w, work = self.place(n)
        if k == 0 and self.in_psum:
            act.wait_ge(self.offsets_spread, u + 1)
        if n >= self.SLOTS:
            act.wait_ge(self.lo_ready, n - self.SLOTS + 1)
        for i in range(2):
            act.activation(work[:, i, :], self.off_places(u)[0], ACT.Identity,
                           bias=self.attention[:, k + i, j:j + 1]).then_inc(self.upper_ready, 1)

    def dve_score(self, dve, n):
        u, k, j, at, w, work = self.place(n)
        for i in range(2):
            dve.wait_ge(self.upper_ready, 2 * n + i + 1)
            dve.scalar_tensor_tensor(out=work[:, i, :], in0=self.off_places(u)[1],
                                     scalar=self.source02[:, k + i, j:j + 1], in1=work[:, i, :],
                                     op0=ALU.add, op1=ALU.max).then_inc(self.score_ready, 1)

    def act_exp(self, act, n):
        work = self.place(n)[-1]
        act.wait_ge(self.score_ready, 2 * n + 2)
        act.activation(work, work, ACT.Exp).then_inc(self.exp_ready, 1)

    def dve_weight(self, dve, n):
        u, k, j, at, w, work = self.place(n)
        dve.wait_ge(self.exp_ready, n + 1)
        dve.scalar_tensor_tensor(out=work, in0=work, scalar=1.0, in1=self.s.CT[:, k:k + 2, at:at + w],
                                 op0=ALU.min, op1=ALU.mult).then_inc(self.weight_ready, 1)

    def act_hi(self, act, n, used, per_unit):
        u, k, j, at, w, work = self.place(n)
        act.wait_ge(self.weight_ready, n + 1)
        if u >= 2:
            act.wait_ge(used, per_unit * (u - 1))
        act.activation(self.hi[:, u % 2, k:k + 2, 0:w], work, ACT.Copy).then_inc(self.hi_ready, 1)

    def pool_lo(self, pool, n):
        u, k, j, at, w, work = self.place(n)
        pool.wait_ge(self.hi_ready, n + 1)
        pool.tensor_tensor(self.lo[:, u % 2, k:k + 2, 0:w], work, self.hi[:, u % 2, k:k + 2, 0:w], ALU.subtract
                           ).then_inc(self.lo_ready, 1)


def aggregate_heads(nc, s, attention, source02, offsets, h_hi, h_lo, bias, scratch_hi, scratch_lo, ahead):
    units = [(j, block) for j in range(HEADS) for block in BLOCKS]
    HCC = HID // P
    chunks = len(units) * HCC
    with ExitStack() as scope:
        sb = lambda name, shape, dtype: sbuf(nc, scope, f"g1_{name}", shape, dtype)
        sem = lambda name: semaphore(nc, scope, f"g1_{name}")

        def off_places(u):
            return [s.ps[2 * (u % 2) + i][:, 0:units[u][1][1]] for i in range(2)]

        DEN, AGG = s.ps[4], (s.ps[5], s.ps[6], s.ps[7])
        spare = s.x1[:, :, :].rearrange("p t d -> p (t d)").bitcast(F16)[:, 0:2 * NT * 512]
        weights = EdgeWeights(nc, s, scope, "g1", units, 512, attention, source02, offsets, off_places,
                              True, lo=spare.rearrange("p (a t w) -> p a t w", a=2, t=NT))
        inverse = sb("inverse", [P, 2, 512], F32)
        value = sb("value", [P, 2, 512], F32)
        expd = s.x1[:, :, :].rearrange("p t d -> p (t d)")[:, NT * 512:(NT + 2) * 512].rearrange("p (a w) -> p a w", a=2)
        out_hi = sb("out_hi", [P, 2, 512], F16)
        out_lo = sb("out_lo", [P, 2, 512], F16)
        b1 = sb("b1", [P, HC], F32)
        b1_loaded = sem("b1_loaded")
        den_summed = sem("den_summed")
        inverse_ready = sem("inverse_ready")
        summed = sem("summed")
        scaled = sem("scaled")
        exp2_ready = sem("exp2_ready")
        relu_ready = sem("relu_ready")
        elu_ready = sem("elu_ready")
        out_hi_ready = sem("out_hi_ready")
        out_lo_ready = sem("out_lo_ready")
        stored = [sem(f"stored{i}") for i in range(2)]
        block = scope.enter_context(nc.Block())

        def width(c):
            return units[c // HCC][1][1]

        due = (3, 4, 6, 7)
        slot_after = {u * EdgeWeights.KP + due[i]: (u - 1) * HCC + i for u in range(1, len(units)) for i in range(HCC)}

        def slots_left(steps):
            return range(sum(n < steps for n in slot_after), chunks + 2)

        @block.sync
        def _(sp):
            ahead(sp)
            with nc.allow_non_contiguous_dma(reason="one short vector per partition"):
                sp.dma_start(b1[:, :], bias.rearrange("(c p) -> p c", p=P)).then_inc(b1_loaded, 16)
            for n in range(chunks):
                (j, (at, w)), c = units[n // HCC], n % HCC
                sp.wait_ge(out_lo_ready, n + 1)
                sp.dma_start(scratch_hi[j * HCC + c, :, at:at + w], out_hi[:, n % 2, 0:w]).then_inc(stored[n % 2], 16)
                sp.dma_start(scratch_lo[j * HCC + c, :, at:at + w], out_lo[:, n % 2, 0:w]).then_inc(stored[n % 2], 16)
            for i in range(2):
                sp.wait_ge(stored[i], 32 * (chunks // 2))

        @block.scalar
        def _(act):
            def finish(slot):
                if 0 <= slot - 1 < chunks:
                    n = slot - 1
                    w = width(n)
                    act.wait_ge(elu_ready, n + 1)
                    if n >= 2:
                        act.wait_ge(stored[n % 2], 32 * (n // 2))
                    act.activation(out_hi[:, n % 2, 0:w], value[:, n % 2, 0:w], ACT.Copy, bias=-1.0
                                   ).then_inc(out_hi_ready, 1)
                if slot < chunks:
                    n = slot
                    w = width(n)
                    col = units[n // HCC][0] * HCC + n % HCC
                    act.wait_ge(scaled, n + 1)
                    act.activation(expd[:, n % 2, 0:w], value[:, n % 2, 0:w], ACT.Exp, bias=b1[:, col:col + 1]
                                   ).then_inc(exp2_ready, 1)
                    act.wait_ge(exp2_ready, n + 1)
                    act.activation(value[:, n % 2, 0:w], value[:, n % 2, 0:w], ACT.Relu, bias=b1[:, col:col + 1]
                                   ).then_inc(relu_ready, 1)

            act.wait_ge(b1_loaded, 16)
            for n in range(weights.steps + 2):
                if n < weights.steps:
                    weights.act_upper(act, n)
                if 0 <= n - 1 < weights.steps:
                    weights.act_exp(act, n - 1)
                if 0 <= n - 2:
                    weights.act_hi(act, n - 2, summed, HCC)
                if n in slot_after:
                    finish(slot_after[n])
            for slot in slots_left(weights.steps + 2):
                finish(slot)

        @block.vector
        def _(dve):
            def finish(slot):
                if 0 <= slot - 2 < chunks:
                    n = slot - 2
                    w = width(n)
                    dve.wait_ge(out_hi_ready, n + 1)
                    dve.scalar_tensor_tensor(out=out_lo[:, n % 2, 0:w], in0=value[:, n % 2, 0:w], scalar=1.0,
                                             in1=out_hi[:, n % 2, 0:w], op0=ALU.subtract, op1=ALU.subtract
                                             ).then_inc(out_lo_ready, 1)
                if 0 <= slot - 1 < chunks:
                    n = slot - 1
                    w = width(n)
                    dve.wait_ge(relu_ready, n + 1)
                    dve.scalar_tensor_tensor(out=value[:, n % 2, 0:w], in0=expd[:, n % 2, 0:w], scalar=1.0,
                                             in1=value[:, n % 2, 0:w], op0=ALU.min, op1=ALU.add).then_inc(elu_ready, 1)
                if slot < chunks:
                    n = slot
                    w = width(n)
                    u = n // HCC
                    if n % HCC == 0:
                        dve.wait_ge(den_summed, u + 1)
                        dve.reciprocal(inverse[:, u % 2, 0:w], DEN[:, 0:w]).then_inc(inverse_ready, 1)
                        dve.wait_ge(inverse_ready, u + 1)
                    dve.wait_ge(summed, n + 1)
                    if n >= 2:
                        dve.wait_ge(out_lo_ready, n - 1)
                    dve.tensor_tensor(value[:, n % 2, 0:w], AGG[n % 3][:, 0:w], inverse[:, u % 2, 0:w],
                                      ALU.mult).then_inc(scaled, 1)

            for n in range(weights.steps + 1):
                if n < weights.steps:
                    weights.dve_score(dve, n)
                if n >= 1:
                    weights.dve_weight(dve, n - 1)
                if n in slot_after:
                    finish(slot_after[n])
            for slot in slots_left(weights.steps + 1):
                finish(slot)

        @block.gpsimd
        def _(pool):
            for n in range(weights.steps):
                weights.pool_lo(pool, n)

        @block.tensor
        def _(pe):
            weights.spread(pe, 0)
            weights.spread(pe, 1)
            for u, (j, (at, w)) in enumerate(units):
                pe.wait_ge(weights.lo_ready, EdgeWeights.KP * (u + 1))
                if u + 2 < len(units):
                    weights.spread(pe, u + 2)
                p_hi, p_lo = weights.hi[:, u % 2, :, 0:w], weights.lo[:, u % 2, :, 0:w]
                if u >= 1:
                    pe.wait_ge(inverse_ready, u)
                for k in range(NT):
                    pe.matmul(DEN[:, 0:w], s.ones16[:, :], p_hi[:, k, :], start=(k == 0), stop=False)
                    ins = pe.matmul(DEN[:, 0:w], s.ones16[:, :], p_lo[:, k, :], start=False, stop=(k == NT - 1))
                ins.then_inc(den_summed, 1)
                for c in range(HCC):
                    n = u * HCC + c
                    if n >= 3:
                        pe.wait_ge(scaled, n - 2)
                    cols = slice((j * HCC + c) * P, (j * HCC + c + 1) * P)
                    for k in range(NT):
                        ins = pair_product(pe, AGG[n % 3][:, 0:w], h_hi[:, k, cols], h_lo[:, k, cols],
                                           p_hi[:, k, :], p_lo[:, k, :], k == 0, k == NT - 1)
                    ins.then_inc(summed, 1)


W2_SLOTS = 3


def load_w2(eng, w32, weights, q, sem):
    eng.dma_start(w32[:, q % W2_SLOTS, :], weights[q * P:(q + 1) * P, :]).then_inc(sem, 16)


def project_hidden(nc, s, weights, w32, w_loaded, att_src, att_dst, scratch_hi, scratch_lo, h_hi, h_lo, attention):
    with ExitStack() as scope:
        sb = lambda name, shape, dtype: sbuf(nc, scope, f"p2_{name}", shape, dtype)
        sem = lambda name: semaphore(nc, scope, f"p2_{name}")
        w_hi = sb("w_hi", [P, HC, D], F16)
        w_lo = sb("w_lo", [P, HC, D], F16)
        x_hi = sb("x_hi", [P, 2, HC, 256], F16)
        x_lo = sb("x_lo", [P, 2, HC, 256], F16)
        att = sb("att", [P, 2, D], F32)
        product = sb("product", [P, 2, DHALF], F32)
        halves = sb("halves", [P, NT, 2, 2], F32)
        x_loaded = [sem(f"x_loaded{i}") for i in range(2)]
        att_loaded = sem("att_loaded")
        w_hi_ready = sem("w_hi_ready")
        w_lo_ready = sem("w_lo_ready")
        summed = sem("summed")
        hi_ready = sem("hi_ready")
        lo_ready = sem("lo_ready")
        scored = sem("scored")
        EARLY_BANKS = 4
        block = scope.enter_context(nc.Block())
        blocks = [(at, min(256, N - at)) for at in range(0, N, 256)]

        @block.sync
        def _(sp):
            for q in range(W2_SLOTS, HC):
                sp.wait_ge(w_lo_ready, q - W2_SLOTS + 1)
                load_w2(sp, w32, weights, q, w_loaded[q % W2_SLOTS])

        @block.gpsimd
        def _(pool):
            for b, (at, w) in enumerate(blocks):
                if b == 1:
                    for i, vector in enumerate((att_src, att_dst)):
                        pool.dma_start(att[:, i, :], vector[0:1, :].to_broadcast([P, D])).then_inc(att_loaded, 16)
                if b >= 2:
                    pool.wait_ge(summed, 4 * (b - 1))
                for tile, dram in ((x_hi, scratch_hi), (x_lo, scratch_lo)):
                    pool.dma_start(tile[:, b % 2, :, 0:w], dram[:, :, at:at + w].rearrange("c p n -> p c n")
                                   ).then_inc(x_loaded[b % 2], 16)

        @block.scalar
        def _(act):
            for q in range(HC):
                act.wait_ge(w_loaded[q % W2_SLOTS], 16 * (q // W2_SLOTS + 1))
                act.activation(w_hi[:, q, :], w32[:, q % W2_SLOTS, :], ACT.Copy, scale=WSCALE).then_inc(w_hi_ready, 1)
            for n in range(2 * NT):
                t, half = divmod(n, 2)
                r, cols = rows(t), slice(half * DHALF, (half + 1) * DHALF)
                act.wait_ge(summed, n + 1)
                act.activation(h_hi[0:r, t, cols], s.ps[n % 6][0:r, 0:DHALF], ACT.Copy, scale=1 / WSCALE
                               ).then_inc(hi_ready, 1)

        @block.vector
        def _(dve):
            for q in range(HC):
                dve.wait_ge(w_hi_ready, q + 1)
                dve.scalar_tensor_tensor(out=w_lo[:, q, :], in0=w32[:, q % W2_SLOTS, :], scalar=WSCALE,
                                         in1=w_hi[:, q, :], op0=ALU.mult, op1=ALU.subtract).then_inc(w_lo_ready, 1)
            dve.memset(h_hi[:, :, D:D + 2], 0.0)
            dve.memset(h_lo[:, :, D:D + 2], 0.0)
            dve.memset(h_hi[96:P, NT - 1, 0:D], 0.0)
            dve.memset(h_lo[96:P, NT - 1, 0:D], 0.0)
            dve.memset(halves[:, :, :, :], 0.0).then_inc(scored, 1)
            dve.wait_ge(att_loaded, 32)
            dve.wait_ge(scored, 1)
            dve.memset(h_hi[:, :, D:D + 1], 1.0)
            for n in range(2 * NT):
                t, half = divmod(n, 2)
                r, cols = rows(t), slice(half * DHALF, (half + 1) * DHALF)
                dve.wait_ge(hi_ready, n + 1)
                if n >= 1:
                    dve.wait_ge(lo_ready, n)
                for i in range(2):
                    dve.tensor_tensor_reduce(out=product[0:r, i, :], in0=s.ps[n % 6][0:r, 0:DHALF],
                                             in1=att[0:r, i, cols], scale=1 / WSCALE, scalar=0.0, op0=ALU.mult,
                                             op1=ALU.add, accum_out=halves[0:r, t, i, half:half + 1])
                dve.scalar_tensor_tensor(out=h_lo[0:r, t, cols], in0=s.ps[n % 6][0:r, 0:DHALF], scalar=1 / WSCALE,
                                         in1=h_hi[0:r, t, cols], op0=ALU.mult, op1=ALU.subtract).then_inc(lo_ready, 1)
            dve.wait_ge(lo_ready, 2 * NT)
            dve.tensor_tensor(attention[:, :, 0:2], halves[:, :, :, 0], halves[:, :, :, 1], ALU.add)

        @block.tensor
        def _(pe):
            pe.wait_ge(x_loaded[0], 32)
            for k in range(HC):
                pe.wait_ge(w_lo_ready, k + 1)
                for n in range(EARLY_BANKS):
                    t, half = divmod(n, 2)
                    cols = slice(half * DHALF, (half + 1) * DHALF)
                    b, at = t // 2, (t % 2) * P
                    ins = pair_product(pe, s.ps[n][:, 0:DHALF], x_hi[:, b, k, at:at + P], x_lo[:, b, k, at:at + P],
                                       w_hi[:, k, cols], w_lo[:, k, cols], k == 0, k == HC - 1)
                    if k == HC - 1:
                        ins.then_inc(summed, 1)
            for n in range(EARLY_BANKS, 2 * NT):
                t, half = divmod(n, 2)
                r, cols = rows(t), slice(half * DHALF, (half + 1) * DHALF)
                b, at = t // 2, (t % 2) * P
                pe.wait_ge(x_loaded[b % 2], 32 * (b // 2 + 1))
                if n >= 6:
                    pe.wait_ge(lo_ready, n - 5)
                for k in range(HC):
                    ins = pair_product(pe, s.ps[n % 6][0:r, 0:DHALF], x_hi[:, b % 2, k, at:at + r],
                                       x_lo[:, b % 2, k, at:at + r], w_hi[:, k, cols], w_lo[:, k, cols],
                                       k == 0, k == HC - 1)
                ins.then_inc(summed, 1)


def aggregate_nodes(nc, s, attention, source02, offsets_b, h_hi, h_lo, x_dram, bias, x1, x1_stats, x1_dram):
    units = [(0, (at, min(256, N - at))) for at in range(0, N, 256)]
    with ExitStack() as scope:
        sb = lambda name, shape, dtype: sbuf(nc, scope, f"g2_{name}", shape, dtype)
        sem = lambda name: semaphore(nc, scope, f"g2_{name}")

        def off_places(u):
            at, w = units[u][1]
            return [offsets_b[:, i, at:at + w] for i in range(2)]

        weights = EdgeWeights(nc, s, scope, "g2", units, 256, attention, source02, None, off_places, False)
        b2 = sb("b2", [P, D], F32)
        inverse = sb("inverse", [P, NT], F32)
        loaded = sem("loaded")
        pads_zeroed = sem("pads_zeroed")
        based = sem("based")
        summed = sem("summed")
        inverse_ready = sem("inverse_ready")
        added = sem("added")
        kept = sem("kept")
        block = scope.enter_context(nc.Block())

        @block.sync
        def _(sp):
            sp.dma_start(b2[:, :], bias.rearrange("(a d) -> a d", a=1).to_broadcast([P, D])).then_inc(loaded, 16)
            sp.wait_ge(pads_zeroed, 1)
            load_nodes(sp, x1, x_dram, loaded)
            for t in range(NT):
                sp.wait_ge(added, 2 * (t + 1))
                sp.dma_start(x1_dram[t * P:t * P + rows(t), :], x1[0:rows(t), t, :]).then_inc(kept, 16)
            sp.wait_ge(kept, 16 * NT)

        @block.scalar
        def _(act):
            for n in range(weights.steps + 2):
                if n < weights.steps:
                    weights.act_upper(act, n)
                if 0 <= n - 1 < weights.steps:
                    weights.act_exp(act, n - 1)
                if 0 <= n - 2:
                    weights.act_hi(act, n - 2, summed, 2)

        @block.vector
        def _(dve):
            def finish(t):
                r = rows(t)
                lead, tail = s.ps[2 + 2 * (t % 3)], s.ps[3 + 2 * (t % 3)]
                dve.wait_ge(summed, t + 1)
                dve.reciprocal(inverse[0:r, t:t + 1], tail[0:r, DHALF:DHALF + 1]).then_inc(inverse_ready, 1)
                dve.wait_ge(inverse_ready, t + 1)
                for half, bank in ((0, lead), (1, tail)):
                    cols = slice(half * DHALF, (half + 1) * DHALF)
                    dve.scalar_tensor_tensor(out=x1[0:r, t, cols], in0=bank[0:r, 0:DHALF],
                                             scalar=inverse[0:r, t:t + 1], in1=x1[0:r, t, cols], op0=ALU.mult,
                                             op1=ALU.add).then_inc(added, 1)
                for half in range(2):
                    dve.wait_ge(added, 2 * t + half + 1)
                    dve.bn_stats(x1_stats[:, t, half, :], x1[:, t, half * DHALF:(half + 1) * DHALF])

            dve.memset(x1[96:P, NT - 1, :], 0.0).then_inc(pads_zeroed, 1)
            for n in range(weights.steps + 1):
                if n < weights.steps:
                    weights.dve_score(dve, n)
                if n >= 1:
                    weights.dve_weight(dve, n - 1)
                if n == EdgeWeights.KP:
                    dve.wait_ge(loaded, 48)
                    for t in range(NT):
                        dve.tensor_tensor(x1[0:rows(t), t, :], x1[0:rows(t), t, :], b2[0:rows(t), :], ALU.add
                                          ).then_inc(based, 1)
                    dve.wait_ge(based, NT)
                u, q = divmod(n, EdgeWeights.KP)
                if 2 <= u < len(units) and q == 1:
                    finish(2 * u - 3)
                if 1 <= u < len(units) and q == 3:
                    finish(2 * u - 2)
            for t in range(NT - 3, NT):
                finish(t)

        @block.gpsimd
        def _(pool):
            for n in range(weights.steps):
                weights.pool_lo(pool, n)

        @block.tensor
        def _(pe):
            for t in range(NT):
                u, at = t // 2, (t % 2) * P
                r = rows(t)
                if t % 2 == 0:
                    pe.wait_ge(weights.lo_ready, EdgeWeights.KP * (u + 1))
                if t >= 3:
                    pe.wait_ge(added, 2 * (t - 2))
                lead, tail = s.ps[2 + 2 * (t % 3)], s.ps[3 + 2 * (t % 3)]
                for half, bank in ((0, lead), (1, tail)):
                    cols = slice(half * DHALF, (half + 1) * DHALF + half)
                    out = bank[0:r, 0:DHALF + half]
                    for k in range(NT):
                        ins = pair_product(pe, out, weights.hi[:, u % 2, k, at:at + r],
                                           weights.lo[:, u % 2, k, at:at + r], h_hi[:, k, cols], h_lo[:, k, cols],
                                           k == 0, k == NT - 1)
                ins.then_inc(summed, 1)


def load_qkv(eng, w32, w_qkv, i, m, sem):
    eng.dma_start(w32[:, (3 * i + m) % 2, :, :], w_qkv[:, m * D + i * P:m * D + (i + 1) * P]
                  .rearrange("(k p) n -> p k n", p=P)).then_inc(sem, 16)


def attend(nc, s, xt, w_qkv, w32, w_loaded, out_hi, out_lo):
    SLOTS = len(BLOCKS) * NT
    WIDTH = [512, 512, NPAD - 1024]
    scale = float(HD) ** -0.5
    todo = [[("qk", m, g)] for m in range(2) for g in range(3)]
    QK_JOBS = len(todo)
    maxima_jobs = [("max", hd, t, g) for hd in range(2) for t in range(NT) for g in range(3)]
    MAX_SLOTS = SLOTS - QK_JOBS - 4
    V_TILES = 2
    V_AT = (1, 3, 5, 7, 9)
    for n in range(MAX_SLOTS):
        count = -(-len(maxima_jobs) // (MAX_SLOTS - n))
        todo.append([maxima_jobs.pop(0) for _ in range(count)])
        if n in V_AT:
            todo[-1].insert(0, ("v", 2, V_AT.index(n)))
    todo += [[], [("row", 0)], [("row", 1), ("row", 2)], []]
    jobs = [job for slot_jobs in todo for job in slot_jobs]
    JOBS = len(jobs)
    plan = [[jobs.index(job) for job in slot_jobs] for slot_jobs in todo]
    LAST_MAX = max(n for n, job in enumerate(jobs) if job[0] == "max")
    LAST_V = max(n for n, job in enumerate(jobs) if job[0] == "v")
    act_jobs = [n for n, job in enumerate(jobs) if job[0] != "max"]
    SPLIT_SLOTS = {9: 0, 13: 1, 19: 2}
    RING = 4
    with ExitStack() as scope:
        sb = lambda name, shape, dtype: sbuf(nc, scope, f"a_{name}", shape, dtype)
        sem = lambda name: semaphore(nc, scope, f"a_{name}")
        w_hi = sb("w_hi", [P, 3, DC, P], F16)
        w_lo = sb("w_lo", [P, 3, DC, P], F16)
        q1, q2, k1, k2 = (sb(name, [P, 2, 2, NPAD], F16) for name in ("q1", "q2", "k1", "k2"))
        v_hi = sb("v_hi", [P, 2, NT, P], F16)
        v_lo = sb("v_lo", [P, 2, NT, P], F16)
        maxima = sb("maxima", [P, 2 * NT, 3], F32)
        greatest = sb("greatest", [P, 2, NT], F32)
        stack = sb("stack", [P, NT, P], F16)
        work = sb("work", [P, RING, 2, 512], F32)
        p_hi = sb("p_hi", [P, RING, 2, 512], F16)
        p_lo = sb("p_lo", [P, RING, 2, 512], F16)
        inverse = sb("inverse", [P, 512], F32)
        value = sb("value", [P, 2, 512], F32)
        zeroed = sem("zeroed")
        stacks_zeroed = sem("stacks_zeroed")
        constants_ready = sem("constants_ready")
        w_hi_ready = sem("w_hi_ready")
        w_lo_ready = sem("w_lo_ready")
        job_product = sem("job_product")
        job_act = sem("job_act")
        job_dve = sem("job_dve")
        maxima_ready = sem("maxima_ready")
        scores_ready = sem("scores_ready")
        exp_ready = sem("exp_ready")
        hi_ready = sem("hi_ready")
        lo_ready = [sem(f"lo_ready{i}") for i in range(2)]
        pv_done = sem("pv_done")
        den_copied = sem("den_copied")
        acc_copied = sem("acc_copied")
        inverse_ready = sem("inverse_ready")
        value_ready = sem("value_ready")
        out_hi_ready = sem("out_hi_ready")
        out_lo_ready = sem("out_lo_ready")
        ACC, DEN = s.ps[4], s.ps[5]
        blocks_done = PAIRS * len(BLOCKS)
        block = scope.enter_context(nc.Block())

        def slot(n):
            i, r = divmod(n, SLOTS)
            b, k = divmod(r, NT)
            return i, b, k, BLOCKS[b][0], BLOCKS[b][1], rows(k)

        def pools(n):
            i, r = divmod(n, SLOTS)
            if i == PAIRS - 1:
                return n % 2 == 1
            return r % 4 != 0 if QK_JOBS <= r < QK_JOBS + MAX_SLOTS else r % 3 == 2

        def job_bank(i, n):
            return s.ps[6 + (i * JOBS + n) % 2]

        def act_count(i, n):
            return i * len(act_jobs) + sum(m <= n for m in act_jobs)

        def wait_lo(eng, n):
            eng.wait_ge(lo_ready[pools(n)], sum(pools(m) == pools(n) for m in range(n + 1)))

        def split_weights(eng, n):
            i, b, k, at, w, r = slot(n)
            eng.wait_ge(hi_ready, n + 1)
            eng.tensor_tensor(p_lo[0:r, n % RING, :, 0:w], work[0:r, n % RING, :, 0:w], p_hi[0:r, n % RING, :, 0:w],
                              ALU.subtract).then_inc(lo_ready[pools(n)], 1)

        def copy_den(act, nb):
            w = BLOCKS[nb % len(BLOCKS)][1]
            act.wait_ge(pv_done, NT * (nb + 1))
            if nb >= 1:
                act.wait_ge(value_ready, nb)
            act.activation(inverse[:, 0:w], DEN[:, 0:w], ACT.Copy).then_inc(den_copied, 1)

        def copy_acc(dve, nb):
            w = BLOCKS[nb % len(BLOCKS)][1]
            dve.wait_ge(pv_done, NT * (nb + 1))
            if nb >= 2:
                dve.wait_ge(out_lo_ready, nb - 1)
            dve.tensor_copy(value[:, nb % 2, 0:w], ACC[:, 0:w]).then_inc(acc_copied, 1)

        def finish_hi(act, nb):
            i, b = divmod(nb, len(BLOCKS))
            at, w = BLOCKS[b]
            act.wait_ge(value_ready, nb + 1)
            act.activation(out_hi[:, i, at:at + w], value[:, nb % 2, 0:w], ACT.Copy).then_inc(out_hi_ready, 1)

        def finish_value(dve, nb):
            w = BLOCKS[nb % len(BLOCKS)][1]
            dve.wait_ge(den_copied, nb + 1)
            dve.reciprocal(inverse[:, 0:w], inverse[:, 0:w]).then_inc(inverse_ready, 1)
            dve.wait_ge(inverse_ready, nb + 1)
            dve.wait_ge(acc_copied, nb + 1)
            dve.tensor_tensor(value[:, nb % 2, 0:w], value[:, nb % 2, 0:w], inverse[:, 0:w], ALU.mult
                              ).then_inc(value_ready, 1)

        def finish_lo(dve, nb):
            i, b = divmod(nb, len(BLOCKS))
            at, w = BLOCKS[b]
            dve.wait_ge(out_hi_ready, nb + 1)
            dve.tensor_tensor(out_lo[:, i, at:at + w], value[:, nb % 2, 0:w], out_hi[:, i, at:at + w], ALU.subtract
                              ).then_inc(out_lo_ready, 1)

        @block.sync
        def _(sp):
            for n in range(3 * PAIRS):
                i, m = divmod(n, 3)
                if n < 2:
                    continue
                sp.wait_ge(w_lo_ready, n - 1)
                load_qkv(sp, w32, w_qkv, i, m, w_loaded[n % 2])

        @block.gpsimd
        def _(pool):
            pool.memset(stack[:, :, :], 0.0).then_inc(zeroed, 1)
            pool.memset(maxima[:, :, :], 0.0).then_inc(zeroed, 1)
            pool.wait_ge(zeroed, 2)
            pool.wait_ge(stacks_zeroed, 2)
            for hd, b in ((0, 64), (1, 0)):
                pool.memset(k2[b:b + 1, :, hd, :], 1.0)
                ins = pool.memset(k2[b + 32:b + 33, :, hd, :], 1.0)
            ins.then_inc(constants_ready, 1)
            for n in range(PAIRS * SLOTS):
                if pools(n):
                    split_weights(pool, n)

        @block.scalar
        def _(act):
            def split(i, m):
                n = 3 * i + m
                act.wait_ge(w_loaded[n % 2], 16 * (n // 2 + 1))
                if i >= 1:
                    act.wait_ge(job_product, (i - 1) * JOBS + (QK_JOBS if m < 2 else LAST_V + 1))
                act.activation(w_hi[:, m, :, :], w32[:, n % 2, :, :], ACT.Copy, scale=WSCALE).then_inc(w_hi_ready, 1)

            def job(i, n):
                kind, *what = jobs[n]
                if kind == "max":
                    return
                bank = job_bank(i, n)
                act.wait_ge(job_product, i * JOBS + n + 1)
                if kind == "qk":
                    m, g = what
                    first = (q1, k1)[m]
                    w = WIDTH[g]
                    act.activation(first[0:64, i % 2, 0, g * 512:g * 512 + w], bank[0:64, 0:w], ACT.Copy,
                                   scale=1 / WSCALE)
                    ins = act.activation(first[64:P, i % 2, 1, g * 512:g * 512 + w], bank[64:P, 0:w], ACT.Copy,
                                         scale=1 / WSCALE)
                elif kind == "v":
                    g = what[1]
                    tiles = slice(V_TILES * g, V_TILES * (g + 1))
                    ins = act.activation(v_hi[:, i % 2, tiles, :].rearrange("p t n -> p (t n)"), bank[:, 0:V_TILES * P],
                                         ACT.Copy, scale=1 / WSCALE)
                else:
                    g, = what
                    ins = act.activation(q2[64:97, i % 2, 0, g * 512:g * 512 + WIDTH[g]], bank[64:97, 0:WIDTH[g]],
                                         ACT.Copy)
                ins.then_inc(job_act, 1)

            for m in range(3):
                split(0, m)
            act.wait_ge(stacks_zeroed, 2)
            for n in range(JOBS):
                job(0, n)
            for m in range(3):
                split(1, m)
            for n in range(PAIRS * SLOTS):
                i, b, k, at, w, r = slot(n)
                act.wait_ge(scores_ready, n + 1)
                if n >= RING:
                    wait_lo(act, n - RING)
                for hd in range(2):
                    ins = act.activation(work[0:r, n % RING, hd, 0:w], s.ps[2 * (n % 2) + hd][0:r, 0:w], ACT.Exp,
                                         scale=scale)
                ins.then_inc(exp_ready, 1)
                if k == 2 and n > NT:
                    copy_den(act, n // NT - 1)
                act.wait_ge(exp_ready, n + 1)
                if n >= RING:
                    act.wait_ge(pv_done, n - RING + 1)
                act.activation(p_hi[0:r, n % RING, :, 0:w], work[0:r, n % RING, :, 0:w], ACT.Copy).then_inc(hi_ready, 1)
                if k == 5 and n > NT:
                    finish_hi(act, n // NT - 1)
                if i + 1 < PAIRS:
                    for j in plan[n % SLOTS]:
                        job(i + 1, j)
                    if n % SLOTS in SPLIT_SLOTS and i + 2 < PAIRS:
                        split(i + 2, SPLIT_SLOTS[n % SLOTS])
            copy_den(act, blocks_done - 1)
            finish_hi(act, blocks_done - 1)

        @block.vector
        def _(dve):
            def split(i, m):
                n = 3 * i + m
                dve.wait_ge(w_hi_ready, n + 1)
                dve.scalar_tensor_tensor(out=w_lo[:, m, :, :], in0=w32[:, n % 2, :, :], scalar=WSCALE,
                                         in1=w_hi[:, m, :, :], op0=ALU.mult, op1=ALU.subtract).then_inc(w_lo_ready, 1)

            def job(i, n):
                kind, *what = jobs[n]
                bank = job_bank(i, n)
                if kind == "qk":
                    m, g = what
                    w = WIDTH[g]
                    cols = slice(g * 512, g * 512 + w)
                    first = (q1, k1)[m]
                    dve.wait_ge(job_act, act_count(i, n))
                    for hd, (a, b) in enumerate(((0, 64), (64, 0))):
                        hi = first[a:a + 64, i % 2, hd, cols]
                        lo = q2[a:a + 64, i % 2, hd, cols] if m == 0 else k1[b:b + 64, i % 2, hd, cols]
                        again = q1[b:b + 64, i % 2, hd, cols] if m == 0 else k2[a:a + 64, i % 2, hd, cols]
                        dve.scalar_tensor_tensor(out=lo, in0=bank[a:a + 64, 0:w], scalar=1 / WSCALE, in1=hi,
                                                 op0=ALU.mult, op1=ALU.subtract)
                        ins = dve.tensor_copy(again, hi)
                elif kind == "v":
                    g = what[1]
                    tiles = slice(V_TILES * g, V_TILES * (g + 1))
                    dve.wait_ge(job_act, act_count(i, n))
                    ins = dve.scalar_tensor_tensor(
                        out=v_lo[:, i % 2, tiles, :].rearrange("p t n -> p (t n)"), in0=bank[:, 0:V_TILES * P],
                        scalar=1 / WSCALE, in1=v_hi[:, i % 2, tiles, :].rearrange("p t n -> p (t n)"),
                        op0=ALU.mult, op1=ALU.subtract)
                elif kind == "max":
                    hd, t, g = what
                    dve.wait_ge(job_product, i * JOBS + n + 1)
                    ins = dve.tensor_reduce(maxima[0:rows(t), hd * NT + t, g:g + 1], bank[0:rows(t), 0:BLOCKS[g][1]],
                                            AX.X, ALU.max)
                else:
                    g, = what
                    dve.wait_ge(job_act, act_count(i, n))
                    ins = dve.tensor_copy(q2[0:33, i % 2, 1, g * 512:g * 512 + WIDTH[g]], bank[0:33, 0:WIDTH[g]])
                ins.then_inc(job_dve, 1)
                if n == LAST_MAX:
                    dve.wait_ge(job_dve, i * JOBS + n + 1)
                    dve.tensor_reduce(greatest[:, :, :].rearrange("p h t -> p (h t)"), maxima[:, :, :], AX.X, ALU.max
                                      ).then_inc(maxima_ready, 1)
                    dve.wait_ge(maxima_ready, 5 * i + 1)
                    for hd, b in ((0, 64), (1, 0)):
                        dve.tensor_scalar(stack[:, :, b], greatest[:, hd, :], -1.0, None, ALU.mult
                                          ).then_inc(maxima_ready, 1)
                    dve.wait_ge(maxima_ready, 5 * i + 3)
                    for hd, b in ((0, 64), (1, 0)):
                        dve.scalar_tensor_tensor(out=stack[:, :, b + 32], in0=greatest[:, hd, :], scalar=-1.0,
                                                 in1=stack[:, :, b], op0=ALU.mult, op1=ALU.subtract
                                                 ).then_inc(maxima_ready, 1)

            split(0, 0)
            dve.memset(q2[:, :, :, :], 0.0).then_inc(stacks_zeroed, 1)
            split(0, 1)
            dve.memset(k2[:, :, :, :], 0.0).then_inc(stacks_zeroed, 1)
            split(0, 2)
            dve.wait_ge(constants_ready, 1)
            for n in range(JOBS):
                job(0, n)
            for m in range(3):
                split(1, m)
            for n in range(PAIRS * SLOTS):
                i, b, k, at, w, r = slot(n)
                if k == 2 and n > NT:
                    copy_acc(dve, n // NT - 1)
                if not pools(n):
                    split_weights(dve, n)
                if k == 3 and n > NT:
                    finish_value(dve, n // NT - 1)
                if k == 7 and n > NT:
                    finish_lo(dve, n // NT - 1)
                if i + 1 < PAIRS:
                    for j in plan[n % SLOTS]:
                        job(i + 1, j)
                    if n % SLOTS in SPLIT_SLOTS and i + 2 < PAIRS:
                        split(i + 2, SPLIT_SLOTS[n % SLOTS])
            copy_acc(dve, blocks_done - 1)
            finish_value(dve, blocks_done - 1)
            finish_lo(dve, blocks_done - 1)

        @block.tensor
        def _(pe):
            xt_hi, xt_lo = xt

            def job(i, n):
                kind, *what = jobs[n]
                bank = job_bank(i, n)
                if i * JOBS + n >= 2:
                    pe.wait_ge(job_dve, i * JOBS + n - 1)
                if kind == "qk":
                    m, g = what
                    w = WIDTH[g]
                    if g == 0:
                        pe.wait_ge(w_lo_ready, 3 * i + m + 1)
                    for k in range(DC):
                        cols = slice(g * 512, g * 512 + w)
                        ins = pair_product(pe, bank[:, 0:w], w_hi[:, m, k, :], w_lo[:, m, k, :], xt_hi[:, k, cols],
                                           xt_lo[:, k, cols], k == 0, k == DC - 1)
                elif kind == "v":
                    g = what[1]
                    if g == 0:
                        pe.wait_ge(w_lo_ready, 3 * i + 3)
                    for t in range(V_TILES * g, V_TILES * (g + 1)):
                        for k in range(DC):
                            nodes = slice(t * P, (t + 1) * P)
                            ins = pair_product(pe, bank[:, (t % V_TILES) * P:(t % V_TILES + 1) * P], xt_hi[:, k, nodes],
                                               xt_lo[:, k, nodes], w_hi[:, 2, k, :], w_lo[:, 2, k, :], k == 0,
                                               k == DC - 1)
                elif kind == "max":
                    hd, t, g = what
                    at, w = BLOCKS[g]
                    if n == QK_JOBS:
                        pe.wait_ge(job_dve, i * JOBS + QK_JOBS)
                    ins = pe.matmul(bank[0:rows(t), 0:w], q1[:, i % 2, hd, t * P:t * P + rows(t)],
                                    k1[:, i % 2, hd, at:at + w], start=True, stop=True)
                else:
                    g, = what
                    pe.wait_ge(maxima_ready, 5 * i + 5)
                    for t in range(4 * g, min(4 * g + 4, NT)):
                        ins = pe.matmul(bank[:, (t % 4) * P:(t % 4 + 1) * P], stack[:, t, :], s.ident16[:, :],
                                        start=True, stop=True)
                ins.then_inc(job_product, 1)

            def scores(n):
                i, b, k, at, w, r = slot(n)
                if n % SLOTS == 0:
                    pe.wait_ge(job_dve, (i + 1) * JOBS)
                if n >= 2:
                    pe.wait_ge(exp_ready, n - 1)
                for hd in range(2):
                    out = s.ps[2 * (n % 2) + hd][0:r, 0:w]
                    keys = slice(k * P, k * P + r)
                    pe.matmul(out, k1[:, i % 2, hd, keys], q1[:, i % 2, hd, at:at + w], start=True, stop=False)
                    ins = pe.matmul(out, k2[:, i % 2, hd, keys], q2[:, i % 2, hd, at:at + w], start=False, stop=True)
                ins.then_inc(scores_ready, 1)

            def values(n):
                i, b, k, at, w, r = slot(n)
                wait_lo(pe, n)
                if k == 0 and n >= NT:
                    pe.wait_ge(acc_copied, n // NT)
                    pe.wait_ge(den_copied, n // NT)
                for v, p, first, last in ((v_hi, p_hi, True, False), (v_hi, p_lo, False, False), (v_lo, p_hi, False, True)):
                    for hd in range(2):
                        dims = slice(hd * HD, (hd + 1) * HD)
                        pe.matmul(ACC[dims, 0:w], v[0:r, i % 2, k, dims], p[0:r, n % RING, hd, 0:w],
                                  start=(first and k == 0), stop=(last and k == NT - 1))
                for p, first in ((p_hi, True), (p_lo, False)):
                    for hd in range(2):
                        dims = slice(hd * HD, (hd + 1) * HD)
                        ins = pe.matmul(DEN[dims, 0:w], s.ones16[0:r, 0:HD], p[0:r, n % RING, hd, 0:w],
                                        start=(first and k == 0), stop=(not first and k == NT - 1))
                ins.then_inc(pv_done, 1)

            for n in range(JOBS):
                job(0, n)
            scores(0)
            for n in range(PAIRS * SLOTS):
                i = n // SLOTS
                if n + 1 < PAIRS * SLOTS:
                    scores(n + 1)
                todo_now = plan[n % SLOTS] if i + 1 < PAIRS else []
                for j in todo_now[0:2]:
                    job(i + 1, j)
                if n >= 2:
                    values(n - 2)
                for j in todo_now[2:]:
                    job(i + 1, j)
            values(PAIRS * SLOTS - 2)
            values(PAIRS * SLOTS - 1)


def project_out(nc, s, xt, w_proj, x2, x2_stats):
    with ExitStack() as scope:
        w32 = sbuf(nc, scope, "o_w32", [P, DC, D], F32)
        w_hi = sbuf(nc, scope, "o_w_hi", [P, DC, D], F16)
        w_lo = sbuf(nc, scope, "o_w_lo", [P, DC, D], F16)
        w_loaded = [semaphore(nc, scope, f"o_w_loaded{i}") for i in range(DC)]
        w_hi_ready = semaphore(nc, scope, "o_w_hi_ready")
        w_lo_ready = semaphore(nc, scope, "o_w_lo_ready")
        summed = semaphore(nc, scope, "o_summed")
        added = semaphore(nc, scope, "o_added")
        block = scope.enter_context(nc.Block())

        @block.sync
        def _(sp):
            for k in range(DC):
                sp.dma_start(w32[:, k, :], w_proj[k * P:(k + 1) * P, :]).then_inc(w_loaded[k], 16)

        @block.scalar
        def _(act):
            for k in range(DC):
                act.wait_ge(w_loaded[k], 16)
                act.activation(w_hi[:, k, :], w32[:, k, :], ACT.Copy, scale=WSCALE).then_inc(w_hi_ready, 1)

        @block.vector
        def _(dve):
            for k in range(DC):
                dve.wait_ge(w_hi_ready, k + 1)
                dve.scalar_tensor_tensor(out=w_lo[:, k, :], in0=w32[:, k, :], scalar=WSCALE, in1=w_hi[:, k, :],
                                         op0=ALU.mult, op1=ALU.subtract).then_inc(w_lo_ready, 1)
            for n in range(2 * NT):
                t, half = divmod(n, 2)
                place = x2[0:rows(t), t, half * DHALF:(half + 1) * DHALF]
                dve.wait_ge(summed, n + 1)
                dve.scalar_tensor_tensor(out=place, in0=s.ps[n % 4][0:rows(t), 0:DHALF], scalar=1 / WSCALE, in1=place,
                                         op0=ALU.mult, op1=ALU.add).then_inc(added, 1)
                dve.wait_ge(added, n + 1)
                dve.bn_stats(x2_stats[:, t, half, :], x2[:, t, half * DHALF:(half + 1) * DHALF])

        @block.tensor
        def _(pe):
            for n in range(2 * NT):
                t, half = divmod(n, 2)
                nodes = slice(t * P, t * P + rows(t))
                cols = slice(half * DHALF, (half + 1) * DHALF)
                if n >= 4:
                    pe.wait_ge(added, n - 3)
                for k in range(DC):
                    if n == 0:
                        pe.wait_ge(w_lo_ready, k + 1)
                    ins = pair_product(pe, s.ps[n % 4][0:rows(t), 0:DHALF], xt[0][:, k, nodes], xt[1][:, k, nodes],
                                       w_hi[:, k, cols], w_lo[:, k, cols], k == 0, k == DC - 1)
                ins.then_inc(summed, 1)


def load_piece(eng, w32, w1, w2, q, loaded):
    e, j = divmod(q, PIECES)
    tile = w32[:, q % W_SLOTS, :]
    if j < DC // 2:
        eng.dma_start(tile.rearrange("p (k n) -> p k n", k=2),
                      w1[e, 2 * j * P:2 * (j + 1) * P, :].rearrange("(k p) n -> p k n", p=P)
                      ).then_inc(loaded[q % W_SLOTS], 16)
    else:
        f = j - DC // 2
        eng.dma_start(tile, w2[e, f * P:(f + 1) * P, :]).then_inc(loaded[q % W_SLOTS], 16)


PIECES = DC // 2 + FC
W_SLOTS = 3
EARLY = 2
PER_TILE = 3


class ExpertWeights:
    AT_NORM = (range(0, 6), range(6, 9))

    def __init__(self, nc, scope, w1, w2):
        self.w1, self.w2 = w1, w2
        self.arena = sbuf(nc, scope, "arena", [P, EXPERTS, 2, PIECES * D], F16)
        self.w32 = sbuf(nc, scope, "x_w32", [P, W_SLOTS, D], F32)
        self.loaded = [semaphore(nc, scope, f"x_loaded{i}") for i in range(W_SLOTS)]
        self.scaled = semaphore(nc, scope, "x_scaled")
        self.hi_ready = semaphore(nc, scope, "x_hi_ready")
        self.lo_ready = semaphore(nc, scope, "x_lo_ready")

    def space(self, e, count, dtype):
        flat = self.arena[:, e:e + 2, :, :].rearrange("p e i n -> p (e i n)")
        return (flat.bitcast(F32) if dtype == F32 else flat)[:, 0:count]

    def load(self, eng, pieces):
        for q in pieces:
            if q >= W_SLOTS:
                eng.wait_ge(self.lo_ready, q - W_SLOTS + 1)
            load_piece(eng, self.w32, self.w1, self.w2, q, self.loaded)

    def part(self, q, i):
        e, j = divmod(q, PIECES)
        return self.arena[:, e, i, j * D:(j + 1) * D]

    def split_hi(self, act, pieces):
        for q in pieces:
            act.wait_ge(self.loaded[q % W_SLOTS], 16 * (q // W_SLOTS + 1))
            act.activation(self.part(q, 0), self.w32[:, q % W_SLOTS, :], ACT.Copy, scale=WSCALE
                           ).then_inc(self.hi_ready, 1)

    def scale_split_hi(self, act, pieces):
        for q in pieces:
            act.wait_ge(self.loaded[q % W_SLOTS], 16 * (q // W_SLOTS + 1))
            act.activation(self.w32[:, q % W_SLOTS, :], self.w32[:, q % W_SLOTS, :], ACT.Copy, scale=WSCALE
                           ).then_inc(self.scaled, 1)
            act.wait_ge(self.scaled, q + 1)
            act.activation(self.part(q, 0), self.w32[:, q % W_SLOTS, :], ACT.Copy).then_inc(self.hi_ready, 1)

    def subtract_hi(self, pool, pieces):
        for q in pieces:
            pool.wait_ge(self.hi_ready, q + 1)
            pool.tensor_tensor(self.part(q, 1), self.w32[:, q % W_SLOTS, :], self.part(q, 0), ALU.subtract
                               ).then_inc(self.lo_ready, 1)

    def split_lo(self, dve, pieces):
        for q in pieces:
            dve.wait_ge(self.hi_ready, q + 1)
            dve.scalar_tensor_tensor(out=self.part(q, 1), in0=self.w32[:, q % W_SLOTS, :], scalar=WSCALE,
                                     in1=self.part(q, 0), op0=ALU.mult, op1=ALU.subtract).then_inc(self.lo_ready, 1)


def pieces_of(i):
    first = EARLY * PIECES + i * PER_TILE
    return range(min(first, EXPERTS * PIECES), min(first + PER_TILE, EXPERTS * PIECES))


def route(nc, s, xt, w_router, row_pair, weights, slot_of, gate_of, expert_of):
    with ExitStack() as scope:
        sb = lambda name, shape, dtype: sbuf(nc, scope, f"r_{name}", shape, dtype)
        sem = lambda name: semaphore(nc, scope, f"r_{name}")
        w32 = sb("w32", [P, DC, EXPERTS], F32)
        w_hi = sb("w_hi", [P, DC, EXPERTS], F16)
        w_lo = sb("w_lo", [P, DC, EXPERTS], F16)
        logits = sb("logits", [P, NT, EXPERTS], F32)
        above = sb("above", [P, NT, EXPERTS, EXPERTS], F32)
        equal = sb("equal", [P, NT, EXPERTS, EXPERTS], F32)
        lower = sb("lower", [P, EXPERTS, EXPERTS], F32)
        rank = sb("rank", [P, NT, EXPERTS], F32)
        largest = sb("largest", [P, NT], F32)
        total = sb("total", [P, NT], F32)
        gates = sb("gates", [P, NT, EXPERTS], F32)
        chosen = sb("chosen", [P, NT, EXPERTS], F16)
        slots = sb("slots", [P, NT, EXPERTS], F32)
        of_rank = sb("of_rank", [P, TOP, NT, EXPERTS], F32)
        picked = sb("picked", [P, 2 * TOP, NT, EXPERTS], F32)
        slot_f = sb("slot_f", [P, TOP, NT], F32)
        before = sb("before", [P, P], F16)
        valid = sb("valid", [P, 1], F32)
        tiles_i = sb("tiles_i", [P, EXPERTS], I32)
        tiles = sb("tiles", [P, EXPERTS], F32)
        earlier = sb("earlier", [P, EXPERTS, EXPERTS], F32)
        start = sb("start", [P, EXPERTS], F32)
        end = sb("end", [P, EXPERTS], F32)
        tile_i = sb("tile_i", [1, SLOT_TILES, EXPERTS], I32)
        tile_0 = sb("tile_0", [1, SLOT_TILES], F32)
        tile_f = sb("tile_f", [1, SLOT_TILES, EXPERTS], F32)
        expert_f = sb("expert_f", [1, SLOT_TILES], F32)
        need_f = sb("need_f", [1, SLOT_TILES], F32)
        lack_f = sb("lack_f", [1, SLOT_TILES], F32)
        made_f = sb("made_f", [1, SLOT_TILES], F32)
        most = sb("most", [1, 1], F32)
        loaded = sem("loaded")
        lower_ready = sem("lower_ready")
        split = sem("split")
        summed = sem("summed")
        dve_step = sem("dve_step")
        shifted = sem("shifted")
        exp_ready = sem("exp_ready")
        chosen_ready = sem("chosen_ready")
        counted = sem("counted")
        slots_ready = sem("slots_ready")
        scattered = sem("scattered")
        early = range(weights.AT_NORM[1].stop, EARLY * PIECES)
        block = scope.enter_context(nc.Block())

        @block.sync
        def _(sp):
            with nc.allow_non_contiguous_dma(reason="eight columns"):
                sp.dma_start(w32[:, :, :], w_router.rearrange("(k p) n -> p k n", p=P)).then_inc(loaded, 16)
            weights.load(sp, early)

        @block.gpsimd
        def _(pool):
            pool.memset(lower[:, :, :], 1.0).then_inc(lower_ready, 1)
            pool.memset(before[:, :], 1.0).then_inc(lower_ready, 1)
            pool.memset(valid[:, :], 1.0).then_inc(lower_ready, 1)
            pool.wait_ge(lower_ready, 3)
            pool.affine_select(out=lower[:, :, :], in_=lower[:, :, :], compare_op=ALU.is_gt, fill=0.0, base=0,
                               pattern=[[1, EXPERTS], [-1, EXPERTS]], channel_multiplier=0).then_inc(lower_ready, 1)
            pool.affine_select(out=before[:, :], in_=before[:, :], compare_op=ALU.is_gt, fill=0.0, base=0,
                               pattern=[[1, P]], channel_multiplier=-1).then_inc(lower_ready, 1)
            pool.affine_select(out=valid[:, :], in_=valid[:, :], compare_op=ALU.is_gt, fill=0.0, base=LAST,
                               pattern=[[0, 1]], channel_multiplier=-1).then_inc(lower_ready, 1)
            pool.iota(tile_i[:, :, :], pattern=[[1, SLOT_TILES], [0, EXPERTS]], base=0, channel_multiplier=0
                      ).then_inc(lower_ready, 1)
            pool.wait_ge(slots_ready, 1)
            for t in range(NT):
                for k in range(TOP):
                    pool.indirect_dma_start(
                        out=s.slot_rows, in_=row_pair[0:rows(t), t, :, :].rearrange("p i d -> p (i d)"), in_offset=None,
                        out_offset=bass.IndirectOffsetOnAxis(ap=slot_of[0:rows(t), k, t:t + 1], axis=0)
                    ).then_inc(scattered, 16)
            pool.wait_ge(scattered, 16 * TOP * NT)

        @block.vector
        def _(dve):
            steps = [0]

            def link(ins):
                steps[0] += 1
                ins.then_inc(dve_step, 1)
                dve.wait_ge(dve_step, steps[0])

            four = [P, NT, EXPERTS, EXPERTS]
            dve.wait_ge(loaded, 16)
            link(dve.tensor_scalar(w_hi[:, :, :], w32[:, :, :], WSCALE, None, ALU.mult))
            dve.scalar_tensor_tensor(out=w_lo[:, :, :], in0=w32[:, :, :], scalar=WSCALE, in1=w_hi[:, :, :],
                                     op0=ALU.mult, op1=ALU.subtract).then_inc(split, 1)
            dve.wait_ge(summed, 1)
            link(dve.tensor_scalar(logits[:, :, :].rearrange("p t e -> p (t e)"), s.ps[0][:, 0:NT * EXPERTS],
                                   1 / WSCALE, None, ALU.mult))
            mine = logits[:, :, :].unsqueeze(3).to_broadcast(four)
            other = logits[:, :, :].unsqueeze(2).to_broadcast(four)
            dve.tensor_tensor(above[:, :, :, :], other, mine, ALU.is_gt)
            link(dve.tensor_tensor(equal[:, :, :, :], other, mine, ALU.is_equal))
            dve.wait_ge(lower_ready, 7)
            link(dve.tensor_tensor(equal[:, :, :, :], equal[:, :, :, :],
                                   lower[:, :, :].unsqueeze(1).to_broadcast(four), ALU.mult))
            link(dve.tensor_tensor(above[:, :, :, :], above[:, :, :, :], equal[:, :, :, :], ALU.add))
            link(dve.tensor_reduce(rank[:, :, :], above[:, :, :, :], AX.X, ALU.add))
            link(dve.tensor_scalar(chosen[:, :, :], rank[:, :, :], float(TOP), None, ALU.is_lt))
            dve.tensor_scalar(chosen[:, NT - 1, :], chosen[:, NT - 1, :], valid[:, 0:1], None, ALU.mult
                              ).then_inc(chosen_ready, 1)
            for k in range(TOP):
                dve.tensor_scalar(of_rank[:, k, :, :], rank[:, :, :], float(k), None, ALU.is_equal)
            link(dve.tensor_reduce(largest[:, :], logits[:, :, :], AX.X, ALU.max))
            dve.tensor_tensor(logits[:, :, :], logits[:, :, :],
                              largest[:, :].unsqueeze(2).to_broadcast([P, NT, EXPERTS]), ALU.subtract
                              ).then_inc(shifted, 1)
            dve.wait_ge(counted, 1)
            link(dve.tensor_scalar(tiles_i[:, :], s.ps[1][:, NT * EXPERTS:(NT + 1) * EXPERTS], float(P - 1), None,
                                   ALU.add))
            link(dve.tensor_scalar(tiles_i[:, :], tiles_i[:, :], 7, None, ALU.logical_shift_right))
            link(dve.tensor_copy(tiles[:, :], tiles_i[:, :]))
            link(dve.tensor_tensor(earlier[:, :, :], lower[:, :, :],
                                   tiles[:, :].unsqueeze(1).to_broadcast([P, EXPERTS, EXPERTS]), ALU.mult))
            link(dve.tensor_reduce(start[:, :], earlier[:, :, :], AX.X, ALU.add))
            dve.tensor_tensor(end[:, :], start[:, :], tiles[:, :], ALU.add)
            link(dve.scalar_tensor_tensor(
                out=slots[:, :, :], in0=start[:, :].unsqueeze(1).to_broadcast([P, NT, EXPERTS]), scalar=float(P),
                in1=s.ps[1][:, 0:NT * EXPERTS].rearrange("p (t e) -> p t e", e=EXPERTS), op0=ALU.mult, op1=ALU.add))
            link(dve.tensor_tensor(picked[:, 0:TOP, :, :], of_rank[:, :, :, :],
                                   slots[:, :, :].unsqueeze(1).to_broadcast([P, TOP, NT, EXPERTS]), ALU.mult))
            link(dve.tensor_reduce(slot_f[:, :, :], picked[:, 0:TOP, :, :], AX.X, ALU.add))
            dve.tensor_copy(slot_of[:, :, :], slot_f[:, :, :]).then_inc(slots_ready, 1)
            dve.tensor_copy(tile_0[:, :], tile_i[:, :, 0])
            link(dve.tensor_copy(tile_f[:, :, :], tile_i[:, :, :]))
            link(dve.tensor_tensor(tile_f[:, :, :], end[0:1, :].unsqueeze(1).to_broadcast([1, SLOT_TILES, EXPERTS]),
                                   tile_f[:, :, :], ALU.is_le))
            link(dve.tensor_reduce(expert_f[:, :], tile_f[:, :, :], AX.X, ALU.add))
            link(dve.tensor_scalar(expert_f[:, :], expert_f[:, :], float(EXPERTS - 1), None, ALU.min))
            dve.tensor_copy(expert_of[:, 0:SLOT_TILES, 0], expert_f[:, :])
            dve.tensor_scalar(made_f[:, :], tile_0[:, :], float(PER_TILE), float(EARLY * PIECES + PER_TILE), ALU.mult,
                              ALU.add)
            link(dve.tensor_scalar(need_f[:, :], expert_f[:, :], float(PIECES), float(PIECES), ALU.mult, ALU.add))
            dve.tensor_copy(expert_of[:, 0:SLOT_TILES, 1], need_f[:, :])
            link(dve.tensor_tensor(lack_f[:, :], need_f[:, :], made_f[:, :], ALU.is_gt))
            link(dve.tensor_reduce(most[:, :], lack_f[:, :], AX.X, ALU.max))
            dve.tensor_copy(expert_of[:, SLOT_TILES, 1:2], most[:, :])
            dve.wait_ge(exp_ready, 1)
            link(dve.scalar_tensor_tensor(out=gates[:, :, :], in0=rank[:, :, :], scalar=float(TOP),
                                          in1=gates[:, :, :], op0=ALU.is_lt, op1=ALU.mult))
            link(dve.tensor_reduce(total[:, :], gates[:, :, :], AX.X, ALU.add))
            link(dve.reciprocal(total[:, :], total[:, :]))
            link(dve.scalar_tensor_tensor(out=gates[:, :, :], in0=gates[:, :, :], scalar=1 / WSCALE,
                                          in1=total[:, :].unsqueeze(2).to_broadcast([P, NT, EXPERTS]), op0=ALU.mult,
                                          op1=ALU.mult))
            link(dve.tensor_tensor(picked[:, TOP:2 * TOP, :, :], of_rank[:, :, :, :],
                                   gates[:, :, :].unsqueeze(1).to_broadcast([P, TOP, NT, EXPERTS]), ALU.mult))
            dve.tensor_reduce(gate_of[:, :, :], picked[:, TOP:2 * TOP, :, :], AX.X, ALU.add)
            weights.split_lo(dve, early)

        @block.scalar
        def _(act):
            act.wait_ge(shifted, 1)
            act.activation(gates[:, :, :], logits[:, :, :], ACT.Exp).then_inc(exp_ready, 1)
            weights.split_hi(act, early)

        @block.tensor
        def _(pe):
            pe.wait_ge(split, 1)
            for t in range(NT):
                nodes = slice(t * P, (t + 1) * P)
                for k in range(DC):
                    ins = pair_product(pe, s.ps[0][:, t * EXPERTS:(t + 1) * EXPERTS], xt[0][:, k, nodes],
                                       xt[1][:, k, nodes], w_hi[:, k, :], w_lo[:, k, :], k == 0, k == DC - 1)
            ins.then_inc(summed, 1)
            pe.wait_ge(chosen_ready, 1)
            for t in range(NT + 1):
                out = s.ps[1][:, t * EXPERTS:(t + 1) * EXPERTS]
                for i in range(t):
                    ins = pe.matmul(out, s.ones16[:, :], chosen[:, i, :], start=(i == 0), stop=(i == NT - 1))
                if t < NT:
                    ins = pe.matmul(out, before[:, :], chosen[:, t, :], start=(t == 0), stop=True)
            ins.then_inc(counted, 1)


def experts(nc, s, weights, slot_of, gate_of, expert_of, result, x1_dram, slot_out, out):
    with ExitStack() as scope:
        sb = lambda name, shape, dtype: sbuf(nc, scope, f"x_{name}", shape, dtype)
        sem = lambda name: semaphore(nc, scope, f"x_{name}")
        row = sb("row", [P, 2, 2 * D], F16)
        turned = sb("turned", [P, 2, DC, P], F16)
        hidden = sb("hidden", [P, FF], F32)
        hidden_pair = sb("hidden_pair", [P, 2, FF], F16)
        hidden_t = sb("hidden_t", [P, 2, FC, P], F16)
        y = sb("y", [P, D], F32)
        x1 = sb("x1", [P, D], F32)
        gathered = weights.arena[:, :, :, :].rearrange("p e i n -> p (e i n)").bitcast(F32)[:, 0:NT * TOP * D].rearrange(
            "p (t k d) -> p t k d", t=NT, k=TOP)
        row_loaded = [sem(f"row_loaded{i}") for i in range(2)]
        row_turned = sem("row_turned")
        turned_hi = sem("turned_hi")
        turned_lo = sem("turned_lo")
        up_summed = sem("up_summed")
        gelu_ready = sem("gelu_ready")
        hidden_hi = sem("hidden_hi")
        hidden_lo = sem("hidden_lo")
        hidden_turned = sem("hidden_turned")
        hidden_copied = sem("hidden_copied")
        down_summed = sem("down_summed")
        y_ready = sem("y_ready")
        y_stored = sem("y_stored")
        x1_loaded = sem("x1_loaded")
        x1_added = sem("x1_added")
        rows_gathered = [sem(f"rows_gathered{t}") for t in range(NT)]
        combined = sem("combined")
        stored = sem("stored")
        late = range(EARLY * PIECES, EXPERTS * PIECES)
        LAST_SPLIT = max(i for i in range(SLOT_TILES) if len(pieces_of(i)) > 0)
        X1_FROM = 2
        ROW_HI, ROW_LO, UP, HID, DOWN = s.ps[0], s.ps[1], s.ps[2], s.ps[4], (s.ps[5], s.ps[6])
        block = scope.enter_context(nc.Block())

        @block.sync
        def _(sp):
            def load_rows(i):
                if i >= 2:
                    sp.wait_ge(row_turned, i - 1)
                sp.dma_start(row[:, i % 2, :], s.slot_rows[i * P:(i + 1) * P, :]).then_inc(row_loaded[i % 2], 16)

            def store_y(i):
                sp.wait_ge(y_ready, i + 1)
                sp.dma_start(slot_out[i * P:(i + 1) * P, :], y[:, :]).then_inc(y_stored, 16)

            load_rows(0)
            load_rows(1)
            at_once = sp.value_load(expert_of[0:1, SLOT_TILES:SLOT_TILES + 1, 1], min_val=0, max_val=1)
            with sp.If(at_once > 0):
                weights.load(sp, late)
            with sp.If(at_once < 1):
                weights.load(sp, pieces_of(0))
            for i in range(SLOT_TILES):
                if i + 2 < SLOT_TILES:
                    load_rows(i + 2)
                t = i - X1_FROM
                if 0 <= t < NT:
                    if t >= 1:
                        sp.wait_ge(x1_added, t)
                    sp.dma_start(x1[0:rows(t), :], x1_dram[t * P:t * P + rows(t), :]).then_inc(x1_loaded, 16)
                if i >= 2:
                    store_y(i - 2)
                if len(pieces_of(i + 1)) > 0:
                    with sp.If(at_once < 1):
                        weights.load(sp, pieces_of(i + 1))
            store_y(SLOT_TILES - 2)
            store_y(SLOT_TILES - 1)
            for t in range(NT):
                sp.wait_ge(combined, TOP * (t + 1))
                sp.dma_start(out[t * P:t * P + rows(t), :], result[0:rows(t), t, :]).then_inc(stored, 16)
            sp.wait_ge(stored, 16 * NT)

        @block.gpsimd
        def _(pool):
            pool.wait_ge(y_stored, 16 * SLOT_TILES)
            pool.wait_ge(down_summed, SLOT_TILES)
            for t in range(NT):
                for k in range(TOP):
                    pool.indirect_dma_start(
                        out=gathered[0:rows(t), t, k, :], out_offset=None, in_=slot_out,
                        in_offset=bass.IndirectOffsetOnAxis(ap=slot_of[0:rows(t), k, t:t + 1], axis=0)
                    ).then_inc(rows_gathered[t], 16)

        @block.scalar
        def _(act):
            at_once = act.value_load(expert_of[0:1, SLOT_TILES:SLOT_TILES + 1, 1], min_val=0, max_val=1)
            with act.If(at_once > 0):
                weights.split_hi(act, late)

            def store_y(i):
                act.wait_ge(down_summed, i + 1)
                if i >= 1:
                    act.wait_ge(y_stored, 16 * i)
                for half in range(2):
                    ins = act.activation(y[:, half * DHALF:(half + 1) * DHALF], DOWN[half][:, 0:DHALF], ACT.Copy)
                ins.then_inc(y_ready, 1)

            for i in range(SLOT_TILES):
                act.wait_ge(row_turned, i + 1)
                if i >= 1:
                    act.wait_ge(up_summed, i)
                act.activation(turned[:, 0, :, :].rearrange("p c n -> p (c n)"), ROW_HI[:, :].bitcast(F16)[:, 0:D],
                               ACT.Copy).then_inc(turned_hi, 1)
                if len(pieces_of(i)) > 0:
                    with act.If(at_once < 1):
                        weights.split_hi(act, pieces_of(i))
                if i >= 2:
                    store_y(i - 2)
                act.wait_ge(up_summed, i + 1)
                if i >= 1:
                    act.wait_ge(hidden_lo, i)
                act.activation(hidden[:, :], UP[:, 0:FF], ACT.Gelu, scale=1 / WSCALE).then_inc(gelu_ready, 1)
                act.wait_ge(gelu_ready, i + 1)
                if i >= 1:
                    act.wait_ge(hidden_turned, i)
                act.activation(hidden_pair[:, 0, :], hidden[:, :], ACT.Copy).then_inc(hidden_hi, 1)
            for i in (SLOT_TILES - 2, SLOT_TILES - 1):
                store_y(i)

        @block.vector
        def _(dve):
            at_once = dve.value_load(expert_of[0:1, SLOT_TILES:SLOT_TILES + 1, 1], min_val=0, max_val=1)
            with dve.If(at_once > 0):
                weights.split_lo(dve, late)
            for i in range(SLOT_TILES):
                dve.wait_ge(row_turned, i + 1)
                if i >= 1:
                    dve.wait_ge(up_summed, i)
                dve.tensor_copy(turned[:, 1, :, :].rearrange("p c n -> p (c n)"), ROW_LO[:, :].bitcast(F16)[:, 0:D]
                                ).then_inc(turned_lo, 1)
                if len(pieces_of(i)) > 0:
                    with dve.If(at_once < 1):
                        weights.split_lo(dve, pieces_of(i))
                if i >= 1:
                    dve.wait_ge(hidden_turned, i)
                    if i >= 2:
                        dve.wait_ge(down_summed, i - 1)
                    dve.tensor_copy(hidden_t[:, :, :, :].rearrange("p i f n -> p (i f n)"),
                                    HID[:, :].bitcast(F16)[:, 0:2 * FF]).then_inc(hidden_copied, 1)
                t = i - X1_FROM
                if 0 <= t < NT:
                    dve.wait_ge(x1_loaded, 16 * (t + 1))
                    dve.tensor_tensor(result[0:rows(t), t, :], result[0:rows(t), t, :], x1[0:rows(t), :], ALU.add
                                      ).then_inc(x1_added, 1)
                dve.wait_ge(hidden_hi, i + 1)
                if i >= 1:
                    dve.wait_ge(hidden_turned, i)
                dve.tensor_tensor(hidden_pair[:, 1, :], hidden[:, :], hidden_pair[:, 0, :], ALU.subtract
                                  ).then_inc(hidden_lo, 1)
            dve.wait_ge(hidden_turned, SLOT_TILES)
            dve.wait_ge(down_summed, SLOT_TILES - 1)
            dve.tensor_copy(hidden_t[:, :, :, :].rearrange("p i f n -> p (i f n)"),
                            HID[:, :].bitcast(F16)[:, 0:2 * FF]).then_inc(hidden_copied, 1)
            dve.wait_ge(x1_added, NT)
            for t in range(NT):
                dve.wait_ge(rows_gathered[t], 16 * TOP)
                for k in range(TOP):
                    place = result[0:rows(t), t, :]
                    if k >= 1:
                        dve.wait_ge(combined, TOP * t + k)
                    dve.scalar_tensor_tensor(out=place, in0=gathered[0:rows(t), t, k, :],
                                             scalar=gate_of[0:rows(t), k, t:t + 1], in1=place, op0=ALU.mult,
                                             op1=ALU.add).then_inc(combined, 1)

        @block.tensor
        def _(pe):
            def turn_rows(i):
                pe.wait_ge(row_loaded[i % 2], 16 * (i // 2 + 1))
                if i >= 1:
                    pe.wait_ge(turned_hi, i)
                    pe.wait_ge(turned_lo, i)
                for h, bank in ((0, ROW_HI), (1, ROW_LO)):
                    for c in range(DC):
                        ins = pe.transpose(bank[:, :].bitcast(F16)[:, c * P:(c + 1) * P],
                                           row[:, i % 2, h * D + c * P:h * D + (c + 1) * P], s.ident16[:, :])
                ins.then_inc(row_turned, 1)

            def columns(expert, h, first, width):
                return weights.arena[:, bass.ds(expert, 1), h, first:first + width].rearrange("p e n -> p (e n)")

            def up(i):
                expert = pe.value_load(expert_of[0:1, i:i + 1, 0], min_val=0, max_val=EXPERTS - 1)
                if i <= LAST_SPLIT:
                    pieces = pe.value_load(expert_of[0:1, i:i + 1, 1], min_val=PIECES, max_val=EXPERTS * PIECES)
                    pe.wait_ge(weights.lo_ready, pieces)
                elif i == LAST_SPLIT + 1:
                    pe.wait_ge(weights.lo_ready, EXPERTS * PIECES)
                pe.wait_ge(turned_hi, i + 1)
                pe.wait_ge(turned_lo, i + 1)
                if i >= 1:
                    pe.wait_ge(gelu_ready, i)
                for c in range(DC):
                    ins = pair_product(pe, UP[:, 0:FF], turned[:, 0, c, :], turned[:, 1, c, :],
                                       columns(expert, 0, c * FF, FF), columns(expert, 1, c * FF, FF), c == 0,
                                       c == DC - 1)
                ins.then_inc(up_summed, 1)

            def turn_hidden(i):
                pe.wait_ge(hidden_lo, i + 1)
                if i >= 1:
                    pe.wait_ge(hidden_copied, i)
                for h in range(2):
                    for f in range(FC):
                        ins = pe.transpose(HID[:, :].bitcast(F16)[:, h * FF + f * P:h * FF + (f + 1) * P],
                                           hidden_pair[:, h, f * P:(f + 1) * P], s.ident16[:, :])
                ins.then_inc(hidden_turned, 1)

            def down(i):
                expert = pe.value_load(expert_of[0:1, i:i + 1, 0], min_val=0, max_val=EXPERTS - 1)
                pe.wait_ge(hidden_copied, i + 1)
                if i >= 1:
                    pe.wait_ge(y_ready, i)
                for half in range(2):
                    for f in range(FC):
                        first = DC * FF + f * D + half * DHALF
                        ins = pair_product(pe, DOWN[half][:, 0:DHALF], hidden_t[:, 0, f, :], hidden_t[:, 1, f, :],
                                           columns(expert, 0, first, DHALF), columns(expert, 1, first, DHALF), f == 0,
                                           f == FC - 1)
                ins.then_inc(down_summed, 1)

            turn_rows(0)
            for i in range(SLOT_TILES):
                up(i)
                if i + 1 < SLOT_TILES:
                    turn_rows(i + 1)
                if i >= 1:
                    down(i - 1)
                turn_hidden(i)
            down(SLOT_TILES - 1)


def ffn(nc, s, a, out):
    slot_out = nc.dram_tensor("slot_out", (SLOT_TILES * P, D), F32, kind="Internal").ap()
    with ExitStack() as scope:
        xt = [sbuf(nc, scope, f"fxt_{i}", [P, DC, NPAD], F16) for i in ("hi", "lo")]
        heads_t = [sbuf(nc, scope, f"heads_{i}", [P, DC, NPAD], F16) for i in ("hi", "lo")]
        with ExitStack() as attention:
            qkv_w32 = sbuf(nc, attention, "qkv_w32", [P, 2, DC, P], F32)
            qkv_loaded = [semaphore(nc, attention, f"qkv_loaded{i}") for i in range(2)]

            def load_first_qkv(sp):
                for m in range(2):
                    load_qkv(sp, qkv_w32, a["L0_ffn_Wqkv"], 0, m, qkv_loaded[m])

            norm_transpose(nc, s, "n1", s.x1, s.x1, xt, twice=True, gain=a["L0_ffn_ln1_g"], bias=a["L0_ffn_ln1_b"],
                           ahead=load_first_qkv, x_stats=s.stats)
            attend(nc, s, xt, a["L0_ffn_Wqkv"], qkv_w32, qkv_loaded, *heads_t)
        project_out(nc, s, heads_t, a["L0_ffn_Wproj"], s.x1, s.stats)
    clear_semaphores(nc)
    with ExitStack() as scope:
        slot_of = sbuf(nc, scope, "slot_of", [P, TOP, NT], I32)
        gate_of = sbuf(nc, scope, "gate_of", [P, TOP, NT], F32)
        expert_of = sbuf(nc, scope, "expert_of", [1, SLOT_TILES + 1, 2], I32)
        weights = ExpertWeights(nc, scope, a["L0_ffn_W1"], a["L0_ffn_W2"])
        normed = weights.space(2, NT * D, F32).rearrange("p (t d) -> p t d", t=NT)
        row_pair = weights.space(6, NT * 2 * D, F16).rearrange("p (t i d) -> p t i d", t=NT, i=2)
        both = weights.space(4, 2 * DC * NPAD, F16).rearrange("p (i c n) -> p i c n", i=2, c=DC)
        xt = [both[:, i] for i in range(2)]
        norm_transpose(nc, s, "n2", s.x1, normed, xt, row_gain=a["L0_ffn_ln2_g"], row_bias=a["L0_ffn_ln2_b"],
                       row_pair=row_pair, x_stats=s.stats, beside=weights, ahead=lambda sp: weights.load(sp, range(9)))
        route(nc, s, xt, a["L0_ffn_Wrouter"], row_pair, weights, slot_of, gate_of, expert_of)
        experts(nc, s, weights, slot_of, gate_of, expert_of, s.x1, s.x1_dram, slot_out, out)


def setup(nc, s, scope):
    s.ps = [scope.enter_context(nc.psum_tensor(f"bank{i}", [P, 512], F32)) for i in range(8)]
    s.ident = sbuf(nc, scope, "ident", [P, P], F32)
    s.ident_bf = sbuf(nc, scope, "ident_bf", [P, P], BF16)
    s.ident16 = sbuf(nc, scope, "ident16", [P, P], F16)
    s.ones = sbuf(nc, scope, "ones", [P, P], F32)
    s.ones16 = sbuf(nc, scope, "ones16", [P, P], F16)
    s.x1 = sbuf(nc, scope, "x1", [P, NT, D], F32)
    s.stats = sbuf(nc, scope, "x1_stats", [P, NT, 2, 6], F32)
    constants(nc, s)


def gnn(nc, s, a):
    hidden_hi = nc.dram_tensor("hidden_hi", (HC, P, N), F16, kind="Internal").ap()
    hidden_lo = nc.dram_tensor("hidden_lo", (HC, P, N), F16, kind="Internal").ap()
    with ExitStack() as scope:
        s.CT = sbuf(nc, scope, "CT", [P, NT, CT_COLS], U16)
        s.sel = sbuf(nc, scope, "sel", [8, 8, P], F32)
        attention = sbuf(nc, scope, "attention", [P, NT, 8], F32)
        source02 = sbuf(nc, scope, "source02", [P, NT, HEADS], F32)
        offsets = sbuf(nc, scope, "offsets", [8, NPAD], F32)
        x_loaded = semaphore(nc, scope, "x_loaded")
        count_edges(nc, s, a["x"], x_loaded)
        w2_32 = sbuf(nc, scope, "w2_32", [P, W2_SLOTS, D], F32)
        w2_loaded = [semaphore(nc, scope, f"w2_loaded{i}") for i in range(W2_SLOTS)]

        def load_first_w2(sp):
            for q in range(W2_SLOTS):
                load_w2(sp, w2_32, a["L0_gnn_W2"], q, w2_loaded[q])

        with ExitStack() as layer:
            h_hi = sbuf(nc, layer, "h_hi", [P, NT, HEADS * HID], F16)
            h_lo = sbuf(nc, layer, "h_lo", [P, NT, HEADS * HID], F16)
            with ExitStack() as inner:
                xt = [sbuf(nc, inner, f"xt_{i}", [P, DC, NPAD], F16) for i in ("hi", "lo")]
                w1_32 = sbuf(nc, inner, "w1_32", [P, DC, HID], F32)
                w1_loaded = semaphore(nc, inner, "w1_loaded")
                norm_transpose(nc, s, "n0", s.x1, s.x1, xt, loaded=x_loaded,
                               ahead=lambda sp: load_head(sp, w1_32, a["L0_gnn_W1"], 0, HID, w1_loaded))
                project_nodes(nc, s, "p1", xt, a["L0_gnn_W1"], w1_32, w1_loaded, a["L0_gnn_att_src1"], a["L0_gnn_att_dst1"], HEADS,
                              h_hi, h_lo, attention)
            edge_maxima(nc, s, "m1", HEADS, attention, source02, offsets)
            aggregate_heads(nc, s, attention, source02, offsets, h_hi, h_lo, a["L0_gnn_b1"], hidden_hi, hidden_lo,
                            load_first_w2)
        h_hi = sbuf(nc, scope, "h2_hi", [P, NT, D + 2], F16)
        h_lo = sbuf(nc, scope, "h2_lo", [P, NT, D + 2], F16)
        project_hidden(nc, s, a["L0_gnn_W2"], w2_32, w2_loaded, a["L0_gnn_att_src2"], a["L0_gnn_att_dst2"], hidden_hi, hidden_lo,
                       h_hi, h_lo, attention)
        offsets_b = sbuf(nc, scope, "offsets_b", [P, 2, NPAD], F32)
        edge_maxima(nc, s, "m2", 1, attention, source02, offsets, offsets_b)
        aggregate_nodes(nc, s, attention, source02, offsets_b, h_hi, h_lo, a["x"], a["L0_gnn_b2"], s.x1, s.stats,
                        s.x1_dram)


def program(nc, a, out):
    with ExitStack() as scope:
        s = State()
        State.used.clear()
        setup(nc, s, scope)
        s.src, s.dst = a["src"], a["dst"]
        s.x1_dram = nc.dram_tensor("x1_kept", (N, D), F32, kind="Internal").ap()
        s.slot_rows = nc.dram_tensor("slot_rows", (SLOT_TILES * P, 2 * D), F16, kind="Internal").ap()
        gnn(nc, s, a)
        clear_semaphores(nc)
        ffn(nc, s, a, out)


_INS = ["x", "src", "dst"] + ["L0_gnn_" + n for n in ("W1", "att_src1", "att_dst1", "b1", "W2", "att_src2",
        "att_dst2", "b2")] + ["L0_ffn_" + n for n in ("Wqkv", "Wproj", "Wrouter", "W1", "W2", "ln1_g", "ln1_b",
        "ln2_g", "ln2_b")]


def kernel(**inputs):
    import concourse.bacc as _bacc
    from concourse.bass_utils import run_bass_kernel_spmd as _run

    nc = _bacc.Bacc("TRN2", target_bir_lowering=False, num_devices=1)
    arrays, args = {}, {}
    for name in _INS:
        arrays[f"in_{name}"] = np.ascontiguousarray(inputs[name])
        args[name] = nc.dram_tensor(f"in_{name}", arrays[f"in_{name}"].shape, DT.from_np(arrays[f"in_{name}"].dtype),
                                    kind="ExternalInput").ap()
    out = nc.dram_tensor("out_0", (N, D), F32, kind="ExternalOutput").ap()
    program(nc, args, out)
    r = _run(nc, [arrays], core_ids=[0])
    return r.results[0]["out_0"]
```
